# Optimizing a Trainium2 kernel written in Bass

```python
import numpy as np
import jax
import jax.numpy as jnp

def _softmax(x, axis=-1):
    return jax.nn.softmax(x, axis=axis)

def _gelu(x):
    return jax.nn.gelu(x, approximate=True)

def _silu(x):
    return jax.nn.silu(x)

def _sigmoid(x):
    return jax.nn.sigmoid(x)

def _layernorm(x, axis=-1, eps=1e-05):
    m = jnp.mean(x, axis=axis, keepdims=True)
    v = jnp.var(x, axis=axis, keepdims=True)
    return (x - m) / jnp.sqrt(v + eps)

def _scatter_add(tgt, idx, src, axis=0):
    return tgt.at[idx].add(src)

def _segment_sum(src, seg, n):
    return jax.ops.segment_sum(src, seg, n)
kernel_name = 'mk_perceiver_d1_seqx_r4_5fa88a'

def setup_inputs(seed: int=0):
    np.random.seed(seed)
    _w = jnp.asarray

    def _rec_inputs():
        import jax
        import jax.numpy as jnp
        _rk = jax.random.key(seed)
        x = 7.22e-05 + 1 * jax.random.normal(jax.random.fold_in(_rk, 1), (64, 32, 512), jnp.float32)
        _lenS = 32 - jax.random.randint(jax.random.fold_in(_rk, 7), (64,), 0, max(1, 32 // 4) + 1, jnp.int32)
        _lenS2 = 257 - jax.random.randint(jax.random.fold_in(_rk, 8), (64,), 0, max(1, 257 // 4) + 1, jnp.int32)
        _ctx_512P = jax.random.normal(jax.random.fold_in(_rk, 11), (64, 16, 128), jnp.float32)
        _ctx_512c = jax.random.dirichlet(jax.random.fold_in(_rk, 511), 0.3 * jnp.ones((16,), jnp.float32), (64, 257))
        _ctx_512t = jnp.einsum('bsk,bkd->bsd', _ctx_512c, _ctx_512P)
        _ctx_512t = _ctx_512t * jax.lax.rsqrt(jnp.mean(jnp.square(_ctx_512t)) + 1e-12) * 0.953939
        ctx_512 = -0.000514642 + 1.00011 * (_ctx_512t + 0.3 * jax.random.normal(jax.random.fold_in(_rk, 611), (64, 257, 128), jnp.float32))
        return (x, ctx_512)
    x, ctx_512 = _rec_inputs()

    def _L0_xattn_setup():
        import jax, jax.numpy as jnp
        import numpy as np
        B, S, H, NH, L = (2, 512, 512, 16, 128)
        HD = H // NH
        key = jax.random.key(seed)
        k1, k2, k3, k4, k5 = jax.random.split(key, 5)
        scale = 0.02
        return {'q': jax.random.normal(k1, (B, S, H), dtype=jnp.float32), 'latent_kv': jax.random.normal(k2, (B, S, L), dtype=jnp.float32), 'Wq': jax.random.normal(k3, (H, H), dtype=jnp.float32) * scale, 'Wkv_expand': jax.random.normal(k4, (2 * H, L), dtype=jnp.float32) * scale, 'Wout': jax.random.normal(k5, (H, H), dtype=jnp.float32) * scale}
    _L0_xattn_all = _L0_xattn_setup()
    _L0_xattn_in = {k: v for k, v in _L0_xattn_all.items() if k in ('Wq', 'Wkv_expand', 'Wout')}
    del _L0_xattn_all

    def _L0_attn_setup():
        import jax, jax.numpy as jnp
        import numpy as np
        D_MODEL = 512
        N_HEAD = 16
        MLP_HIDDEN = 1408
        NORMALIZER = 16.0

        def rmsnorm(x, w, eps=1e-05):
            return x * jax.lax.rsqrt(jnp.mean(x * x, axis=-1, keepdims=True) + eps) * w

        def _reference_tuple_inner(x, Wq, Wk, Wkg1, Wkg2, bkg2, Wv, Wg, bg, Wo, ln1_w, ln2_w, W1, W3, W2):
            B, L, d = x.shape
            H = N_HEAD
            hd = d // H
            kd = d // 2 // H
            scaling = (d // H) ** (-0.5)
            xn = rmsnorm(x, ln1_w)
            q = xn @ Wq
            k = xn @ Wk * scaling
            gk = jax.nn.log_sigmoid(xn @ Wkg1 @ Wkg2 + bkg2) / NORMALIZER
            v = xn @ Wv
            g = xn @ Wg + bg
            split = lambda t, dh: t.reshape(B, L, H, dh).transpose(1, 0, 2, 3)
            qh, kh, gh = (split(q, kd), split(k, kd), split(gk, kd))
            vh = split(v, hd)
            S0 = jnp.zeros((B, H, kd, hd), x.dtype)

            def step(S, inp):
                qt, kt, vt, gt = inp
                S = S * jnp.exp(gt)[..., None] + kt[..., None] * vt[..., None, :]
                ot = jnp.einsum('bhk,bhkd->bhd', qt, S)
                return (S, ot)
            Sf, o = jax.lax.scan(step, S0, (qh, kh, vh, gh))
            mu = jnp.mean(o, axis=-1, keepdims=True)
            var = jnp.var(o, axis=-1, keepdims=True)
            o = (o - mu) * jax.lax.rsqrt(var + 1e-05)
            o = o.transpose(1, 0, 2, 3).reshape(B, L, d)
            o = jax.nn.silu(g) * o
            x = x + o @ Wo
            xn2 = rmsnorm(x, ln2_w)
            x = x + jax.nn.silu(xn2 @ W1) * (xn2 @ W3) @ W2
            return (x, Sf)
        key = jax.random.key(seed)
        d, B, L, Hd = (D_MODEL, 2, 1024, MLP_HIDDEN)
        ks = jax.random.split(key, 12)
        w = lambda k, shape, s=0.02: jax.random.normal(k, shape, jnp.float32) * s
        return {'x': jax.random.normal(ks[0], (B, L, d), jnp.float32), 'Wq': w(ks[1], (d, d // 2)), 'Wk': w(ks[2], (d, d // 2)), 'Wkg1': w(ks[3], (d, 16)), 'Wkg2': w(ks[4], (16, d // 2)), 'bkg2': jnp.zeros((d // 2,), jnp.float32), 'Wv': w(ks[5], (d, d)), 'Wg': w(ks[6], (d, d)), 'bg': jnp.zeros((d,), jnp.float32), 'Wo': w(ks[7], (d, d)), 'ln1_w': jnp.ones((d,), jnp.float32), 'ln2_w': jnp.ones((d,), jnp.float32), 'W1': w(ks[8], (d, Hd)), 'W3': w(ks[9], (d, Hd)), 'W2': w(ks[10], (Hd, d))}
    _L0_attn_all = _L0_attn_setup()
    _L0_attn_in = {k: v for k, v in _L0_attn_all.items() if k in ('Wq', 'Wk', 'Wkg1', 'Wkg2', 'bkg2', 'Wv', 'Wg', 'bg', 'Wo', 'ln1_w', 'ln2_w', 'W1', 'W3', 'W2')}
    del _L0_attn_all

    def _L0_ffn_setup():
        import jax, jax.numpy as jnp
        import numpy as np
        B, S, D = (2, 512, 512)
        F = 256
        E = 64
        K = 8
        C = 256
        NORM_TOPK = False

        def _moe(x, gate_w, w_gate, w_up, w_down):
            b, s, d = x.shape
            T = b * s
            x2 = x.reshape(T, d)
            logits = x2 @ gate_w.T
            probs = jax.nn.softmax(logits.astype(jnp.float32), axis=-1)
            top_w, top_i = jax.lax.top_k(probs, K)
            if NORM_TOPK:
                top_w = top_w / jnp.sum(top_w, axis=-1, keepdims=True)
            top_w = top_w.astype(x.dtype)
            flat_e = top_i.reshape(-1)
            flat_w = top_w.reshape(-1)
            tok = jnp.arange(T * K) // K
            onehot = jax.nn.one_hot(flat_e, E, dtype=jnp.int32)
            pos = jnp.sum(jnp.cumsum(onehot, axis=0) * onehot, axis=-1) - 1
            valid = pos < C
            loc = flat_e * C + jnp.minimum(pos, C - 1)
            flat_w = jnp.where(valid, flat_w, 0.0)
            safe_loc = jnp.where(valid, loc, E * C)
            xg = jnp.zeros((E * C + 1, d), dtype=x.dtype).at[safe_loc].set(x2[tok])[:E * C]
            xg = xg.reshape(E, C, d)
            h = jax.nn.silu(jnp.einsum('ecd,edf->ecf', xg, w_gate)) * jnp.einsum('ecd,edf->ecf', xg, w_up)
            y = jnp.einsum('ecf,efd->ecd', h, w_down).reshape(E * C, d)
            y_tok = y[loc] * flat_w[:, None]
            out = jnp.zeros((T, d), dtype=x.dtype).at[tok].add(y_tok)
            return out.reshape(b, s, d)
        key = jax.random.key(seed)
        ks = jax.random.split(key, 5)
        scale = 0.02
        return {'hidden_states': jax.random.normal(ks[0], (B, S, D), dtype=jnp.float32), 'gate_w': jax.random.normal(ks[1], (E, D), dtype=jnp.float32) * scale, 'w_gate': jax.random.normal(ks[2], (E, D, F), dtype=jnp.float32) * scale, 'w_up': jax.random.normal(ks[3], (E, D, F), dtype=jnp.float32) * scale, 'w_down': jax.random.normal(ks[4], (E, F, D), dtype=jnp.float32) * scale}
    _L0_ffn_all = _L0_ffn_setup()
    _L0_ffn_in = {k: v for k, v in _L0_ffn_all.items() if k in ('gate_w', 'w_gate', 'w_up', 'w_down')}
    del _L0_ffn_all
    return {'x': x, 'ctx_512': ctx_512, 'L0_xattn_Wq': _L0_xattn_in['Wq'], 'L0_xattn_Wkv_expand': _L0_xattn_in['Wkv_expand'], 'L0_xattn_Wout': _L0_xattn_in['Wout'], 'L0_attn_Wq': _L0_attn_in['Wq'], 'L0_attn_Wk': _L0_attn_in['Wk'], 'L0_attn_Wkg1': _L0_attn_in['Wkg1'], 'L0_attn_Wkg2': _L0_attn_in['Wkg2'], 'L0_attn_bkg2': _L0_attn_in['bkg2'], 'L0_attn_Wv': _L0_attn_in['Wv'], 'L0_attn_Wg': _L0_attn_in['Wg'], 'L0_attn_bg': _L0_attn_in['bg'], 'L0_attn_Wo': _L0_attn_in['Wo'], 'L0_attn_ln1_w': _L0_attn_in['ln1_w'], 'L0_attn_ln2_w': _L0_attn_in['ln2_w'], 'L0_attn_W1': _L0_attn_in['W1'], 'L0_attn_W3': _L0_attn_in['W3'], 'L0_attn_W2': _L0_attn_in['W2'], 'L0_ffn_gate_w': _L0_ffn_in['gate_w'], 'L0_ffn_w_gate': _L0_ffn_in['w_gate'], 'L0_ffn_w_up': _L0_ffn_in['w_up'], 'L0_ffn_w_down': _L0_ffn_in['w_down']}

def reference(x, ctx_512, L0_xattn_Wq, L0_xattn_Wkv_expand, L0_xattn_Wout, L0_attn_Wq, L0_attn_Wk, L0_attn_Wkg1, L0_attn_Wkg2, L0_attn_bkg2, L0_attn_Wv, L0_attn_Wg, L0_attn_bg, L0_attn_Wo, L0_attn_ln1_w, L0_attn_ln2_w, L0_attn_W1, L0_attn_W3, L0_attn_W2, L0_ffn_gate_w, L0_ffn_w_gate, L0_ffn_w_up, L0_ffn_w_down):
    import jax
    import jax.numpy as jnp

    def _L0_xattn_ref(q, latent_kv, Wq, Wkv_expand, Wout):
        import jax, jax.numpy as jnp
        import numpy as np
        B, S, H, NH, L = (2, 512, 512, 16, 128)
        HD = H // NH
        b, sq, _ = q.shape
        sk = latent_kv.shape[1]
        qp = q @ Wq.T
        kv = latent_kv @ Wkv_expand.T
        k, v = jnp.split(kv, 2, axis=-1)
        qh = qp.reshape(b, sq, NH, HD).transpose(0, 2, 1, 3)
        kh = k.reshape(b, sk, NH, HD).transpose(0, 2, 1, 3)
        vh = v.reshape(b, sk, NH, HD).transpose(0, 2, 1, 3)
        inv_sqrt_d = 1.0 / jnp.sqrt(jnp.float32(HD))
        scores = jnp.einsum('bhqd,bhkd->bhqk', qh, kh) * inv_sqrt_d
        causal = jnp.tril(jnp.ones((sq, sk), dtype=bool))
        scores = jnp.where(causal, scores, jnp.finfo(scores.dtype).min)
        attn = jax.nn.softmax(scores, axis=-1)
        out = jnp.einsum('bhqk,bhkd->bhqd', attn, vh)
        out = out.transpose(0, 2, 1, 3).reshape(b, sq, H)
        return out @ Wout.T

    def _L0_attn_ref(x, Wq, Wk, Wkg1, Wkg2, bkg2, Wv, Wg, bg, Wo, ln1_w, ln2_w, W1, W3, W2):
        import jax, jax.numpy as jnp
        import numpy as np
        D_MODEL = 512
        N_HEAD = 16
        MLP_HIDDEN = 1408
        NORMALIZER = 16.0

        def rmsnorm(x, w, eps=1e-05):
            return x * jax.lax.rsqrt(jnp.mean(x * x, axis=-1, keepdims=True) + eps) * w

        def _reference_tuple_inner(x, Wq, Wk, Wkg1, Wkg2, bkg2, Wv, Wg, bg, Wo, ln1_w, ln2_w, W1, W3, W2):
            B, L, d = x.shape
            H = N_HEAD
            hd = d // H
            kd = d // 2 // H
            scaling = (d // H) ** (-0.5)
            xn = rmsnorm(x, ln1_w)
            q = xn @ Wq
            k = xn @ Wk * scaling
            gk = jax.nn.log_sigmoid(xn @ Wkg1 @ Wkg2 + bkg2) / NORMALIZER
            v = xn @ Wv
            g = xn @ Wg + bg
            split = lambda t, dh: t.reshape(B, L, H, dh).transpose(1, 0, 2, 3)
            qh, kh, gh = (split(q, kd), split(k, kd), split(gk, kd))
            vh = split(v, hd)
            S0 = jnp.zeros((B, H, kd, hd), x.dtype)

            def step(S, inp):
                qt, kt, vt, gt = inp
                S = S * jnp.exp(gt)[..., None] + kt[..., None] * vt[..., None, :]
                ot = jnp.einsum('bhk,bhkd->bhd', qt, S)
                return (S, ot)
            Sf, o = jax.lax.scan(step, S0, (qh, kh, vh, gh))
            mu = jnp.mean(o, axis=-1, keepdims=True)
            var = jnp.var(o, axis=-1, keepdims=True)
            o = (o - mu) * jax.lax.rsqrt(var + 1e-05)
            o = o.transpose(1, 0, 2, 3).reshape(B, L, d)
            o = jax.nn.silu(g) * o
            x = x + o @ Wo
            xn2 = rmsnorm(x, ln2_w)
            x = x + jax.nn.silu(xn2 @ W1) * (xn2 @ W3) @ W2
            return (x, Sf)
        return _reference_tuple_inner(x, Wq, Wk, Wkg1, Wkg2, bkg2, Wv, Wg, bg, Wo, ln1_w, ln2_w, W1, W3, W2)[0]

    def _L0_ffn_ref(hidden_states, gate_w, w_gate, w_up, w_down):
        import jax, jax.numpy as jnp
        import numpy as np
        B, S, D = (2, 512, 512)
        F = 256
        E = 64
        K = 8
        C = 256
        NORM_TOPK = False

        def _moe(x, gate_w, w_gate, w_up, w_down):
            b, s, d = x.shape
            T = b * s
            x2 = x.reshape(T, d)
            logits = x2 @ gate_w.T
            probs = jax.nn.softmax(logits.astype(jnp.float32), axis=-1)
            top_w, top_i = jax.lax.top_k(probs, K)
            if NORM_TOPK:
                top_w = top_w / jnp.sum(top_w, axis=-1, keepdims=True)
            top_w = top_w.astype(x.dtype)
            flat_e = top_i.reshape(-1)
            flat_w = top_w.reshape(-1)
            tok = jnp.arange(T * K) // K
            onehot = jax.nn.one_hot(flat_e, E, dtype=jnp.int32)
            pos = jnp.sum(jnp.cumsum(onehot, axis=0) * onehot, axis=-1) - 1
            valid = pos < C
            loc = flat_e * C + jnp.minimum(pos, C - 1)
            flat_w = jnp.where(valid, flat_w, 0.0)
            safe_loc = jnp.where(valid, loc, E * C)
            xg = jnp.zeros((E * C + 1, d), dtype=x.dtype).at[safe_loc].set(x2[tok])[:E * C]
            xg = xg.reshape(E, C, d)
            h = jax.nn.silu(jnp.einsum('ecd,edf->ecf', xg, w_gate)) * jnp.einsum('ecd,edf->ecf', xg, w_up)
            y = jnp.einsum('ecf,efd->ecd', h, w_down).reshape(E * C, d)
            y_tok = y[loc] * flat_w[:, None]
            out = jnp.zeros((T, d), dtype=x.dtype).at[tok].add(y_tok)
            return out.reshape(b, s, d)
        return _moe(hidden_states, gate_w, w_gate, w_up, w_down)
    x = x + _L0_xattn_ref(_layernorm(x, axis=-1), ctx_512, L0_xattn_Wq, L0_xattn_Wkv_expand, L0_xattn_Wout)
    x = x + _L0_attn_ref(_layernorm(x, axis=-1), L0_attn_Wq, L0_attn_Wk, L0_attn_Wkg1, L0_attn_Wkg2, L0_attn_bkg2, L0_attn_Wv, L0_attn_Wg, L0_attn_bg, L0_attn_Wo, L0_attn_ln1_w, L0_attn_ln2_w, L0_attn_W1, L0_attn_W3, L0_attn_W2)
    x = x + _L0_ffn_ref(_layernorm(x, axis=-1), L0_ffn_gate_w, L0_ffn_w_gate, L0_ffn_w_up, L0_ffn_w_down)
    return x

_drawn_inputs = setup_inputs


def setup_inputs(seed=0):
    import zlib

    import numpy as np

    out = dict(_drawn_inputs(seed))
    spreads = {'L0_attn_bkg2': (0.0, 0.8),
     'L0_attn_bg': (0.0, 0.655),
     'L0_attn_ln1_w': (1.0, 0.6),
     'L0_attn_ln2_w': (1.0, 0.6)}
    factors = {'L0_xattn_Wq': 8.0,
     'L0_attn_Wkg1': 8.0,
     'L0_attn_Wkg2': 8.0,
     'L0_ffn_gate_w': 8.0,
     'L0_ffn_w_gate': 8.0,
     'L0_ffn_w_up': 8.0,
     'L0_ffn_w_down': 8.0}
    for name, (base, spread) in spreads.items():
        noise = np.random.default_rng([zlib.crc32(name.encode()), seed]).standard_normal(out[name].shape)
        drawn = base * np.exp(spread * noise) if base else spread * noise
        out[name] = jnp.asarray(drawn.astype(out[name].dtype))
    for name, factor in factors.items():
        out[name] = (out[name] * factor).astype(out[name].dtype)
    return out
```

```python
import concourse.bass as bass
from concourse import mybir
from contextlib import ExitStack

BATCH, SEQ, D = 64, 32, 512
CTX, CD = 257, 128
P = 128
T = BATCH * SEQ
TILES = 2
GT = TILES * P
GROUPS = T // GT
GB = GT // SEQ
TB = P // SEQ
KD = D // P
H, HD = 16, 32
HG = H // 4
GK = 16
GC = H * GK // P
LR = 16
F1 = 1408
J = F1 // P
SLOTS = 4
WJ = 2 * D + D
E, TOP, CAP, FE = 64, 8, 256, 256
HALVES = CAP // P
WE_N = 2 * KD * FE + (FE // P) * D
ROWS = T + CAP
EPS = 1e-5
NORMALIZER = 16.0
MASKED = -1.0e30
FAR = float(1 << 20)

CONST = [("ident", P), ("causal_add", SEQ), ("causal_mul", P), ("before", P), ("ones", P),
         ("restart", GC * GT), ("even", 1), ("odd", 1), ("expert_id", E), ("expert_slot", E),
         ("neg_half", 32), ("token", 1)]
CONST_N = sum(n for _, n in CONST)
VEC_N = 2 * KD + GC
XW_N = KD * D + 2 * D + KD * D
GW_N = 2 * KD * GC * P + 3 * KD * D + KD * LR

AB_USES = ["xT0", "xT1", "k0", "k1", "q0", "q1", "v0", "v1", "s0", "s1", "oT0", "oT1", "w0", "w1",
           "yT0", "yT1", "kg", "kz", "gv0", "gv1", "gg0", "gg1", "gq", "gk",
           "A00", "A01", "A02", "A03", "A10", "A11", "A12", "A13",
           "o0", "o1", "nT0", "nT1", "wo0", "wo1", "mT0", "mT1"]
AB_BANKS = 4
C_USES = [f"h{j}" for j in range(J)] + ["zT0", "zT1", "lg", "ps"]
C_BANKS = 2


def place(name):
    uses, banks, first = (AB_USES, AB_BANKS, 0) if name in AB_USES else (C_USES, C_BANKS, AB_BANKS)
    n = uses.index(name)
    return first + n % banks, n // banks, len(range(n % banks, len(uses), banks))


TIMELINE = ["a_norm", "c0", "c1", "a_norm2", "c2", "a_turn", "c3", "a_project", "c4", "a_scores",
            "c5", "a_probs", "c6", "a_values", "c7", "a_out", "c8", "b_turn", "c9", "b_gate",
            "b_values", "c10", "b_keys", "c_norm", "b_scores", "c_turn", "b_read", "c_route",
            "c_mask", "b_turn_out", "b_out", "c_slots", "b_norm", "c_scatter"]

V_AB, V_C, A_AB = 47, 78, 2


def first(g):
    return isinstance(g, int) and g == 0


class Chain:

    def __init__(self, eng, sem, base):
        self.eng, self.sem, self.base, self.n = eng, sem, base, 0

    def add(self, ins):
        ins.then_inc(self.sem, 1)
        self.n += 1

    def settle(self):
        self.eng.wait_ge(self.sem, self.base + self.n)

    def link(self, ins):
        self.add(ins)
        self.settle()


def build(nc, x, ctxt, consts, vecs, bg_row, xw, gw, kg2, cw, gate_w, ew, out, phases=2):
    f32, i32, u32 = mybir.dt.float32, mybir.dt.int32, mybir.dt.uint32
    ALU, ACT, AX = mybir.AluOpType, mybir.ActivationFunctionType, mybir.AxisListType

    stack = ExitStack()
    with stack:
        def sb(name, shape, dt=f32):
            return stack.enter_context(nc.sbuf_tensor(name, shape, dt))

        def sem(name):
            return stack.enter_context(nc.semaphore(name))

        z_rows = nc.dram_tensor("z_rows", (ROWS, D), f32, kind="Internal").ap()
        slots_d = nc.dram_tensor("slots_d", (E * CAP, 2), i32, kind="Internal").ap()

        weights = sb("weights", [P, XW_N + GW_N])
        wq_x = weights[:, 0:KD * D].rearrange("p (k n) -> p k n", k=KD)
        wk_x = weights[:, KD * D:KD * D + D]
        wv_x = weights[:, KD * D + D:KD * D + 2 * D]
        wo_x = weights[:, KD * D + 2 * D:XW_N].rearrange("p (k n) -> p k n", k=KD)
        at = XW_N
        wq_g = weights[:, at:at + KD * GC * P].rearrange("p (k n) -> p k n", k=KD); at += KD * GC * P
        wk_g = weights[:, at:at + KD * GC * P].rearrange("p (k n) -> p k n", k=KD); at += KD * GC * P
        wv_g = weights[:, at:at + KD * D].rearrange("p (k n) -> p k n", k=KD); at += KD * D
        wg_g = weights[:, at:at + KD * D].rearrange("p (k n) -> p k n", k=KD); at += KD * D
        wo_g = weights[:, at:at + KD * D].rearrange("p (k n) -> p k n", k=KD); at += KD * D
        wkg1 = weights[:, at:at + KD * LR].rearrange("p (k n) -> p k n", k=KD)
        wkg2 = sb("wkg2", [LR, GC * P])
        w_gate = sb("w_gate", [P, KD, E])
        cring = sb("cring", [P, SLOTS, WJ])
        const = sb("const", [P, CONST_N])
        c, col = {}, 0
        for name, n in CONST:
            c[name] = const[:, col:col + n]
            col += n
        vec = sb("vec", [P, VEC_N])
        ln1, ln2, bkg = vec[:, 0:KD], vec[:, KD:2 * KD], vec[:, 2 * KD:VEC_N]
        bg_b = sb("bg_b", [P, D])

        x_in = sb("x_in", [P, TILES, D])
        ctx_in = sb("ctx_in", [P, SEQ, GB])
        ctx_t = sb("ctx_t", [P, GB, SEQ])
        normed = sb("normed", [P, TILES, D])
        normed_t = sb("normed_t", [P, KD, GT])
        q_t = sb("q_t", [P, HG, GT])
        k_diag = sb("k_diag", [P, HG * GB, 4, SEQ])
        v_sb = sb("v_sb", [P, TILES, D])
        probs = sb("probs", [P, TILES, D])
        pair_t = sb("pair_t", [P, TILES, H, P])
        o_t = sb("o_t", [P, KD, GT])
        x1 = sb("x1", [P, TILES, D])
        y = sb("y", [P, TILES, D])
        kg_sb = sb("kg_sb", [LR, GT])
        gate_z = sb("gate_z", [P, GC * GT])
        gate_e = sb("gate_e", [P, GC * GT])
        gate_sum = sb("gate_sum", [P, GC * GT])
        k_dec = sb("k_dec", [P, GC, GT])
        silu_g = sb("silu_g", [P, TILES, D])
        q_even = normed[:, 0, :].rearrange("p (c t) -> p c t", c=GC)
        q_odd = normed[:, 1, :].rearrange("p (c t) -> p c t", c=GC)
        grow = o_t[:, 0:2, :].rearrange("p a t -> p (a t)")
        shrink = o_t[:, 2:4, :].rearrange("p a t -> p (a t)")
        temp = q_t[:, :, :].rearrange("p a t -> p (a t)").rearrange("p (a t) -> p a t", a=TILES)
        o_sb = probs

        resid = sb("resid", [P, TILES, D])
        normed2_t = sb("normed2_t", [P, KD, GT])
        x2 = sb("x2", [P, TILES, D])
        z = sb("z", [P, TILES, D])
        z_t = sb("z_t", [P, KD, GT])
        h_t = z_t[:, 0:2, :]
        h_e = z_t[:, 2, :]

        stats = sb("stats", [P, TILES, 6])
        mv = sb("mv", [P, TILES, 2])
        var_e = sb("var_e", [P, TILES, H])
        rstd = sb("rstd", [P, TILES, H])
        row_max = sb("row_max", [P, TILES, H])
        row_sum = sb("row_sum", [P, TILES, H])
        head_mean = sb("head_mean", [P, TILES, H])
        c_stats = sb("c_stats", [P, TILES, 6])
        c_mv = sb("c_mv", [P, TILES, 2])
        c_var = sb("c_var", [P, TILES])
        c_rstd = sb("c_rstd", [P, TILES])
        logits = sb("logits", [P, TILES, E])
        neg_max = sb("neg_max", [P, TILES])
        esum = sb("esum", [P, TILES])
        top = sb("top", [P, TILES, TOP])
        top_id = sb("top_id", [P, TILES, TOP], u32)
        top_idf = sb("top_idf", [P, TILES, TOP])
        left = sb("left", [P, TILES, E])
        chosen = sb("chosen", [P, TILES, E])
        chosen_sum = sb("chosen_sum", [P, E])
        pos = sb("pos", [P, TILES, E])
        slot = sb("slot", [P, TILES, E])
        late = sb("late", [P, TILES, E])
        junk = sb("junk", [P, E])
        slot_f = sb("slot_f", [P, TILES, TOP])
        slot_i = sb("slot_i", [P, TILES, TOP], i32)
        payload = sb("payload", [P, TILES, TOP, 2], i32)
        tok = sb("tok", [P, TILES])
        table = sb("table", [P, E * HALVES, 2], i32)

        at = 0

        def over(n):
            nonlocal at
            at += n
            return weights[:, at - n:at]

        e_w = [over(WE_N) for _ in range(2)]
        e_wg = [w[:, 0:KD * FE].rearrange("p (k n) -> p k n", k=KD) for w in e_w]
        e_wu = [w[:, KD * FE:2 * KD * FE].rearrange("p (k n) -> p k n", k=KD) for w in e_w]
        e_wd = [w[:, 2 * KD * FE:WE_N].rearrange("p (k n) -> p k n", k=FE // P) for w in e_w]
        e_x = [over(HALVES * D).rearrange("p (h d) -> p h d", h=HALVES) for _ in range(2)]
        e_xt = [over(KD * CAP).rearrange("p (k t) -> p k t", k=KD) for _ in range(2)]
        e_h = [over(2 * CAP).rearrange("p (f t) -> p f t", f=2) for _ in range(2)]
        e_s = silu_g[:, :, 0:CAP]
        e_y = [x_in, y]
        e_from = [sb(f"e_from{n}", [P, HALVES, 2], i32) for n in range(2)]
        e_slot = [sb(f"e_slot{n}", [P, HALVES, 2], i32) for n in range(2)]

        banks = [stack.enter_context(nc.psum_tensor(f"bank{n}", [P, 512], f32)) for n in range(8)]

        consts_in, xw_in, gw_in, small_in = sem("consts_in"), sem("xw_in"), sem("gw_in"), sem("small_in")
        zeroed, tok_ready, table_set, rows_zeroed = sem("zeroed"), sem("tok_ready"), sem("table_set"), sem("rows_zeroed")
        x_loaded, ctx_loaded, ctx_turned = sem("x_loaded"), sem("ctx_loaded"), sem("ctx_turned")
        bank_full = [sem(f"bank_full{n}") for n in range(6)]
        bank_free = [sem(f"bank_free{n}") for n in range(6)]
        var_ready, rstd_ready = sem("var_ready"), sem("rstd_ready")
        xn_ready, yn_ready, y1n_ready = sem("xn_ready"), sem("yn_ready"), sem("y1n_ready")
        centered, exped, probs_ready = sem("centered"), sem("exped"), sem("probs_ready")
        z_in, softplus_done, decay_in, decays = sem("z_in"), sem("softplus_done"), sem("decay_in"), sem("decays")
        g_exped = sem("g_exped")
        o_centered, o_squared, o_ready = sem("o_centered"), sem("o_squared"), sem("o_ready")
        w_loaded = [sem(f"w_loaded{n}") for n in range(SLOTS)]
        w_free = [sem(f"w_free{n}") for n in range(SLOTS)]
        h_exped = sem("h_exped")
        mlp_done, mlp_read = sem("mlp_done"), sem("mlp_read")
        c_var_ready, c_rstd_ready, z_ready, rows_stored = sem("c_var_ready"), sem("c_rstd_ready"), sem("z_ready"), sem("rows_stored")
        lg_centered, lg_exped, chosen_ready, counted = sem("lg_centered"), sem("lg_exped"), sem("chosen_ready"), sem("counted")
        payload_ready, payload_sent, scattered = sem("payload_ready"), sem("payload_sent"), sem("scattered")
        v_ab, v_c, a_ab = sem("v_ab"), sem("v_c"), sem("a_ab")
        passed = sem("passed")
        table_in = sem("table_in")
        e_loaded = [sem(f"e_loaded{n}") for n in range(2)]
        e_from_set, e_slot_set = sem("e_from_set"), sem("e_slot_set")
        e_rows = [sem(f"e_rows{n}") for n in range(2)]
        e_turned, e_xt_a, e_xt_v = sem("e_turned"), sem("e_xt_a"), sem("e_xt_v")
        e_up, e_silu, e_h_ready = sem("e_up"), sem("e_silu"), sem("e_h_ready")
        e_down, e_y_a, e_y_v, e_added = sem("e_down"), sem("e_y_a"), sem("e_y_v"), sem("e_added")

        def bank(name):
            return banks[place(name)[0]]

        def wait_bank_free(eng, name, g):
            b, n, per = place(name)
            eng.wait_ge(bank_free[b], g * per + n + 1)

        def wait_full(eng, name, g):
            b, n, per = place(name)
            eng.wait_ge(bank_full[b], g * per + n + 1)

        def wait_evacuated(eng, name, g):
            b, n, per = place(name)
            eng.wait_ge(bank_free[b], g * per + n + 2)

        def full(ins, name):
            ins.then_inc(bank_full[place(name)[0]], 1)

        def freed(ins, name):
            ins.then_inc(bank_free[place(name)[0]], 1)

        def chunk(j):
            return j % SLOTS, j // SLOTS, len(range(j % SLOTS, J, SLOTS))

        def apart(eng):
            eng.sem_inc(passed, 1)

        def iterate(eng, step):
            for name in TIMELINE:
                if name[0] in "ab":
                    step(name, 0)
            with eng.Fori(1, GROUPS) as i:
                prev = eng.snap(i - 1)
                for name in TIMELINE:
                    step(name, i if name[0] in "ab" else prev)
            for name in TIMELINE:
                if name[0] == "c":
                    step(name, GROUPS - 1)

        block = stack.enter_context(nc.Block())

        @block.sync
        def _(eng):
            def load_chunk(j, g, first=False):
                s, n, per = chunk(j)
                if not first:
                    eng.wait_ge(w_free[s], g * per + n)
                eng.dma_start(cring[:, s, :], cw[j]).then_inc(w_loaded[s], 16)

            def load_group(g):
                eng.dma_start(x_in[:, :, :], x[bass.ds(g * GT, GT)].rearrange("(t p) d -> p t d", p=P))\
                   .then_inc(x_loaded, 16)
                eng.dma_start(ctx_in[:, :, :], ctxt[bass.ds(g, 1)].rearrange("o p s b -> (o p) s b")[:, 0:SEQ, :])\
                   .then_inc(ctx_loaded, 16)

            eng.dma_start(x_in[:, :, :], x[0:GT].rearrange("(t p) d -> p t d", p=P)).then_inc(x_loaded, 16)
            eng.dma_start(const[:, :], consts).then_inc(consts_in, 16)
            eng.dma_start(ctx_in[:, :, :], ctxt[0][:, 0:SEQ, :]).then_inc(ctx_loaded, 16)
            eng.dma_start(weights[:, 0:XW_N], xw).then_inc(xw_in, 16)
            eng.dma_start(vec[:, :], vecs).then_inc(small_in, 16)
            eng.dma_start(bg_b[:, :], bg_row.to_broadcast([P, D])).then_inc(small_in, 16)
            eng.dma_start(wkg2[:, :], kg2).then_inc(small_in, 16)
            eng.dma_start(w_gate[:, :, :], gate_w).then_inc(small_in, 16)
            eng.dma_start(weights[:, XW_N:], gw).then_inc(gw_in, 16)
            for j in range(SLOTS):
                load_chunk(j, 0, first=True)
            eng.wait_ge(zeroed, 6)
            eng.dma_start(z_rows[T:ROWS].rearrange("(t p) d -> p t d", p=P), x2[:, :, :]).then_inc(rows_zeroed, 16)
            eng.dma_start(out[T:ROWS].rearrange("(t p) d -> p t d", p=P), x2[:, :, :]).then_inc(rows_zeroed, 16)
            eng.dma_start(slots_d.rearrange("(p n) v -> p n v", p=P), table[:, :, :]).then_inc(table_set, 16)

            def step(name, g):
                if name == "a_norm" and not first(g):
                    eng.wait_ge(yn_ready, g * TILES)
                    load_group(g)
                elif name == "c_norm":
                    if not isinstance(g, int):
                        for j in range(SLOTS):
                            load_chunk(j, g + 1)
                    eng.wait_ge(z_ready, (g + 1) * TILES)
                    rows = bass.ds(g * GT, GT)
                    eng.dma_start(out[rows].rearrange("(t p) d -> p t d", p=P), x2[:, :, :]).then_inc(rows_stored, 16)
                    eng.dma_start(z_rows[rows].rearrange("(t p) d -> p t d", p=P), z[:, :, :]).then_inc(rows_stored, 16)
                elif name[0] == "c" and name[1:].isdigit() and int(name[1:]) + SLOTS < J:
                    load_chunk(int(name[1:]) + SLOTS, g)

            iterate(eng, step)
            if phases < 2:
                eng.wait_ge(rows_stored, 32 * GROUPS)
                eng.wait_ge(rows_zeroed, 32)
                return

            def load_expert(e, par):
                eng.dma_start(e_w[par], ew[e] if isinstance(e, int) else ew[bass.ds(e, 1)].rearrange("o p n -> (o p) n"))\
                   .then_inc(e_loaded[par], 16)

            wait_full(eng, "mT1", GROUPS - 1)
            load_expert(0, 0)
            load_expert(1, 1)
            eng.wait_ge(scattered, 16 * TILES * TOP * GROUPS)
            eng.dma_start(table[:, :, :], slots_d.rearrange("(p n) v -> p n v", p=P)).then_inc(table_in, 16)
            with eng.Fori(0, (E - 2) // 2) as m:
                for par in range(2):
                    eng.wait_ge(e_down, (m * 2 + par + 1) * HALVES)
                    load_expert(eng.snap(m * 2 + 2 + par), par)
            eng.wait_ge(rows_stored, 32 * GROUPS)
            eng.wait_ge(rows_zeroed, 32)

        @block.gpsimd
        def _(eng):
            eng.memset(k_diag[:, :, :, :], 0.0).then_inc(zeroed, 1)
            eng.memset(pair_t[:, :, :, :], 0.0).then_inc(zeroed, 1)
            eng.memset(x2[:, :, :], 0.0).then_inc(zeroed, 1)
            eng.memset(chosen_sum[:, :], 0.0).then_inc(zeroed, 1)
            eng.iota(table[:, :, 0].rearrange("p (e h) -> p e h", h=HALVES), [[0, E], [P, HALVES]],
                     base=T, channel_multiplier=1).then_inc(zeroed, 1)
            eng.memset(table[:, :, 1], 0).then_inc(zeroed, 1)
            eng.wait_ge(consts_in, 16)

            def power(n_in, n_out, count_in, count_out, src, dst, n):
                eng.wait_ge(n_in, count_in)
                eng.tensor_tensor(dst, src, c["neg_half"][:, 0:n], ALU.pow).then_inc(n_out, 1)

            def ab_power(g, k, n):
                flat = var_e[:, :, :].rearrange("p t h -> p (t h)")[:, 0:n]
                flat_r = rstd[:, :, :].rearrange("p t h -> p (t h)")[:, 0:n]
                power(var_ready, rstd_ready, g * 5 + k + 1, None, flat, flat_r, n)

            def step(name, g):
                if name == "a_norm":
                    eng.wait_ge(ctx_loaded, (g + 1) * 16)
                    apart(eng)
                    eng.tensor_copy(ctx_t[:, :, :], ctx_in[:, :, :].rearrange("p s b -> p b s")).then_inc(ctx_turned, 1)
                    ab_power(g, 0, TILES)
                elif name == "a_out":
                    ab_power(g, 1, TILES)
                    ab_power(g, 2, TILES)
                elif name == "b_read":
                    ab_power(g, 3, TILES * H)
                elif name == "b_out":
                    ab_power(g, 4, TILES)
                elif name == "c_norm":
                    power(c_var_ready, c_rstd_ready, g + 1, None, c_var[:, :], c_rstd[:, :], TILES)
                elif name == "c_scatter":
                    eng.wait_ge(table_set, 16)
                    for t in range(TILES):
                        eng.wait_ge(payload_ready, g * TILES + t + 1)
                        apart(eng)
                        for k in range(TOP):
                            eng.indirect_dma_start(
                                slots_d, bass.IndirectOffsetOnAxis(ap=slot_i[:, t, k:k + 1].bitcast(u32), axis=0),
                                payload[:, t, k, :], None, bounds_check=E * CAP - 1, oob_is_err=False)\
                               .then_inc(scattered, 16)
                    eng.wait_ge(scattered, (g + 1) * (16 * TILES * TOP))
                    eng.sem_inc(payload_sent, 1)

            iterate(eng, step)
            if phases < 2:
                return

            def slots(e):
                return table[:, e * HALVES:(e + 1) * HALVES, :] if isinstance(e, int) else table[:, bass.ds(e * HALVES, HALVES), :]

            def gather(e, par):
                if not isinstance(e, int):
                    eng.wait_ge(e_turned, (e - 1) * HALVES)
                    apart(eng)
                eng.tensor_copy(e_from[par][:, :, :], slots(e)).then_inc(e_from_set, 1)
                eng.wait_ge(e_from_set, e + 1)
                apart(eng)
                for h in range(HALVES):
                    eng.indirect_dma_start(
                        e_x[par][:, h, :], None, z_rows,
                        bass.IndirectOffsetOnAxis(ap=e_from[par][:, h, 0:1].bitcast(u32), axis=0),
                        bounds_check=ROWS - 1, oob_is_err=False).then_inc(e_rows[par], 16)

            def set_slots(e, par):
                if not isinstance(e, int):
                    eng.wait_ge(e_added, (e - 1) * (16 * HALVES))
                    apart(eng)
                eng.tensor_copy(e_slot[par][:, :, :], slots(e)).then_inc(e_slot_set, 1)
                eng.wait_ge(e_slot_set, e + 1)

            def scatter_add(e, par, first=False):
                for h in range(HALVES):
                    if h == 0:
                        eng.wait_ge(e_y_a, e + 1)
                    else:
                        eng.wait_ge(e_y_v, e + 1)
                    if not (first and h == 0):
                        eng.wait_ge(e_added, (e * HALVES + h) * 16)
                    apart(eng)
                    eng.indirect_dma_start(
                        out, bass.IndirectOffsetOnAxis(ap=e_slot[par][:, h, 0:1].bitcast(u32), axis=0),
                        e_y[par][:, h, :], None, bounds_check=ROWS - 1, oob_is_err=True,
                        compute_op=ALU.add).then_inc(e_added, 16)

            eng.wait_ge(rows_stored, 32 * GROUPS)
            eng.wait_ge(rows_zeroed, 32)
            eng.wait_ge(table_in, 16)
            wait_full(eng, "mT1", GROUPS - 1)
            for e in range(2):
                gather(e, e)
                set_slots(e, e)
            eng.wait_ge(e_turned, HALVES)
            gather(2, 0)
            scatter_add(0, 0, first=True)
            eng.wait_ge(e_added, 16 * HALVES)
            set_slots(2, 0)
            with eng.Fori(0, (E - 4) // 2) as m:
                for par in (1, 0):
                    e = eng.snap(m * 2 + 2 - par)
                    gather(eng.snap(e + 2), par)
                    scatter_add(e, par)
                    set_slots(eng.snap(e + 2), par)
            eng.wait_ge(e_turned, (E - 2) * HALVES)
            gather(E - 1, 1)
            scatter_add(E - 3, 1)
            eng.wait_ge(e_added, (E - 2) * (16 * HALVES))
            set_slots(E - 1, 1)
            scatter_add(E - 2, 0)
            scatter_add(E - 1, 1)
            eng.wait_ge(e_added, 16 * HALVES * E)

        @block.scalar
        def _(eng):
            for s in bank_free:
                eng.sem_inc(s, 1)
            eng.sem_inc(mlp_read, 1)
            eng.sem_inc(payload_sent, 1)
            eng.wait_ge(consts_in, 16)

            def turn_back(name, dst, t, g):
                wait_full(eng, name, g)
                freed(eng.activation(dst[:, :, t * P:(t + 1) * P], bank(name)[:, :].rearrange("p (k t) -> p k t", k=KD),
                                     ACT.Copy), name)

            def step(name, g):
                if name == "a_turn":
                    for t in range(TILES):
                        turn_back(f"xT{t}", normed_t, t, g)
                elif name == "a_project":
                    wait_full(eng, "k0", g)
                    eng.wait_ge(zeroed, 6)
                    for a in range(4):
                        rows = slice(32 * a, 32 * a + 32)
                        last = eng.activation(k_diag[rows, 0:2 * GB, a, :],
                                              bank("k0")[rows, :].rearrange("p (n s) -> p n s", s=SEQ), ACT.Copy)
                    freed(last, "k0")
                    wait_full(eng, "q0", g)
                    freed(eng.activation(q_t[:, 0:2, :], bank("q0")[:, :].rearrange("p (a t) -> p a t", a=2),
                                         ACT.Copy, scale=HD ** -0.5), "q0")
                    wait_full(eng, "v0", g)
                    freed(eng.activation(v_sb[:, 0, :], bank("v0")[:, :], ACT.Copy), "v0")
                elif name == "a_scores":
                    for t in range(TILES):
                        eng.wait_ge(centered, g * TILES + t + 1)
                        eng.activation(probs[:, t, :], probs[:, t, :], ACT.Exp).then_inc(exped, 1)
                elif name == "a_values":
                    for t in range(TILES):
                        turn_back(f"oT{t}", o_t, t, g)
                elif name == "b_gate":
                    wait_full(eng, "kg", g)
                    freed(eng.activation(kg_sb[:, :], bank("kg")[0:LR, 0:GT], ACT.Copy), "kg")
                    eng.wait_ge(z_in, g + 1)
                    chain = Chain(eng, a_ab, g * A_AB)
                    chain.link(eng.activation(gate_e[:, :], gate_z[:, :], ACT.Abs))
                    chain.link(eng.activation(gate_e[:, :], gate_e[:, :], ACT.Exp, scale=-1.0))
                    assert chain.n == A_AB
                    eng.activation(gate_e[:, :], gate_e[:, :], ACT.Ln, bias=1.0).then_inc(softplus_done, 1)
                elif name == "b_values":
                    eng.wait_ge(decay_in, g + 1)
                    eng.activation(grow, gate_z[:, :], ACT.Exp, scale=1.0 / NORMALIZER)
                    eng.activation(shrink, gate_z[:, :], ACT.Exp, scale=-1.0 / NORMALIZER).then_inc(decays, 1)
                    for t in range(TILES):
                        wait_full(eng, f"gv{t}", g)
                        freed(eng.activation(v_sb[:, t, :], bank(f"gv{t}")[:, :], ACT.Copy), f"gv{t}")
                    for t in range(TILES):
                        wait_evacuated(eng, f"gg{t}", g)
                        eng.activation(temp[:, t, :], silu_g[:, t, :], ACT.Exp, scale=-1.0).then_inc(g_exped, 1)
                elif name == "b_read":
                    for t in range(TILES):
                        eng.wait_ge(o_centered, g * TILES + t + 1)
                        eng.activation(temp[:, t, :], o_sb[:, t, :], ACT.Square).then_inc(o_squared, 1)
                elif name == "b_turn_out":
                    for t in range(TILES):
                        turn_back(f"nT{t}", o_t, t, g)
                elif name == "c_turn":
                    for t in range(TILES):
                        turn_back(f"zT{t}", z_t, t, g)
                elif name == "c_route":
                    for t in range(TILES):
                        eng.wait_ge(lg_centered, g * TILES + t + 1)
                        eng.activation(logits[:, t, :], logits[:, t, :], ACT.Exp, bias=neg_max[:, t:t + 1],
                                       accum_out=esum[:, t:t + 1]).then_inc(lg_exped, 1)
                elif name[0] == "c" and name[1:].isdigit():
                    j = int(name[1:])
                    wait_full(eng, f"h{j}", g)
                    if j:
                        wait_evacuated(eng, f"h{j - 1}", g)
                    eng.activation(h_e, bank(f"h{j}")[:, 0:GT], ACT.Exp, scale=-1.0).then_inc(h_exped, 1)

            iterate(eng, step)
            if phases < 2:
                return

            def turn_e(e, par):
                eng.wait_ge(e_turned, e * HALVES + 1)
                eng.activation(e_xt[par][:, :, 0:P], banks[0][:, :].rearrange("p (k t) -> p k t", k=KD),
                               ACT.Copy).then_inc(e_xt_a, 1)

            def silu(e, f):
                eng.wait_ge(e_up, e * 2 + f + 1)
                eng.activation(e_s[:, f, :], banks[2 + f][:, 0:CAP], ACT.Silu).then_inc(e_silu, 1)

            def scale_y(e, par, first=False):
                eng.wait_ge(e_down, e * HALVES + 1)
                if not first:
                    eng.wait_ge(e_added, (e - 1) * (16 * HALVES))
                eng.wait_ge(e_slot_set, e + 1)
                eng.activation(e_y[par][:, 0, :], banks[4][:, :], ACT.Copy,
                               scale=e_slot[par][:, 0, 1:2].bitcast(f32)).then_inc(e_y_a, 1)

            def expert(e, par, first, last):
                silu(e, 0)
                if not first:
                    scale_y(e - 1, 1 - par, first=isinstance(e, int) and e <= 2)
                silu(e, 1)
                if not last:
                    turn_e(e + 1, 1 - par)

            turn_e(0, 0)
            expert_loop(eng, expert)
            scale_y(E - 1, 1)

        @block.tensor
        def _(eng):
            eng.wait_ge(consts_in, 16)

            def turn(name, src, t, g):
                wait_bank_free(eng, name, g)
                for k in range(KD):
                    last = eng.transpose(bank(name)[:, k * P:(k + 1) * P], src[:, t, k * P:(k + 1) * P], c["ident"])
                full(last, name)

            def rows(name, src_t, t, w, g):
                wait_bank_free(eng, name, g)
                for k in range(KD):
                    last = eng.matmul(bank(name)[:, :], src_t[:, k, t * P:(t + 1) * P], w[:, k, :],
                                      start=(k == 0), stop=(k == KD - 1))
                full(last, name)

            def columns(name, w, src_t, first, g):
                wait_bank_free(eng, name, g)
                for n in range(2):
                    for k in range(KD):
                        last = eng.matmul(bank(name)[:, n * GT:(n + 1) * GT], w[:, k, (first + n) * P:(first + n + 1) * P],
                                          src_t[:, k, :], start=(k == 0), stop=(k == KD - 1))
                full(last, name)

            def down(j, g):
                wait_evacuated(eng, f"h{j}", g)
                if j == 0:
                    eng.wait_ge(mlp_read, g * TILES + 1)
                s = chunk(j)[0]
                for t in range(TILES):
                    last = eng.matmul(banks[6 + t][:, :], h_t[:, j % 2, t * P:(t + 1) * P], cring[:, s, 2 * D:WJ],
                                      start=(j == 0), stop=(j == J - 1))
                last.then_inc(w_free[s], 1)

            def step(name, g):
                if name == "a_turn":
                    for t in range(TILES):
                        eng.wait_ge(xn_ready, g * TILES + t + 1)
                        turn(f"xT{t}", normed, t, g)
                elif name == "a_project":
                    if first(g):
                        eng.wait_ge(xw_in, 16)
                    eng.wait_ge(ctx_turned, g + 1)
                    ctx_cols = ctx_t[:, :, :].rearrange("p b s -> p (b s)")
                    for n in range(2):
                        wait_bank_free(eng, f"k{n}", g)
                        for m in range(2):
                            hg = 2 * n + m
                            last = eng.matmul(bank(f"k{n}")[:, m * GT:(m + 1) * GT], wk_x[:, hg * P:(hg + 1) * P],
                                              ctx_cols, start=True, stop=True)
                        full(last, f"k{n}")
                    for t in range(TILES):
                        wait_evacuated(eng, f"xT{t}", g)
                    for n in range(2):
                        columns(f"q{n}", wq_x, normed_t, 2 * n, g)
                    for t in range(TILES):
                        wait_bank_free(eng, f"v{t}", g)
                        full(eng.matmul(bank(f"v{t}")[:, :], ctx_cols[:, t * P:(t + 1) * P], wv_x,
                                        start=True, stop=True), f"v{t}")
                elif name == "a_scores":
                    for n in range(2):
                        wait_evacuated(eng, f"k{n}", g)
                        wait_evacuated(eng, f"q{n}", g)
                    for t in range(TILES):
                        wait_bank_free(eng, f"s{t}", g)
                        for hg in range(HG):
                            for b in range(TB):
                                last = eng.matmul(
                                    bank(f"s{t}")[32 * b:32 * b + 32, hg * P:(hg + 1) * P],
                                    q_t[:, hg, t * P + 32 * b:t * P + 32 * b + 32],
                                    k_diag[:, hg * GB + t * TB + b, :, :].rearrange("p a s -> p (a s)"),
                                    start=True, stop=True)
                        full(last, f"s{t}")
                elif name == "a_values":
                    for t in range(TILES):
                        wait_evacuated(eng, f"v{t}", g)
                        eng.wait_ge(probs_ready, g * TILES + t + 1)
                        wait_bank_free(eng, f"oT{t}", g)
                        for h in range(H):
                            a, hg = h % 4, h // 4
                            last = eng.matmul(bank(f"oT{t}")[32 * a:32 * a + 32, hg * P:(hg + 1) * P],
                                              v_sb[:, t, h * HD:(h + 1) * HD], pair_t[:, t, h, :],
                                              start=True, stop=True)
                        full(last, f"oT{t}")
                elif name == "a_out":
                    for t in range(TILES):
                        wait_evacuated(eng, f"oT{t}", g)
                        rows(f"w{t}", o_t, t, wo_x, g)
                elif name == "b_turn":
                    for t in range(TILES):
                        eng.wait_ge(yn_ready, g * TILES + t + 1)
                        turn(f"yT{t}", normed, t, g)
                elif name == "b_gate":
                    if first(g):
                        eng.wait_ge(gw_in, 16)
                        eng.wait_ge(small_in, 64)
                    for t in range(TILES):
                        wait_evacuated(eng, f"yT{t}", g)
                    wait_bank_free(eng, "kg", g)
                    for k in range(KD):
                        last = eng.matmul(bank("kg")[0:LR, 0:GT], wkg1[:, k, :], normed_t[:, k, :],
                                          start=(k == 0), stop=(k == KD - 1))
                    full(last, "kg")
                    wait_evacuated(eng, "kg", g)
                    wait_bank_free(eng, "kz", g)
                    for n in range(GC):
                        last = eng.matmul(bank("kz")[:, n * GT:(n + 1) * GT], wkg2[:, n * P:(n + 1) * P], kg_sb[:, :],
                                          start=True, stop=True)
                    full(last, "kz")
                elif name == "b_values":
                    for t in range(TILES):
                        rows(f"gv{t}", normed_t, t, wv_g, g)
                    for t in range(TILES):
                        rows(f"gg{t}", normed_t, t, wg_g, g)
                elif name == "b_keys":
                    columns("gq", wq_g, normed_t, 0, g)
                    columns("gk", wk_g, normed_t, 0, g)
                elif name == "b_scores":
                    wait_evacuated(eng, "gq", g)
                    wait_evacuated(eng, "gk", g)
                    for t in range(TILES):
                        for r in range(4):
                            wait_bank_free(eng, f"A{t}{r}", g)
                        for n in range(GC):
                            for par, q in ((0, q_even), (1, q_odd)):
                                for r in range(4):
                                    feats = slice(32 * r, 32 * r + 32)
                                    last = eng.matmul(bank(f"A{t}{r}")[:, (2 * n + par) * P:(2 * n + par + 1) * P],
                                                      k_dec[feats, n, t * P:(t + 1) * P], q[feats, n, t * P:(t + 1) * P],
                                                      start=True, stop=True)
                                    if n == GC - 1 and par == 1:
                                        full(last, f"A{t}{r}")
                elif name == "b_read":
                    for t in range(TILES):
                        wait_evacuated(eng, f"gv{t}", g)
                        for r in range(4):
                            wait_evacuated(eng, f"A{t}{r}", g)
                        wait_bank_free(eng, f"o{t}", g)
                        for h in range(H):
                            n, r, par = h // 8, h % 8 // 2, h % 2
                            last = eng.matmul(bank(f"o{t}")[:, h * HD:(h + 1) * HD], pair_t[:, t, 4 * r + 2 * n + par, :],
                                              v_sb[:, t, h * HD:(h + 1) * HD], start=True, stop=True)
                        full(last, f"o{t}")
                elif name == "b_turn_out":
                    for t in range(TILES):
                        eng.wait_ge(o_ready, g * TILES + t + 1)
                        turn(f"nT{t}", o_sb, t, g)
                elif name == "b_out":
                    for t in range(TILES):
                        wait_evacuated(eng, f"nT{t}", g)
                        rows(f"wo{t}", o_t, t, wo_g, g)
                elif name == "b_norm":
                    for t in range(TILES):
                        eng.wait_ge(y1n_ready, g * TILES + t + 1)
                        turn(f"mT{t}", normed, t, g)
                elif name == "c_norm":
                    down(J - 1, g)
                elif name == "c_turn":
                    for t in range(TILES):
                        eng.wait_ge(z_ready, g * TILES + t + 1)
                        turn(f"zT{t}", z, t, g)
                elif name == "c_route":
                    for t in range(TILES):
                        wait_evacuated(eng, f"zT{t}", g)
                    wait_bank_free(eng, "lg", g)
                    for t in range(TILES):
                        for k in range(KD):
                            last = eng.matmul(bank("lg")[:, t * E:(t + 1) * E], z_t[:, k, t * P:(t + 1) * P],
                                              w_gate[:, k, :], start=(k == 0), stop=(k == KD - 1))
                    full(last, "lg")
                elif name == "c_slots":
                    eng.wait_ge(chosen_ready, g * TILES + TILES)
                    eng.wait_ge(counted, g + 1)
                    wait_bank_free(eng, "ps", g)
                    eng.matmul(bank("ps")[:, 0:E], c["ones"], chosen_sum[:, :], start=True, stop=False)
                    eng.matmul(bank("ps")[:, 0:E], c["before"], chosen[:, 0, :], start=False, stop=True)
                    eng.matmul(bank("ps")[:, E:2 * E], c["ones"], chosen_sum[:, :], start=True, stop=False)
                    eng.matmul(bank("ps")[:, E:2 * E], c["ones"], chosen[:, 0, :], start=False, stop=False)
                    full(eng.matmul(bank("ps")[:, E:2 * E], c["before"], chosen[:, 1, :], start=False, stop=True), "ps")
                elif name[0] == "c" and name[1:].isdigit():
                    j = int(name[1:])
                    s, n, per = chunk(j)
                    if j == 0:
                        for t in range(TILES):
                            wait_evacuated(eng, f"mT{t}", g)
                    eng.wait_ge(w_loaded[s], (g * per + n + 1) * 16)
                    wait_bank_free(eng, f"h{j}", g)
                    w = cring[:, s, 0:2 * D].rearrange("p (m k f) -> p m k f", m=2, k=KD)
                    for m in range(2):
                        for k in range(KD):
                            last = eng.matmul(bank(f"h{j}")[:, m * GT:(m + 1) * GT], w[:, m, k, :], normed2_t[:, k, :],
                                              start=(k == 0), stop=(k == KD - 1))
                    full(last, f"h{j}")
                    if j:
                        down(j - 1, g)

            iterate(eng, step)
            if phases < 2:
                return

            def turn_e(e, par):
                eng.wait_ge(e_rows[par], ((e - par) // 2 + 1) * (16 * HALVES) if isinstance(e, int)
                            else (e - par + 2) * (8 * HALVES))
                for h in range(HALVES):
                    if not (isinstance(e, int) and e == 0):
                        eng.wait_ge((e_xt_a, e_xt_v)[h], e)
                    for k in range(KD):
                        last = eng.transpose(banks[h][:, k * P:(k + 1) * P], e_x[par][:, h, k * P:(k + 1) * P], c["ident"])
                    last.then_inc(e_turned, 1)

            def up(e, par, f, first):
                if f == 0:
                    eng.wait_ge(e_loaded[par], ((e - par) // 2 + 1) * 16 if isinstance(e, int) else (e - par + 2) * 8)
                    eng.wait_ge(e_xt_a, e + 1)
                    eng.wait_ge(e_xt_v, e + 1)
                if not first:
                    eng.wait_ge(e_h_ready, e * 2 - 1 + f)
                for m, w in ((0, e_wg[par]), (1, e_wu[par])):
                    for k in range(KD):
                        last = eng.matmul(banks[2 + f][:, m * CAP:(m + 1) * CAP], w[:, k, f * P:(f + 1) * P],
                                          e_xt[par][:, k, :], start=(k == 0), stop=(k == KD - 1))
                last.then_inc(e_up, 1)

            def down_e(e, par, first):
                eng.wait_ge(e_h_ready, e * 2 + 2)
                for h in range(HALVES):
                    if not first:
                        eng.wait_ge((e_y_a, e_y_v)[h], e)
                    for f in range(2):
                        last = eng.matmul(banks[4 + h][:, :], e_h[par][:, f, h * P:(h + 1) * P], e_wd[par][:, f, :],
                                          start=(f == 0), stop=(f == 1))
                    last.then_inc(e_down, 1)

            def expert(e, par, first, last):
                up(e, par, 0, first)
                if not first:
                    down_e(e - 1, 1 - par, first=isinstance(e, int) and e == 1)
                up(e, par, 1, first)
                if not last:
                    turn_e(e + 1, 1 - par)

            turn_e(0, 0)
            expert_loop(eng, expert)
            down_e(E - 1, 1, False)

        @block.vector
        def _(eng):
            eng.wait_ge(consts_in, 16)
            eng.wait_ge(small_in, 64)
            eng.wait_ge(zeroed, 6)
            tok_set = Chain(eng, tok_ready, 0)
            for t in range(TILES):
                tok_set.add(eng.tensor_scalar(tok[:, t:t + 1], c["token"], float(t * P), None, ALU.add))
            tok_set.settle()
            chains = {}

            def chain(which, g):
                if which not in chains:
                    sem_, per = (v_ab, V_AB) if which == "ab" else (v_c, V_C)
                    chains[which] = Chain(eng, sem_, g * per)
                return chains[which]

            def end(which):
                n = chains.pop(which).n
                assert n == (V_AB if which == "ab" else V_C), (which, n)

            def heads(ap):
                return ap.rearrange("p (h d) -> p h d", d=HD)

            def per_head(ap):
                return ap.unsqueeze(2).to_broadcast([P, H, HD])

            def moments(ch, src, st, m):
                for t in range(TILES):
                    ch.add(eng.bn_stats(st[:, t, :], src[:, t, :]))
                ch.settle()
                apart(eng)
                for t in range(TILES):
                    ch.add(eng.bn_aggr(m[:, t, :], st[:, t, :]))
                ch.settle()

            r2 = rstd[:, :, :].rearrange("p t h -> p (t h)")
            v2 = var_e[:, :, :].rearrange("p t h -> p (t h)")
            spare = row_max[:, :, :].rearrange("p t h -> p (t h)")

            def step(name, g):
                if name == "a_norm":
                    ch = chain("ab", g)
                    eng.wait_ge(x_loaded, (g + 1) * 16)
                    moments(ch, x_in, stats, mv)
                    eng.tensor_scalar(v2[:, 0:TILES], mv[:, :, 1], EPS, None, ALU.add).then_inc(var_ready, 1)
                elif name == "a_norm2":
                    eng.wait_ge(rstd_ready, g * 5 + 1)
                    for t in range(TILES):
                        eng.tensor_scalar(normed[:, t, :], x_in[:, t, :], mv[:, t, 0:1], r2[:, t:t + 1],
                                          ALU.subtract, ALU.mult).then_inc(xn_ready, 1)
                elif name == "a_project":
                    wait_full(eng, "k1", g)
                    for a in range(4):
                        rows = slice(32 * a, 32 * a + 32)
                        last = eng.tensor_copy(k_diag[rows, 2 * GB:4 * GB, a, :],
                                               bank("k1")[rows, :].rearrange("p (n s) -> p n s", s=SEQ))
                    freed(last, "k1")
                    wait_full(eng, "q1", g)
                    freed(eng.tensor_scalar(q_t[:, 2:4, :], bank("q1")[:, :].rearrange("p (a t) -> p a t", a=2),
                                            HD ** -0.5, None, ALU.mult), "q1")
                    wait_full(eng, "v1", g)
                    freed(eng.tensor_copy(v_sb[:, 1, :], bank("v1")[:, :]), "v1")
                elif name == "a_scores":
                    ch = chain("ab", g)
                    for t in range(TILES):
                        wait_full(eng, f"s{t}", g)
                        freed(eng.tensor_tensor(heads(probs[:, t, :]), heads(bank(f"s{t}")[:, :]),
                                                c["causal_add"].unsqueeze(1).to_broadcast([P, H, SEQ]), ALU.add), f"s{t}")
                        wait_evacuated(eng, f"s{t}", g)
                        ch.link(eng.tensor_reduce(row_max[:, t, :], heads(probs[:, t, :]), AX.X, ALU.max))
                        eng.tensor_tensor(heads(probs[:, t, :]), heads(probs[:, t, :]), per_head(row_max[:, t, :]),
                                          ALU.subtract).then_inc(centered, 1)
                elif name == "a_probs":
                    ch = chain("ab", g)
                    for t in range(TILES):
                        eng.wait_ge(exped, g * TILES + t + 1)
                        ch.link(eng.tensor_reduce(row_sum[:, t, :], heads(probs[:, t, :]), AX.X, ALU.add))
                        ch.link(eng.reciprocal(row_sum[:, t, :], row_sum[:, t, :]))
                        ch.link(eng.tensor_tensor(heads(probs[:, t, :]), heads(probs[:, t, :]),
                                                  per_head(row_sum[:, t, :]), ALU.mult))
                        for b in range(TB):
                            rows = slice(32 * b, 32 * b + 32)
                            last = eng.transpose(pair_t[rows, t, :, 32 * b:32 * b + 32], heads(probs[rows, t, :]))
                        last.then_inc(probs_ready, 1)
                elif name == "a_out":
                    ch = chain("ab", g)
                    for t in range(TILES):
                        wait_full(eng, f"w{t}", g)
                        freed(eng.tensor_tensor(x1[:, t, :], x_in[:, t, :], bank(f"w{t}")[:, :], ALU.add), f"w{t}")
                    wait_evacuated(eng, "w0", g)
                    wait_evacuated(eng, "w1", g)
                    moments(ch, x1, stats, mv)
                    eng.tensor_scalar(v2[:, 0:TILES], mv[:, :, 1], EPS, None, ALU.add).then_inc(var_ready, 1)
                    eng.wait_ge(rstd_ready, g * 5 + 2)
                    for t in range(TILES):
                        ch.add(eng.tensor_scalar(y[:, t, :], x1[:, t, :], mv[:, t, 0:1], r2[:, t:t + 1],
                                                 ALU.subtract, ALU.mult))
                    ch.link(eng.tensor_tensor(spare[:, 0:TILES], mv[:, :, 1], r2[:, 0:TILES], ALU.mult))
                    ch.link(eng.tensor_tensor(spare[:, 0:TILES], spare[:, 0:TILES], r2[:, 0:TILES], ALU.mult))
                    eng.tensor_scalar(v2[:, 0:TILES], spare[:, 0:TILES], EPS, None, ALU.add).then_inc(var_ready, 1)
                    eng.wait_ge(rstd_ready, g * 5 + 3)
                    for t in range(TILES):
                        eng.tensor_scalar(normed[:, t, :], y[:, t, :], r2[:, t:t + 1], None, ALU.mult).then_inc(yn_ready, 1)
                elif name == "b_turn":
                    for t in range(TILES):
                        wait_full(eng, f"yT{t}", g)
                        freed(eng.tensor_tensor(normed_t[:, :, t * P:(t + 1) * P],
                                                bank(f"yT{t}")[:, :].rearrange("p (k t) -> p k t", k=KD),
                                                ln1.unsqueeze(2).to_broadcast([P, KD, P]), ALU.mult), f"yT{t}")
                elif name == "b_gate":
                    ch = chain("ab", g)
                    wait_full(eng, "kz", g)
                    for n in range(GC):
                        cols = slice(n * GT, (n + 1) * GT)
                        ins = eng.tensor_scalar(gate_z[:, cols], bank("kz")[:, cols], bkg[:, n:n + 1], None, ALU.add)
                        if n == 0:
                            ch.add(ins)
                    freed(ins, "kz")
                    wait_evacuated(eng, "kz", g)
                    eng.tensor_scalar(spare[:, 0:1], mv[:, 0, 0:1], 1.0, None, ALU.mult).then_inc(z_in, 1)
                    eng.wait_ge(softplus_done, g + 1)
                    ch.link(eng.scalar_tensor_tensor(gate_z[:, :], gate_z[:, :], 0.0, gate_e[:, :], ALU.min, ALU.subtract))
                    ch.link(eng.tensor_tensor_scan(gate_sum[:, :], c["restart"], gate_z[:, :], 0.0, ALU.mult, ALU.add))
                    sums = gate_sum[:, :].rearrange("p (n s) -> p n s", s=SEQ)
                    ch.link(eng.tensor_tensor(gate_z[:, :].rearrange("p (n s) -> p n s", s=SEQ), sums,
                                              sums[:, :, SEQ // 2 - 1:SEQ // 2].to_broadcast([P, GC * GB, SEQ]), ALU.subtract))
                    eng.tensor_scalar(gate_z[:, :], gate_z[:, :], -80.0 * NORMALIZER, 80.0 * NORMALIZER,
                                      ALU.max, ALU.min).then_inc(decay_in, 1)
                elif name == "b_values":
                    ch = chain("ab", g)
                    for t in range(TILES):
                        wait_full(eng, f"gg{t}", g)
                        freed(eng.tensor_tensor(silu_g[:, t, :], bank(f"gg{t}")[:, :], bg_b[:, :], ALU.add), f"gg{t}")
                    for t in range(TILES):
                        eng.wait_ge(g_exped, g * TILES + t + 1)
                        ch.link(eng.tensor_scalar(temp[:, t, :], temp[:, t, :], 1.0, None, ALU.add))
                        ch.link(eng.reciprocal(temp[:, t, :], temp[:, t, :]))
                        ch.add(eng.tensor_tensor(silu_g[:, t, :], silu_g[:, t, :], temp[:, t, :], ALU.mult))
                elif name == "b_keys":
                    ch = chain("ab", g)
                    eng.wait_ge(decays, g + 1)
                    wait_full(eng, "gq", g)
                    ch.add(eng.scalar_tensor_tensor(q_even.rearrange("p c t -> p (c t)"), bank("gq")[:, :], c["even"], grow,
                                                    ALU.mult, ALU.mult))
                    freed(eng.scalar_tensor_tensor(q_odd.rearrange("p c t -> p (c t)"), bank("gq")[:, :], c["odd"], grow,
                                                   ALU.mult, ALU.mult), "gq")
                    wait_full(eng, "gk", g)
                    freed(eng.scalar_tensor_tensor(k_dec[:, :, :].rearrange("p c t -> p (c t)"), bank("gk")[:, :], HD ** -0.5,
                                                   shrink, ALU.mult, ALU.mult), "gk")
                elif name == "b_scores":
                    for t in range(TILES):
                        for r in range(4):
                            wait_full(eng, f"A{t}{r}", g)
                            freed(eng.tensor_tensor(pair_t[:, t, 4 * r:4 * r + 4, :],
                                                    bank(f"A{t}{r}")[:, :].rearrange("p (n t) -> p n t", t=P),
                                                    c["causal_mul"].unsqueeze(1).to_broadcast([P, 4, P]), ALU.mult), f"A{t}{r}")
                elif name == "b_read":
                    ch = chain("ab", g)
                    for t in range(TILES):
                        wait_full(eng, f"o{t}", g)
                        o = heads(bank(f"o{t}")[:, :])
                        ch.link(eng.tensor_reduce(head_mean[:, t, :], o, AX.X, ALU.add))
                        ch.link(eng.tensor_scalar(head_mean[:, t, :], head_mean[:, t, :], 1.0 / HD, None, ALU.mult))
                        freed(eng.tensor_tensor(heads(o_sb[:, t, :]), o, per_head(head_mean[:, t, :]), ALU.subtract), f"o{t}")
                        wait_evacuated(eng, f"o{t}", g)
                        eng.tensor_scalar(spare[:, 0:1], mv[:, 0, 0:1], 1.0, None, ALU.mult).then_inc(o_centered, 1)
                    for t in range(TILES):
                        eng.wait_ge(o_squared, g * TILES + t + 1)
                        ch.link(eng.tensor_reduce(row_sum[:, t, :], heads(temp[:, t, :]), AX.X, ALU.add))
                    eng.tensor_scalar(v2, row_sum[:, :, :].rearrange("p t h -> p (t h)"), 1.0 / HD, EPS,
                                      ALU.mult, ALU.add).then_inc(var_ready, 1)
                    eng.wait_ge(rstd_ready, g * 5 + 4)
                    for t in range(TILES):
                        ch.link(eng.tensor_tensor(heads(o_sb[:, t, :]), heads(o_sb[:, t, :]), per_head(rstd[:, t, :]), ALU.mult))
                        eng.tensor_tensor(o_sb[:, t, :], o_sb[:, t, :], silu_g[:, t, :], ALU.mult).then_inc(o_ready, 1)
                elif name == "b_out":
                    ch = chain("ab", g)
                    for t in range(TILES):
                        wait_full(eng, f"wo{t}", g)
                        freed(eng.tensor_tensor(y[:, t, :], y[:, t, :], bank(f"wo{t}")[:, :], ALU.add), f"wo{t}")
                    wait_evacuated(eng, "wo0", g)
                    wait_evacuated(eng, "wo1", g)
                    moments(ch, y, stats, mv)
                    ch.link(eng.tensor_tensor(spare[:, 0:TILES], mv[:, :, 0], mv[:, :, 0], ALU.mult))
                    ch.link(eng.tensor_tensor(spare[:, 0:TILES], spare[:, 0:TILES], mv[:, :, 1], ALU.add))
                    eng.tensor_scalar(v2[:, 0:TILES], spare[:, 0:TILES], EPS, None, ALU.add).then_inc(var_ready, 1)
                    for t in range(TILES):
                        ch.add(eng.tensor_tensor(resid[:, t, :], x1[:, t, :], y[:, t, :], ALU.add))
                    eng.wait_ge(rstd_ready, g * 5 + 5)
                    for t in range(TILES):
                        eng.tensor_scalar(normed[:, t, :], y[:, t, :], r2[:, t:t + 1], None, ALU.mult).then_inc(y1n_ready, 1)
                elif name == "b_norm":
                    chain("ab", g).settle()
                    for t in range(TILES):
                        wait_full(eng, f"mT{t}", g)
                        freed(eng.tensor_tensor(normed2_t[:, :, t * P:(t + 1) * P],
                                                bank(f"mT{t}")[:, :].rearrange("p (k t) -> p k t", k=KD),
                                                ln2.unsqueeze(2).to_broadcast([P, KD, P]), ALU.mult), f"mT{t}")
                    end("ab")
                elif name == "c_norm":
                    ch = chain("c", g)
                    s, n, per = chunk(J - 1)
                    eng.wait_ge(w_free[s], g * per + n + 1)
                    for t in range(TILES):
                        eng.tensor_tensor(x2[:, t, :], resid[:, t, :], banks[6 + t][:, :], ALU.add).then_inc(mlp_read, 1)
                    eng.wait_ge(mlp_read, (g + 1) * TILES + 1)
                    moments(ch, x2, c_stats, c_mv)
                    eng.tensor_scalar(c_var[:, :], c_mv[:, :, 1], EPS, None, ALU.add).then_inc(c_var_ready, 1)
                    eng.wait_ge(c_rstd_ready, g + 1)
                    for t in range(TILES):
                        eng.tensor_scalar(z[:, t, :], x2[:, t, :], c_mv[:, t, 0:1], c_rstd[:, t:t + 1],
                                          ALU.subtract, ALU.mult).then_inc(z_ready, 1)
                elif name == "c_route":
                    ch = chain("c", g)
                    wait_full(eng, "lg", g)
                    freed(eng.tensor_copy(logits[:, :, :], bank("lg")[:, 0:TILES * E].rearrange("p (t e) -> p t e", e=E)), "lg")
                    wait_evacuated(eng, "lg", g)
                    for t in range(TILES):
                        apart(eng)
                        ch.link(eng.max(top[:, t, :], logits[:, t, :]))
                        eng.tensor_scalar(neg_max[:, t:t + 1], top[:, t, 0:1], -1.0, None, ALU.mult).then_inc(lg_centered, 1)
                elif name == "c_mask":
                    ch = chain("c", g)
                    for t in range(TILES):
                        eng.wait_ge(lg_exped, g * TILES + t + 1)
                        ch.link(eng.reciprocal(esum[:, t:t + 1], esum[:, t:t + 1]))
                        ch.link(eng.tensor_scalar(logits[:, t, :], logits[:, t, :], esum[:, t:t + 1], None, ALU.mult))
                        apart(eng)
                        ch.link(eng.max(top[:, t, :], logits[:, t, :]))
                        apart(eng)
                        ch.add(eng.max_index(top_id[:, t, :], top[:, t, :], logits[:, t, :]))
                        ch.link(eng.match_replace(left[:, t, :], top[:, t, :], logits[:, t, :], -1.0))
                        eng.tensor_scalar(chosen[:, t, :], left[:, t, :], 0.0, None, ALU.is_lt).then_inc(chosen_ready, 1)
                    ch.settle()
                    eng.tensor_copy(top_idf[:, :, :], top_id[:, :, :]).then_inc(counted, 1)
                elif name == "c_slots":
                    ch = chain("c", g)
                    wait_full(eng, "ps", g)
                    freed(eng.tensor_copy(pos[:, :, :], bank("ps")[:, 0:TILES * E].rearrange("p (t e) -> p t e", e=E)), "ps")
                    wait_evacuated(eng, "ps", g)
                    eng.wait_ge(counted, g + 1)
                    for t in range(TILES):
                        ch.link(eng.tensor_tensor(chosen_sum[:, :], chosen_sum[:, :], chosen[:, t, :], ALU.add))
                    ids = c["expert_slot"].unsqueeze(1).to_broadcast([P, TILES, E])
                    ch.add(eng.tensor_scalar(late[:, :, :], pos[:, :, :], float(P), -float(P * P - 1), ALU.is_ge, ALU.mult))
                    ch.link(eng.scalar_tensor_tensor(slot[:, :, :], pos[:, :, :], float(P), ids, ALU.mult, ALU.add))
                    ch.link(eng.tensor_tensor(slot[:, :, :], slot[:, :, :], late[:, :, :], ALU.add))
                    ch.link(eng.tensor_scalar(late[:, :, :], pos[:, :, :], float(CAP), FAR, ALU.is_ge, ALU.mult))
                    ch.link(eng.tensor_tensor(slot[:, :, :], slot[:, :, :], late[:, :, :], ALU.add))
                    eng.wait_ge(payload_sent, g + 1)
                    for t in range(TILES):
                        for k in range(TOP):
                            ch.link(eng.scalar_tensor_tensor(junk[:, :], c["expert_id"], top_idf[:, t, k:k + 1], slot[:, t, :],
                                                             ALU.is_equal, ALU.mult, accum_out=slot_f[:, t, k:k + 1]))
                        ch.add(eng.tensor_copy(slot_i[:, t, :], slot_f[:, t, :]))
                        ch.add(eng.tensor_copy(payload[:, t, :, 0], tok[:, t:t + 1].to_broadcast([P, TOP])))
                        ch.link(eng.tensor_copy(payload[:, t, :, 1].bitcast(f32), top[:, t, :]))
                        eng.tensor_scalar(tok[:, t:t + 1], tok[:, t:t + 1], float(GT), None, ALU.add).then_inc(payload_ready, 1)
                    eng.wait_ge(payload_ready, (g + 1) * TILES)
                    eng.wait_ge(rows_stored, (g + 1) * 32)
                    end("c")
                elif name[0] == "c" and name[1:].isdigit():
                    ch = chain("c", g)
                    j = int(name[1:])
                    eng.wait_ge(h_exped, g * J + j + 1)
                    if j == 0:
                        eng.wait_ge(rows_zeroed, 32)
                    ch.link(eng.tensor_scalar(h_e, h_e, 1.0, None, ALU.add))
                    ch.link(eng.reciprocal(h_e, h_e))
                    ch.link(eng.tensor_tensor(h_e, h_e, bank(f"h{j}")[:, 0:GT], ALU.mult))
                    freed(eng.tensor_tensor(h_t[:, j % 2, :], h_e, bank(f"h{j}")[:, GT:2 * GT], ALU.mult), f"h{j}")

            iterate(eng, step)
            if phases < 2:
                return

            def turn_e(e, par):
                eng.wait_ge(e_turned, e * HALVES + 2)
                eng.tensor_copy(e_xt[par][:, :, P:2 * P], banks[1][:, :].rearrange("p (k t) -> p k t", k=KD))\
                   .then_inc(e_xt_v, 1)

            def gate(e, par, f):
                eng.wait_ge(e_silu, e * 2 + f + 1)
                eng.tensor_tensor(e_h[par][:, f, :], e_s[:, f, :], banks[2 + f][:, CAP:2 * CAP], ALU.mult)\
                   .then_inc(e_h_ready, 1)

            def scale_y(e, par, first=False):
                eng.wait_ge(e_down, e * HALVES + 2)
                if not first:
                    eng.wait_ge(e_added, (e - 1) * (16 * HALVES))
                eng.wait_ge(e_slot_set, e + 1)
                eng.tensor_scalar(e_y[par][:, 1, :], banks[5][:, :], e_slot[par][:, 1, 1:2].bitcast(f32), None, ALU.mult)\
                   .then_inc(e_y_v, 1)

            def expert(e, par, first, last):
                gate(e, par, 0)
                if not first:
                    scale_y(e - 1, 1 - par, first=isinstance(e, int) and e <= 2)
                gate(e, par, 1)
                if not last:
                    turn_e(e + 1, 1 - par)

            turn_e(0, 0)
            expert_loop(eng, expert)
            scale_y(E - 1, 1)


def expert_loop(eng, step):
    step(0, 0, first=True, last=False)
    step(1, 1, first=False, last=False)
    step(2, 0, first=False, last=False)
    with eng.Fori(0, (E - 4) // 2) as m:
        step(eng.snap(m * 2 + 3), 1, first=False, last=False)
        step(eng.snap(m * 2 + 4), 0, first=False, last=False)
    step(E - 1, 1, first=False, last=True)


def shape_constants():
    import numpy as np
    p = np.arange(P)
    a = {
        "ident": np.eye(P),
        "causal_add": np.where(np.arange(SEQ)[None, :] <= (p % SEQ)[:, None], 0.0, MASKED),
        "causal_mul": (p[:, None] // SEQ == p[None, :] // SEQ) & (p[:, None] <= p[None, :]),
        "before": p[:, None] < p[None, :],
        "ones": np.ones((P, P)),
        "restart": np.tile((np.arange(GC * GT) % SEQ != 0)[None, :], (P, 1)),
        "even": (p % 32 < GK)[:, None],
        "odd": (p % 32 >= GK)[:, None],
        "expert_id": np.tile(np.arange(E)[None, :], (P, 1)),
        "expert_slot": np.tile(HALVES * np.arange(E)[None, :], (P, 1)),
        "neg_half": np.full((P, 32), -0.5),
        "token": p[:, None],
    }
    return np.ascontiguousarray(np.concatenate([a[n].astype(np.float32) for n, _ in CONST], axis=1))


def lay_out(inputs):
    import numpy as np

    def chunks(w):
        k = w.shape[0] // P
        return w.reshape(k, P, -1).transpose(1, 0, 2).reshape(P, -1)

    g = {k: np.asarray(v) for k, v in inputs.items()}
    kv = g["L0_xattn_Wkv_expand"].T
    w13 = [g[n].reshape(KD, P, J, P).transpose(2, 1, 0, 3).reshape(J, P, D) for n in ("L0_attn_W1", "L0_attn_W3")]
    per_expert = [g[n].reshape(E, -1, P, g[n].shape[2]).transpose(0, 2, 1, 3).reshape(E, P, -1)
                  for n in ("L0_ffn_w_gate", "L0_ffn_w_up", "L0_ffn_w_down")]
    arrays = {
        "x": g["x"].reshape(T, D),
        "ctxt": g["ctx_512"].reshape(GROUPS, GB, CTX, CD).transpose(0, 3, 2, 1),
        "consts": shape_constants(),
        "vecs": np.concatenate([g["L0_attn_ln1_w"].reshape(KD, P).T, g["L0_attn_ln2_w"].reshape(KD, P).T,
                                g["L0_attn_bkg2"].reshape(GC, P).T], axis=1),
        "bg_row": g["L0_attn_bg"].reshape(1, D),
        "xw": np.concatenate([chunks(g["L0_xattn_Wq"].T), kv, chunks(g["L0_xattn_Wout"].T)], axis=1),
        "gw": np.concatenate([chunks(g[f"L0_attn_{n}"]) for n in ("Wq", "Wk", "Wv", "Wg", "Wo", "Wkg1")], axis=1),
        "kg2": g["L0_attn_Wkg2"],
        "cw": np.concatenate(w13 + [g["L0_attn_W2"].reshape(J, P, D)], axis=2),
        "gate_w": g["L0_ffn_gate_w"].T.reshape(KD, P, E).transpose(1, 0, 2),
        "ew": np.concatenate(per_expert, axis=2),
    }
    return {k: np.ascontiguousarray(v) for k, v in arrays.items()}


def kernel(**inputs):
    import concourse.bacc as bacc
    from concourse.bass_utils import run_bass_kernel_spmd

    nc = bacc.Bacc("TRN2", target_bir_lowering=False, num_devices=1)
    arrays = lay_out(inputs)
    handles = {k: nc.dram_tensor(f"in_{k}", v.shape, mybir.dt.from_np(v.dtype), kind="ExternalInput").ap()
               for k, v in arrays.items()}
    out = nc.dram_tensor("out", (ROWS, D), mybir.dt.float32, kind="ExternalOutput").ap()
    build(nc, out=out, **handles)
    result = run_bass_kernel_spmd(nc, [{f"in_{k}": v for k, v in arrays.items()}], core_ids=[0])
    return result.results[0]["out"][0:T].reshape(BATCH, SEQ, D)
```

```python
import concourse.bass as bass
from concourse import mybir
from contextlib import ExitStack

BATCH, SEQ, D = 64, 32, 512
CTX, CD = 257, 128
P = 128
T = BATCH * SEQ
TILES = 2
GT = TILES * P
GROUPS = T // GT
GB = GT // SEQ
TB = P // SEQ
KD = D // P
H, HD = 16, 32
HG = H // 4
GK = 16
GC = H * GK // P
LR = 16
F1 = 1408
J = F1 // P
SLOTS = 4
WJ = 2 * D + D
E, TOP, CAP, FE = 64, 8, 256, 256
HALVES = CAP // P
AHEAD = 4
WE_N = 2 * KD * FE + (FE // P) * D
ROWS = T + CAP
EPS = 1e-5
NORMALIZER = 16.0
MASKED = -1.0e30
FAR = float(1 << 20)

CONST = [("ident", P), ("causal_add", SEQ), ("causal_mul", P), ("before", P), ("ones", P),
         ("restart", GC * GT), ("even", 1), ("odd", 1), ("expert_id", E), ("expert_slot", E),
         ("neg_half", 32), ("token", 1)]
CONST_N = sum(n for _, n in CONST)
VEC_N = 2 * KD + GC
XW_N = KD * D + 2 * D + KD * D
GW_N = 2 * KD * GC * P + 3 * KD * D + KD * LR

AB_USES = ["xT0", "xT1", "k0", "k1", "q0", "q1", "v0", "v1", "s0", "s1", "oT0", "oT1", "w0", "w1",
           "yT0", "yT1", "kg", "gv0", "gv1", "kz", "gg0", "gg1", "gq", "gk",
           "A00", "A01", "A02", "A03", "A10", "A11", "A12", "A13",
           "o0", "o1", "nT0", "nT1", "wo0", "wo1"]
AB_BANKS = 4
C_USES = ["mT0", "mT1"] + [f"h{j}" for j in range(J)] + ["zT0", "zT1", "lg", "ps"]
C_BANKS = 2


def place(name):
    uses, banks, first = (AB_USES, AB_BANKS, 0) if name in AB_USES else (C_USES, C_BANKS, AB_BANKS)
    n = uses.index(name)
    return first + n % banks, n // banks, len(range(n % banks, len(uses), banks))


TIMELINE = ["a_turn", "a_project", "c_begin", "a_scores", "c0", "c1", "a_probs", "c2", "a_values",
            "a_out", "next_load", "c3", "b_turn", "c4", "b_gate", "b_values", "b_decay", "b_silu",
            "b_keys", "c5", "b_scores", "c6", "b_read", "c7", "b_read2", "c8", "next_norm", "c9",
            "b_turn_out", "c10", "c_norm", "b_out", "c_turn", "c_route", "c_mask", "c_slots",
            "c_scatter"]

V_N, V_AB, V_C, A_AB = 4, 39, 56, 2


def first(g):
    return isinstance(g, int) and g == 0


class Chain:

    def __init__(self, eng, sem, base):
        self.eng, self.sem, self.base, self.n = eng, sem, base, 0

    def add(self, ins):
        ins.then_inc(self.sem, 1)
        self.n += 1

    def settle(self):
        self.eng.wait_ge(self.sem, self.base + self.n)

    def link(self, ins):
        self.add(ins)
        self.settle()


def build(nc, x, ctxt, consts, vecs, bg_row, xw, gw, kg2, cw, gate_w, ew, out, phases=2):
    f32, i32, u32 = mybir.dt.float32, mybir.dt.int32, mybir.dt.uint32
    f32r = mybir.dt.float32r
    ALU, ACT, AX = mybir.AluOpType, mybir.ActivationFunctionType, mybir.AxisListType

    stack = ExitStack()
    with stack:
        def sb(name, shape, dt=f32):
            return stack.enter_context(nc.sbuf_tensor(name, shape, dt))

        def sem(name):
            return stack.enter_context(nc.semaphore(name))

        z_rows = nc.dram_tensor("z_rows", (ROWS, D), f32, kind="Internal").ap()
        slots_d = nc.dram_tensor("slots_d", (E * CAP, 2), i32, kind="Internal").ap()

        wkg2 = sb("wkg2", [LR, GC * P])
        w_gate = sb("w_gate", [P, KD, E])
        cring = sb("cring", [P, SLOTS, WJ])
        const = sb("const", [P, CONST_N])
        c, col = {}, 0
        for name, n in CONST:
            c[name] = const[:, col:col + n]
            col += n
        vec = sb("vec", [P, VEC_N])
        ln1, ln2, bkg = vec[:, 0:KD], vec[:, KD:2 * KD], vec[:, 2 * KD:VEC_N]
        bg_b = sb("bg_b", [P, D])

        normed = sb("normed", [P, TILES, D])
        resid = sb("resid", [P, TILES, D])
        normed2_t = sb("normed2_t", [P, KD, GT])
        x2 = sb("x2", [P, TILES, D])
        z = sb("z", [P, TILES, D])
        z_t = sb("z_t", [P, KD, GT])
        h_t = z_t[:, 0:2, :]
        h_e = z_t[:, 2, :]

        stats = sb("stats", [P, TILES, 6])
        mv = sb("mv", [P, TILES, 2])
        var_e = sb("var_e", [P, TILES, H])
        rstd = sb("rstd", [P, TILES, H])
        row_max = sb("row_max", [P, TILES, H])
        row_sum = sb("row_sum", [P, TILES, H])
        head_mean = sb("head_mean", [P, TILES, H])
        n_stats = sb("n_stats", [P, TILES, 6])
        n_mv = sb("n_mv", [P, TILES, 2])
        n_var = sb("n_var", [P, TILES])
        n_rstd = sb("n_rstd", [P, TILES])
        c_stats = sb("c_stats", [P, TILES, 6])
        c_mv = sb("c_mv", [P, TILES, 2])
        c_var = sb("c_var", [P, TILES])
        c_rstd = sb("c_rstd", [P, TILES])
        logits = sb("logits", [P, TILES, E])
        neg_max = sb("neg_max", [P, TILES])
        esum = sb("esum", [P, TILES])
        top = sb("top", [P, TILES, TOP])
        top_id = sb("top_id", [P, TILES, TOP], u32)
        top_idf = sb("top_idf", [P, TILES, TOP])
        left = sb("left", [P, TILES, E])
        chosen = sb("chosen", [P, TILES, E])
        chosen_sum = sb("chosen_sum", [P, E])
        pos = sb("pos", [P, TILES, E])
        slot = sb("slot", [P, TILES, E])
        late = sb("late", [P, TILES, E])
        junk = sb("junk", [P, E])
        slot_f = sb("slot_f", [P, TILES, TOP])
        slot_i = sb("slot_i", [P, TILES, TOP], i32)
        payload = sb("payload", [P, TILES, TOP, 2], i32)
        tok = sb("tok", [P, TILES])
        table = sb("table", [P, E * HALVES, 2], i32)

        e_slot = [sb(f"e_slot{n}", [P, HALVES, 2], i32) for n in range(AHEAD)]

        attentions = ExitStack()

        def ab(name, shape, dt=f32):
            return attentions.enter_context(nc.sbuf_tensor(name, shape, dt))

        weights = ab("weights", [P, XW_N + GW_N])
        wq_x = weights[:, 0:KD * D].rearrange("p (k n) -> p k n", k=KD)
        wk_x = weights[:, KD * D:KD * D + D]
        wv_x = weights[:, KD * D + D:KD * D + 2 * D]
        wo_x = weights[:, KD * D + 2 * D:XW_N].rearrange("p (k n) -> p k n", k=KD)
        at = XW_N
        wq_g = weights[:, at:at + KD * GC * P].rearrange("p (k n) -> p k n", k=KD); at += KD * GC * P
        wk_g = weights[:, at:at + KD * GC * P].rearrange("p (k n) -> p k n", k=KD); at += KD * GC * P
        wv_g = weights[:, at:at + KD * D].rearrange("p (k n) -> p k n", k=KD); at += KD * D
        wg_g = weights[:, at:at + KD * D].rearrange("p (k n) -> p k n", k=KD); at += KD * D
        wo_g = weights[:, at:at + KD * D].rearrange("p (k n) -> p k n", k=KD); at += KD * D
        wkg1 = weights[:, at:at + KD * LR].rearrange("p (k n) -> p k n", k=KD)
        x_in = ab("x_in", [P, TILES, D])
        ctx_in = ab("ctx_in", [P, SEQ, GB])
        ctx_t = ab("ctx_t", [P, GB, SEQ])
        normed_t = ab("normed_t", [P, KD, GT])
        q_t = ab("q_t", [P, HG, GT])
        k_diag = ab("k_diag", [P, HG * GB, 4, SEQ])
        v_sb = ab("v_sb", [P, TILES, D])
        probs = ab("probs", [P, TILES, D])
        pair_t = ab("pair_t", [P, TILES, H, P])
        o_t = ab("o_t", [P, KD, GT])
        x1 = ab("x1", [P, TILES, D])
        y = ab("y", [P, TILES, D])
        kg_sb = ab("kg_sb", [LR, GT])
        gate_z = ab("gate_z", [P, GC * GT])
        gate_e = ab("gate_e", [P, GC * GT])
        gate_sum = ab("gate_sum", [P, GC * GT])
        k_dec = ab("k_dec", [P, GC, GT])
        silu_g = ab("silu_g", [P, TILES, D])
        q_even = normed[:, 0, :].rearrange("p (c t) -> p c t", c=GC)
        q_odd = normed[:, 1, :].rearrange("p (c t) -> p c t", c=GC)
        grow = o_t[:, 0:2, :].rearrange("p a t -> p (a t)")
        shrink = o_t[:, 2:4, :].rearrange("p a t -> p (a t)")
        temp = q_t[:, :, :].rearrange("p a t -> p (a t)").rearrange("p (a t) -> p a t", a=TILES)
        o_sb = probs

        attentions.close()

        GU, DN = 2 * KD * FE, (FE // P) * D
        e_w = [sb(f"e_w{n}", [P, WE_N]) for n in range(2)]
        e_gu_hi = [sb(f"e_gu_hi{n}", [P, GU], f32r) for n in range(2)]
        e_gu_lo = [sb(f"e_gu_lo{n}", [P, GU], f32r) for n in range(2)]
        e_d_hi = [sb(f"e_d_hi{n}", [P, DN], f32r) for n in range(2)]
        e_d_lo = [sb(f"e_d_lo{n}", [P, DN], f32r) for n in range(2)]
        e_x = [sb(f"e_x{n}", [P, HALVES, D]) for n in range(AHEAD)]
        e_xt_hi = [sb(f"e_xt_hi{n}", [P, KD, CAP], f32r) for n in range(2)]
        e_xt_lo = [sb(f"e_xt_lo{n}", [P, KD, CAP], f32r) for n in range(2)]
        e_s = sb("e_s", [P, 2, CAP])
        e_h = sb("e_h", [P, 2, CAP])
        e_h_hi = [sb(f"e_h_hi{n}", [P, 2, CAP], f32r) for n in range(2)]
        e_h_lo = [sb(f"e_h_lo{n}", [P, 2, CAP], f32r) for n in range(2)]
        e_y = [sb(f"e_y{n}", [P, HALVES, D]) for n in range(2)]

        banks = [stack.enter_context(nc.psum_tensor(f"bank{n}", [P, 512], f32)) for n in range(8)]

        consts_in, xw_in, gw_in, small_in = sem("consts_in"), sem("xw_in"), sem("gw_in"), sem("small_in")
        zeroed, tok_ready, table_set, rows_zeroed = sem("zeroed"), sem("tok_ready"), sem("table_set"), sem("rows_zeroed")
        x_loaded, ctx_loaded, ctx_turned = sem("x_loaded"), sem("ctx_loaded"), sem("ctx_turned")
        bank_full = [sem(f"bank_full{n}") for n in range(6)]
        bank_free = [sem(f"bank_free{n}") for n in range(6)]
        n_var_ready, n_rstd_ready = sem("n_var_ready"), sem("n_rstd_ready")
        var_ready, rstd_ready = sem("var_ready"), sem("rstd_ready")
        xn_ready, yn_ready, y1n_ready = sem("xn_ready"), sem("yn_ready"), sem("y1n_ready")
        centered, exped, probs_ready = sem("centered"), sem("exped"), sem("probs_ready")
        z_in, softplus_done, decay_in, decays = sem("z_in"), sem("softplus_done"), sem("decay_in"), sem("decays")
        g_tanhed = sem("g_tanhed")
        o_centered, o_squared, o_ready = sem("o_centered"), sem("o_squared"), sem("o_ready")
        w_loaded = [sem(f"w_loaded{n}") for n in range(SLOTS)]
        w_free = [sem(f"w_free{n}") for n in range(SLOTS)]
        h_tanhed = sem("h_tanhed")
        mlp_done, mlp_read = sem("mlp_done"), sem("mlp_read")
        c_var_ready, c_rstd_ready, z_ready, rows_stored = sem("c_var_ready"), sem("c_rstd_ready"), sem("z_ready"), sem("rows_stored")
        lg_centered, lg_exped, chosen_ready, counted = sem("lg_centered"), sem("lg_exped"), sem("chosen_ready"), sem("counted")
        payload_ready, payload_sent, scattered = sem("payload_ready"), sem("payload_sent"), sem("scattered")
        v_next, v_ab, v_c, a_ab = sem("v_next"), sem("v_ab"), sem("v_c"), sem("a_ab")
        passed = sem("passed")
        table_in = sem("table_in")
        e_gu_in = [sem(f"e_gu_in{n}") for n in range(2)]
        e_d_in = [sem(f"e_d_in{n}") for n in range(2)]
        e_slot_set = sem("e_slot_set")
        e_rows = [sem(f"e_rows{n}") for n in range(AHEAD)]
        e_gu_hi_set, e_gu_lo_set, e_d_hi_set, e_d_lo_set = (sem(n) for n in ("e_gu_hi_set", "e_gu_lo_set", "e_d_hi_set", "e_d_lo_set"))
        e_turned, e_xt_hi_set, e_xt_lo_set = sem("e_turned"), sem("e_xt_hi_set"), sem("e_xt_lo_set")
        e_up, e_silu, e_h_set, e_h_hi_set, e_h_lo_set = (sem(n) for n in ("e_up", "e_silu", "e_h_set", "e_h_hi_set", "e_h_lo_set"))
        e_down, e_y_a, e_y_v, e_added = sem("e_down"), sem("e_y_a"), sem("e_y_v"), sem("e_added")

        def bank(name):
            return banks[place(name)[0]]

        def wait_bank_free(eng, name, g):
            b, n, per = place(name)
            eng.wait_ge(bank_free[b], g * per + n + 1)

        def wait_full(eng, name, g):
            b, n, per = place(name)
            eng.wait_ge(bank_full[b], g * per + n + 1)

        def wait_evacuated(eng, name, g):
            b, n, per = place(name)
            eng.wait_ge(bank_free[b], g * per + n + 2)

        def full(ins, name):
            ins.then_inc(bank_full[place(name)[0]], 1)

        def freed(ins, name):
            ins.then_inc(bank_free[place(name)[0]], 1)

        def chunk(j):
            return j % SLOTS, j // SLOTS, len(range(j % SLOTS, J, SLOTS))

        def apart(eng):
            eng.sem_inc(passed, 1)

        def iterate(eng, step):
            step("next_load", 0)
            step("next_norm", 0)
            for name in TIMELINE:
                if name[0] != "c":
                    step(name, 1 if name[0] == "n" else 0)
            with eng.Fori(1, GROUPS - 1) as i:
                before, after = eng.snap(i - 1), eng.snap(i + 1)
                for name in TIMELINE:
                    step(name, {"c": before, "n": after}.get(name[0], i))
            for name in TIMELINE:
                if name[0] != "n":
                    step(name, GROUPS - 2 if name[0] == "c" else GROUPS - 1)
            for name in TIMELINE:
                if name[0] == "c":
                    step(name, GROUPS - 1)

        block = stack.enter_context(nc.Block())

        @block.sync
        def _(eng):
            def load_chunk(j, g, first=False):
                s, n, per = chunk(j)
                if not first:
                    eng.wait_ge(w_free[s], g * per + n)
                eng.dma_start(cring[:, s, :], cw[j]).then_inc(w_loaded[s], 16)

            def load_group(g):
                eng.dma_start(x_in[:, :, :], x[bass.ds(g * GT, GT)].rearrange("(t p) d -> p t d", p=P))\
                   .then_inc(x_loaded, 16)
                eng.dma_start(ctx_in[:, :, :], ctxt[bass.ds(g, 1)].rearrange("o p s b -> (o p) s b")[:, 0:SEQ, :])\
                   .then_inc(ctx_loaded, 16)

            eng.dma_start(x_in[:, :, :], x[0:GT].rearrange("(t p) d -> p t d", p=P)).then_inc(x_loaded, 16)
            eng.dma_start(const[:, :], consts).then_inc(consts_in, 16)
            eng.dma_start(ctx_in[:, :, :], ctxt[0][:, 0:SEQ, :]).then_inc(ctx_loaded, 16)
            eng.dma_start(weights[:, 0:XW_N], xw).then_inc(xw_in, 16)
            eng.dma_start(vec[:, :], vecs).then_inc(small_in, 16)
            eng.dma_start(bg_b[:, :], bg_row.to_broadcast([P, D])).then_inc(small_in, 16)
            eng.dma_start(wkg2[:, :], kg2).then_inc(small_in, 16)
            eng.dma_start(w_gate[:, :, :], gate_w).then_inc(small_in, 16)
            eng.dma_start(weights[:, XW_N:], gw).then_inc(gw_in, 16)
            for j in range(SLOTS):
                load_chunk(j, 0, first=True)
            eng.wait_ge(zeroed, 6)
            eng.dma_start(z_rows[T:ROWS].rearrange("(t p) d -> p t d", p=P), x2[:, :, :]).then_inc(rows_zeroed, 16)
            eng.dma_start(out[T:ROWS].rearrange("(t p) d -> p t d", p=P), x2[:, :, :]).then_inc(rows_zeroed, 16)
            eng.dma_start(slots_d.rearrange("(p n) v -> p n v", p=P), table[:, :, :]).then_inc(table_set, 16)

            def step(name, g):
                if name == "next_load" and not first(g):
                    eng.wait_ge(yn_ready, g * TILES)
                    load_group(g)
                elif name == "c_norm":
                    if not (isinstance(g, int) and g == GROUPS - 1):
                        for j in range(SLOTS):
                            load_chunk(j, g + 1)
                    eng.wait_ge(z_ready, (g + 1) * TILES)
                    rows = bass.ds(g * GT, GT)
                    eng.dma_start(out[rows].rearrange("(t p) d -> p t d", p=P), x2[:, :, :]).then_inc(rows_stored, 16)
                    eng.dma_start(z_rows[rows].rearrange("(t p) d -> p t d", p=P), z[:, :, :]).then_inc(rows_stored, 16)
                elif name[0] == "c" and name[1:].isdigit() and int(name[1:]) + SLOTS < J:
                    load_chunk(int(name[1:]) + SLOTS, g)

            iterate(eng, step)
            if phases < 2:
                eng.wait_ge(rows_stored, 32 * GROUPS)
                eng.wait_ge(rows_zeroed, 32)
                return

            def load_expert(e, par):
                w = ew[e] if isinstance(e, int) else ew[bass.ds(e, 1)].rearrange("o p n -> (o p) n")
                eng.dma_start(e_w[par][:, 0:GU], w[:, 0:GU]).then_inc(e_gu_in[par], 16)
                eng.dma_start(e_w[par][:, GU:WE_N], w[:, GU:WE_N]).then_inc(e_d_in[par], 16)

            wait_full(eng, "wo1", GROUPS - 1)
            eng.wait_ge(y1n_ready, TILES * GROUPS)
            load_expert(0, 0)
            load_expert(1, 1)
            eng.wait_ge(scattered, 16 * TILES * TOP * GROUPS)
            eng.dma_start(table[:, :, :], slots_d.rearrange("(p n) v -> p n v", p=P)).then_inc(table_in, 16)
            with eng.Fori(0, (E - 2) // 2) as m:
                for par in range(2):
                    eng.wait_ge(e_d_lo_set, m * 2 + par + 1)
                    load_expert(eng.snap(m * 2 + 2 + par), par)
            eng.wait_ge(rows_stored, 32 * GROUPS)
            eng.wait_ge(rows_zeroed, 32)

        @block.gpsimd
        def _(eng):
            eng.memset(k_diag[:, :, :, :], 0.0).then_inc(zeroed, 1)
            eng.memset(pair_t[:, :, :, :], 0.0).then_inc(zeroed, 1)
            eng.memset(x2[:, :, :], 0.0).then_inc(zeroed, 1)
            eng.memset(chosen_sum[:, :], 0.0).then_inc(zeroed, 1)
            eng.iota(table[:, :, 0].rearrange("p (e h) -> p e h", h=HALVES), [[0, E], [P, HALVES]],
                     base=T, channel_multiplier=1).then_inc(zeroed, 1)
            eng.memset(table[:, :, 1], 0).then_inc(zeroed, 1)
            eng.wait_ge(consts_in, 16)

            def power(ready, done, count, src, dst, n):
                eng.wait_ge(ready, count)
                eng.tensor_tensor(dst, src, c["neg_half"][:, 0:n], ALU.pow).then_inc(done, 1)

            def ab_power(g, k, at, n):
                flat = var_e[:, :, :].rearrange("p t h -> p (t h)")[:, at:at + n]
                flat_r = rstd[:, :, :].rearrange("p t h -> p (t h)")[:, at:at + n]
                power(var_ready, rstd_ready, g * 5 + k + 1, flat, flat_r, n)

            def step(name, g):
                if name == "next_norm":
                    eng.wait_ge(ctx_loaded, (g + 1) * 16)
                    apart(eng)
                    eng.tensor_copy(ctx_t[:, :, :], ctx_in[:, :, :].rearrange("p s b -> p b s")).then_inc(ctx_turned, 1)
                    power(n_var_ready, n_rstd_ready, g + 1, n_var[:, :], n_rstd[:, :], TILES)
                elif name == "a_out":
                    ab_power(g, 0, 0, TILES)
                    ab_power(g, 1, 0, TILES)
                elif name == "b_read":
                    for t in range(TILES):
                        ab_power(g, 2 + t, t * H, H)
                elif name == "b_out":
                    ab_power(g, 4, 0, TILES)
                elif name == "c_norm":
                    power(c_var_ready, c_rstd_ready, g + 1, c_var[:, :], c_rstd[:, :], TILES)
                elif name == "c_scatter":
                    eng.wait_ge(table_set, 16)
                    for t in range(TILES):
                        eng.wait_ge(payload_ready, g * TILES + t + 1)
                        apart(eng)
                        for k in range(TOP):
                            eng.indirect_dma_start(
                                slots_d, bass.IndirectOffsetOnAxis(ap=slot_i[:, t, k:k + 1].bitcast(u32), axis=0),
                                payload[:, t, k, :], None, bounds_check=E * CAP - 1, oob_is_err=False)\
                               .then_inc(scattered, 16)
                    eng.wait_ge(scattered, (g + 1) * (16 * TILES * TOP))
                    eng.sem_inc(payload_sent, 1)

            iterate(eng, step)
            if phases < 2:
                return

            def slots(e):
                return table[:, e * HALVES:(e + 1) * HALVES, :] if isinstance(e, int) else table[:, bass.ds(e * HALVES, HALVES), :]

            def gather(e, n):
                if not (isinstance(e, int) and e < AHEAD):
                    eng.wait_ge(e_turned, (e - AHEAD + 1) * HALVES)
                    eng.wait_ge(e_added, (e - AHEAD + 1) * (HALVES * 16))
                    apart(eng)
                eng.tensor_copy(e_slot[n][:, :, :], slots(e)).then_inc(e_slot_set, 1)
                eng.wait_ge(e_slot_set, e + 1)
                apart(eng)
                for h in range(HALVES):
                    eng.indirect_dma_start(
                        e_x[n][:, h, :], None, z_rows,
                        bass.IndirectOffsetOnAxis(ap=e_slot[n][:, h, 0:1].bitcast(u32), axis=0),
                        bounds_check=ROWS - 1, oob_is_err=False).then_inc(e_rows[n], 16)

            def scatter_add(e, n):
                for h in range(HALVES):
                    eng.wait_ge((e_y_a, e_y_v)[h], e + 1)
                    if h == 0 and not first(e):
                        eng.wait_ge(e_added, e * (HALVES * 16))
                    apart(eng)
                    eng.indirect_dma_start(
                        out, bass.IndirectOffsetOnAxis(ap=e_slot[n][:, h, 0:1].bitcast(u32), axis=0),
                        e_y[n % 2][:, h, :], None, bounds_check=ROWS - 1, oob_is_err=True,
                        compute_op=ALU.add).then_inc(e_added, 16)

            eng.wait_ge(rows_stored, 32 * GROUPS)
            eng.wait_ge(rows_zeroed, 32)
            eng.wait_ge(table_in, 16)
            wait_full(eng, "wo1", GROUPS - 1)
            for e in range(AHEAD - 1):
                gather(e, e)
            gather(AHEAD - 1, AHEAD - 1)
            scatter_add(0, 0)
            with eng.Fori(0, (E - AHEAD) // AHEAD) as m:
                for n in range(1, AHEAD + 1):
                    e = eng.snap(m * AHEAD + n)
                    gather(eng.snap(e + AHEAD - 1), n - 1)
                    scatter_add(e, n % AHEAD)
            for e in range(E - AHEAD + 1, E):
                scatter_add(e, e % AHEAD)
            eng.wait_ge(e_added, 16 * HALVES * E)

        @block.scalar
        def _(eng):
            for s in bank_free:
                eng.sem_inc(s, 1)
            eng.sem_inc(mlp_read, 1)
            eng.sem_inc(payload_sent, 1)
            eng.wait_ge(consts_in, 16)

            def turn_back(name, dst, t, g):
                wait_full(eng, name, g)
                freed(eng.activation(dst[:, :, t * P:(t + 1) * P], bank(name)[:, :].rearrange("p (k t) -> p k t", k=KD),
                                     ACT.Copy), name)

            def step(name, g):
                if name == "a_turn":
                    for t in range(TILES):
                        turn_back(f"xT{t}", normed_t, t, g)
                elif name == "a_project":
                    wait_full(eng, "k0", g)
                    eng.wait_ge(zeroed, 6)
                    for a in range(4):
                        rows = slice(32 * a, 32 * a + 32)
                        last = eng.activation(k_diag[rows, 0:2 * GB, a, :],
                                              bank("k0")[rows, :].rearrange("p (n s) -> p n s", s=SEQ), ACT.Copy)
                    freed(last, "k0")
                    wait_full(eng, "q0", g)
                    freed(eng.activation(q_t[:, 0:2, :], bank("q0")[:, :].rearrange("p (a t) -> p a t", a=2),
                                         ACT.Copy, scale=HD ** -0.5), "q0")
                    wait_full(eng, "v0", g)
                    freed(eng.activation(v_sb[:, 0, :], bank("v0")[:, :], ACT.Copy), "v0")
                elif name == "a_scores":
                    for t in range(TILES):
                        eng.wait_ge(centered, g * TILES + t + 1)
                        eng.activation(probs[:, t, :], probs[:, t, :], ACT.Exp).then_inc(exped, 1)
                elif name == "a_values":
                    for t in range(TILES):
                        turn_back(f"oT{t}", o_t, t, g)
                elif name == "b_gate":
                    wait_full(eng, "kg", g)
                    freed(eng.activation(kg_sb[:, :], bank("kg")[0:LR, 0:GT], ACT.Copy), "kg")
                elif name == "b_values":
                    for t in range(TILES):
                        wait_full(eng, f"gv{t}", g)
                        freed(eng.activation(v_sb[:, t, :], bank(f"gv{t}")[:, :], ACT.Copy), f"gv{t}")
                elif name == "b_decay":
                    eng.wait_ge(z_in, g + 1)
                    chain = Chain(eng, a_ab, g * A_AB)
                    chain.link(eng.activation(gate_e[:, :], gate_z[:, :], ACT.Abs))
                    chain.link(eng.activation(gate_e[:, :], gate_e[:, :], ACT.Exp, scale=-1.0))
                    assert chain.n == A_AB
                    eng.activation(gate_e[:, :], gate_e[:, :], ACT.Ln, bias=1.0).then_inc(softplus_done, 1)
                elif name == "b_silu":
                    eng.wait_ge(decay_in, g + 1)
                    eng.activation(grow, gate_z[:, :], ACT.Exp, scale=1.0 / NORMALIZER)
                    eng.activation(shrink, gate_z[:, :], ACT.Exp, scale=-1.0 / NORMALIZER).then_inc(decays, 1)
                    for t in range(TILES):
                        wait_evacuated(eng, f"gg{t}", g)
                        eng.activation(temp[:, t, :], silu_g[:, t, :], ACT.Tanh, scale=0.5).then_inc(g_tanhed, 1)
                elif name == "b_read":
                    for t in range(TILES):
                        eng.wait_ge(o_centered, g * TILES + t + 1)
                        eng.activation(temp[:, t, :], o_sb[:, t, :], ACT.Square).then_inc(o_squared, 1)
                elif name == "b_turn_out":
                    for t in range(TILES):
                        turn_back(f"nT{t}", o_t, t, g)
                elif name == "c_turn":
                    for t in range(TILES):
                        turn_back(f"zT{t}", z_t, t, g)
                elif name == "c_route":
                    for t in range(TILES):
                        eng.wait_ge(lg_centered, g * TILES + t + 1)
                        eng.activation(logits[:, t, :], logits[:, t, :], ACT.Exp, bias=neg_max[:, t:t + 1],
                                       accum_out=esum[:, t:t + 1]).then_inc(lg_exped, 1)
                elif name[0] == "c" and name[1:].isdigit():
                    j = int(name[1:])
                    wait_full(eng, f"h{j}", g)
                    if j:
                        wait_evacuated(eng, f"h{j - 1}", g)
                    eng.activation(h_e, bank(f"h{j}")[:, 0:GT], ACT.Tanh, scale=0.5).then_inc(h_tanhed, 1)

            iterate(eng, step)
            if phases < 2:
                return

            def split_up(e, par):
                if not (isinstance(e, int) and e < 2):
                    eng.wait_ge(e_up, (e - 1) * 2)
                eng.wait_ge(e_gu_in[par], loads(e, par, 2))
                eng.activation(e_gu_hi[par][:, :], e_w[par][:, 0:GU], ACT.Copy).then_inc(e_gu_hi_set, 1)

            def split_down(e, par):
                if not (isinstance(e, int) and e < 2):
                    eng.wait_ge(e_down, (e - 1) * HALVES)
                eng.wait_ge(e_d_in[par], loads(e, par, 2))
                eng.activation(e_d_hi[par][:, :], e_w[par][:, GU:WE_N], ACT.Copy).then_inc(e_d_hi_set, 1)

            def turn_e(e, par):
                for h in range(HALVES):
                    eng.wait_ge(e_turned, e * HALVES + h + 1)
                    eng.activation(e_xt_hi[par][:, :, h * P:(h + 1) * P], banks[h][:, :].rearrange("p (k t) -> p k t", k=KD),
                                   ACT.Copy).then_inc(e_xt_hi_set, 1)

            def silu(e, f):
                eng.wait_ge(e_up, e * 2 + f + 1)
                eng.activation(e_s[:, f, :], banks[2 + f][:, 0:CAP], ACT.Silu).then_inc(e_silu, 1)

            def scale_y(e, n, first=False):
                eng.wait_ge(e_down, e * HALVES + 1)
                if not first:
                    eng.wait_ge(e_added, (e - 1) * (16 * HALVES))
                eng.wait_ge(e_slot_set, e + 1)
                eng.activation(e_y[n % 2][:, 0, :], banks[4][:, :], ACT.Copy,
                               scale=e_slot[n][:, 0, 1:2].bitcast(f32)).then_inc(e_y_a, 1)

            def expert(e, n, first, last):
                par = n % 2
                if not last:
                    split_up(e + 1, 1 - par)
                silu(e, 0)
                if not first:
                    scale_y(e - 1, (n - 1) % AHEAD, first=isinstance(e, int) and e <= 2)
                if not last:
                    turn_e(e + 1, 1 - par)
                    split_down(e + 1, 1 - par)
                silu(e, 1)

            split_up(0, 0)
            split_down(0, 0)
            turn_e(0, 0)
            expert_loop(eng, expert)
            scale_y(E - 1, AHEAD - 1)

        @block.tensor
        def _(eng):
            eng.wait_ge(consts_in, 16)

            def turn(name, src, t, g):
                wait_bank_free(eng, name, g)
                for k in range(KD):
                    last = eng.transpose(bank(name)[:, k * P:(k + 1) * P], src[:, t, k * P:(k + 1) * P], c["ident"])
                full(last, name)

            def rows(name, src_t, t, w, g):
                wait_bank_free(eng, name, g)
                for k in range(KD):
                    last = eng.matmul(bank(name)[:, :], src_t[:, k, t * P:(t + 1) * P], w[:, k, :],
                                      start=(k == 0), stop=(k == KD - 1))
                full(last, name)

            def columns(name, w, src_t, first, g):
                wait_bank_free(eng, name, g)
                for n in range(2):
                    for k in range(KD):
                        last = eng.matmul(bank(name)[:, n * GT:(n + 1) * GT], w[:, k, (first + n) * P:(first + n + 1) * P],
                                          src_t[:, k, :], start=(k == 0), stop=(k == KD - 1))
                full(last, name)

            def down(j, g):
                wait_evacuated(eng, f"h{j}", g)
                if j == 0:
                    eng.wait_ge(mlp_read, g * TILES + 1)
                s = chunk(j)[0]
                for t in range(TILES):
                    last = eng.matmul(banks[6 + t][:, :], h_t[:, j % 2, t * P:(t + 1) * P], cring[:, s, 2 * D:WJ],
                                      start=(j == 0), stop=(j == J - 1))
                last.then_inc(w_free[s], 1)

            def step(name, g):
                if name == "a_turn":
                    for t in range(TILES):
                        eng.wait_ge(xn_ready, g * TILES + t + 1)
                        turn(f"xT{t}", temp, t, g)
                elif name == "a_project":
                    if first(g):
                        eng.wait_ge(xw_in, 16)
                    eng.wait_ge(ctx_turned, g + 1)
                    ctx_cols = ctx_t[:, :, :].rearrange("p b s -> p (b s)")
                    for n in range(2):
                        wait_bank_free(eng, f"k{n}", g)
                        for m in range(2):
                            hg = 2 * n + m
                            last = eng.matmul(bank(f"k{n}")[:, m * GT:(m + 1) * GT], wk_x[:, hg * P:(hg + 1) * P],
                                              ctx_cols, start=True, stop=True)
                        full(last, f"k{n}")
                    for t in range(TILES):
                        wait_evacuated(eng, f"xT{t}", g)
                    for n in range(2):
                        columns(f"q{n}", wq_x, normed_t, 2 * n, g)
                    for t in range(TILES):
                        wait_bank_free(eng, f"v{t}", g)
                        full(eng.matmul(bank(f"v{t}")[:, :], ctx_cols[:, t * P:(t + 1) * P], wv_x,
                                        start=True, stop=True), f"v{t}")
                elif name == "a_scores":
                    for n in range(2):
                        wait_evacuated(eng, f"k{n}", g)
                        wait_evacuated(eng, f"q{n}", g)
                    for t in range(TILES):
                        wait_bank_free(eng, f"s{t}", g)
                        for hg in range(HG):
                            for b in range(TB):
                                last = eng.matmul(
                                    bank(f"s{t}")[32 * b:32 * b + 32, hg * P:(hg + 1) * P],
                                    q_t[:, hg, t * P + 32 * b:t * P + 32 * b + 32],
                                    k_diag[:, hg * GB + t * TB + b, :, :].rearrange("p a s -> p (a s)"),
                                    start=True, stop=True)
                        full(last, f"s{t}")
                elif name == "a_values":
                    for t in range(TILES):
                        wait_evacuated(eng, f"v{t}", g)
                        eng.wait_ge(probs_ready, g * TILES + t + 1)
                        wait_bank_free(eng, f"oT{t}", g)
                        for h in range(H):
                            a, hg = h % 4, h // 4
                            last = eng.matmul(bank(f"oT{t}")[32 * a:32 * a + 32, hg * P:(hg + 1) * P],
                                              v_sb[:, t, h * HD:(h + 1) * HD], pair_t[:, t, h, :],
                                              start=True, stop=True)
                        full(last, f"oT{t}")
                elif name == "a_out":
                    for t in range(TILES):
                        wait_evacuated(eng, f"oT{t}", g)
                        rows(f"w{t}", o_t, t, wo_x, g)
                elif name == "b_turn":
                    for t in range(TILES):
                        eng.wait_ge(yn_ready, g * TILES + t + 1)
                        turn(f"yT{t}", normed, t, g)
                elif name == "b_gate":
                    if first(g):
                        eng.wait_ge(gw_in, 16)
                        eng.wait_ge(small_in, 64)
                    for t in range(TILES):
                        wait_evacuated(eng, f"yT{t}", g)
                    wait_bank_free(eng, "kg", g)
                    for k in range(KD):
                        last = eng.matmul(bank("kg")[0:LR, 0:GT], wkg1[:, k, :], normed_t[:, k, :],
                                          start=(k == 0), stop=(k == KD - 1))
                    full(last, "kg")
                elif name == "b_values":
                    for t in range(TILES):
                        rows(f"gv{t}", normed_t, t, wv_g, g)
                elif name == "b_decay":
                    wait_evacuated(eng, "kg", g)
                    wait_bank_free(eng, "kz", g)
                    for n in range(GC):
                        last = eng.matmul(bank("kz")[:, n * GT:(n + 1) * GT], wkg2[:, n * P:(n + 1) * P], kg_sb[:, :],
                                          start=True, stop=True)
                    full(last, "kz")
                elif name == "b_silu":
                    for t in range(TILES):
                        rows(f"gg{t}", normed_t, t, wg_g, g)
                elif name == "b_keys":
                    columns("gq", wq_g, normed_t, 0, g)
                    columns("gk", wk_g, normed_t, 0, g)
                elif name == "b_scores":
                    wait_evacuated(eng, "gq", g)
                    wait_evacuated(eng, "gk", g)
                    for t in range(TILES):
                        for r in range(4):
                            wait_bank_free(eng, f"A{t}{r}", g)
                        for n in range(GC):
                            for par, q in ((0, q_even), (1, q_odd)):
                                for r in range(4):
                                    feats = slice(32 * r, 32 * r + 32)
                                    last = eng.matmul(bank(f"A{t}{r}")[:, (2 * n + par) * P:(2 * n + par + 1) * P],
                                                      k_dec[feats, n, t * P:(t + 1) * P], q[feats, n, t * P:(t + 1) * P],
                                                      start=True, stop=True)
                                    if n == GC - 1 and par == 1:
                                        full(last, f"A{t}{r}")
                elif name == "b_read":
                    for t in range(TILES):
                        wait_evacuated(eng, f"gv{t}", g)
                        for r in range(4):
                            wait_evacuated(eng, f"A{t}{r}", g)
                        wait_bank_free(eng, f"o{t}", g)
                        for h in range(H):
                            n, r, par = h // 8, h % 8 // 2, h % 2
                            last = eng.matmul(bank(f"o{t}")[:, h * HD:(h + 1) * HD], pair_t[:, t, 4 * r + 2 * n + par, :],
                                              v_sb[:, t, h * HD:(h + 1) * HD], start=True, stop=True)
                        full(last, f"o{t}")
                elif name == "b_turn_out":
                    for t in range(TILES):
                        eng.wait_ge(o_ready, g * TILES + t + 1)
                        turn(f"nT{t}", o_sb, t, g)
                elif name == "b_out":
                    for t in range(TILES):
                        wait_evacuated(eng, f"nT{t}", g)
                        rows(f"wo{t}", o_t, t, wo_g, g)
                elif name == "c_begin":
                    for t in range(TILES):
                        eng.wait_ge(y1n_ready, g * TILES + t + 1)
                        turn(f"mT{t}", normed, t, g)
                elif name == "c_norm":
                    down(J - 1, g)
                elif name == "c_turn":
                    for t in range(TILES):
                        eng.wait_ge(z_ready, g * TILES + t + 1)
                        turn(f"zT{t}", z, t, g)
                elif name == "c_route":
                    for t in range(TILES):
                        wait_evacuated(eng, f"zT{t}", g)
                    wait_bank_free(eng, "lg", g)
                    for t in range(TILES):
                        for k in range(KD):
                            last = eng.matmul(bank("lg")[:, t * E:(t + 1) * E], z_t[:, k, t * P:(t + 1) * P],
                                              w_gate[:, k, :], start=(k == 0), stop=(k == KD - 1))
                    full(last, "lg")
                elif name == "c_slots":
                    eng.wait_ge(chosen_ready, g * TILES + TILES)
                    eng.wait_ge(counted, g + 1)
                    wait_bank_free(eng, "ps", g)
                    eng.matmul(bank("ps")[:, 0:E], c["ones"], chosen_sum[:, :], start=True, stop=False)
                    eng.matmul(bank("ps")[:, 0:E], c["before"], chosen[:, 0, :], start=False, stop=True)
                    eng.matmul(bank("ps")[:, E:2 * E], c["ones"], chosen_sum[:, :], start=True, stop=False)
                    eng.matmul(bank("ps")[:, E:2 * E], c["ones"], chosen[:, 0, :], start=False, stop=False)
                    full(eng.matmul(bank("ps")[:, E:2 * E], c["before"], chosen[:, 1, :], start=False, stop=True), "ps")
                elif name[0] == "c" and name[1:].isdigit():
                    j = int(name[1:])
                    s, n, per = chunk(j)
                    if j == 0:
                        for t in range(TILES):
                            wait_evacuated(eng, f"mT{t}", g)
                    eng.wait_ge(w_loaded[s], (g * per + n + 1) * 16)
                    wait_bank_free(eng, f"h{j}", g)
                    w = cring[:, s, 0:2 * D].rearrange("p (m k f) -> p m k f", m=2, k=KD)
                    for m in range(2):
                        for k in range(KD):
                            last = eng.matmul(bank(f"h{j}")[:, m * GT:(m + 1) * GT], w[:, m, k, :], normed2_t[:, k, :],
                                              start=(k == 0), stop=(k == KD - 1))
                    full(last, f"h{j}")
                    if j:
                        down(j - 1, g)

            iterate(eng, step)
            if phases < 2:
                return

            def turn_e(e, n):
                eng.wait_ge(e_rows[n], loads(e, n, AHEAD, HALVES))
                for h in range(HALVES):
                    if not (isinstance(e, int) and e == 0):
                        eng.wait_ge(e_xt_lo_set, (e - 1) * HALVES + h + 1)
                    for k in range(KD):
                        last = eng.transpose(banks[h][:, k * P:(k + 1) * P], e_x[n][:, h, k * P:(k + 1) * P], c["ident"])
                    last.then_inc(e_turned, 1)

            def three_passes(out_, w_hi, w_lo, m_hi, m_lo, start, stop):
                eng.matmul(out_, w_hi, m_hi, start=start, stop=False)
                eng.matmul(out_, w_hi, m_lo, start=False, stop=False)
                return eng.matmul(out_, w_lo, m_hi, start=False, stop=stop)

            def up(e, par, f, first):
                if f == 0:
                    eng.wait_ge(e_gu_lo_set, e + 1)
                    eng.wait_ge(e_xt_lo_set, (e + 1) * HALVES)
                if not first:
                    eng.wait_ge(e_h_set, e * 2 - 1 + f)
                hi, lo = (w[par][:, :].rearrange("p (m k f) -> p m k f", m=2, k=KD) for w in (e_gu_hi, e_gu_lo))
                cols = slice(f * P, (f + 1) * P)
                for m in range(2):
                    for k in range(KD):
                        last = three_passes(banks[2 + f][:, m * CAP:(m + 1) * CAP], hi[:, m, k, cols], lo[:, m, k, cols],
                                            e_xt_hi[par][:, k, :], e_xt_lo[par][:, k, :], k == 0, k == KD - 1)
                last.then_inc(e_up, 1)

            def down_e(e, par, first):
                eng.wait_ge(e_d_lo_set, e + 1)
                hi, lo = (w[par][:, :].rearrange("p (f d) -> p f d", d=D) for w in (e_d_hi, e_d_lo))
                eng.wait_ge(e_h_lo_set, e * 2 + 2)
                for h in range(HALVES):
                    if not first:
                        eng.wait_ge((e_y_a, e_y_v)[h], e)
                    cols = slice(h * P, (h + 1) * P)
                    for f in range(2):
                        last = three_passes(banks[4 + h][:, :], e_h_hi[par][:, f, cols], e_h_lo[par][:, f, cols],
                                            hi[:, f, :], lo[:, f, :], f == 0, f == 1)
                    last.then_inc(e_down, 1)

            def expert(e, n, first, last):
                par = n % 2
                up(e, par, 0, first)
                if not first:
                    down_e(e - 1, 1 - par, first=isinstance(e, int) and e == 1)
                if not last:
                    turn_e(e + 1, (n + 1) % AHEAD)
                up(e, par, 1, first)

            turn_e(0, 0)
            expert_loop(eng, expert)
            down_e(E - 1, 1, False)

        @block.vector
        def _(eng):
            eng.wait_ge(consts_in, 16)
            eng.wait_ge(small_in, 64)
            eng.wait_ge(zeroed, 6)
            tok_set = Chain(eng, tok_ready, 0)
            for t in range(TILES):
                tok_set.add(eng.tensor_scalar(tok[:, t:t + 1], c["token"], float(t * P), None, ALU.add))
            tok_set.settle()
            chains = {}

            def chain(which, g):
                if which not in chains:
                    sem_, per = {"next": (v_next, V_N), "ab": (v_ab, V_AB), "c": (v_c, V_C)}[which]
                    chains[which] = Chain(eng, sem_, g * per)
                return chains[which]

            def end(which):
                n = chains.pop(which).n
                assert n == {"next": V_N, "ab": V_AB, "c": V_C}[which], (which, n)

            def heads(ap):
                return ap.rearrange("p (h d) -> p h d", d=HD)

            def per_head(ap):
                return ap.unsqueeze(2).to_broadcast([P, H, HD])

            def moments(ch, src, st, m):
                for t in range(TILES):
                    ch.add(eng.bn_stats(st[:, t, :], src[:, t, :]))
                ch.settle()
                apart(eng)
                for t in range(TILES):
                    ch.add(eng.bn_aggr(m[:, t, :], st[:, t, :]))
                ch.settle()

            r2 = rstd[:, :, :].rearrange("p t h -> p (t h)")
            v2 = var_e[:, :, :].rearrange("p t h -> p (t h)")
            spare = row_max[:, :, :].rearrange("p t h -> p (t h)")

            def step(name, g):
                if name == "next_norm":
                    eng.wait_ge(x_loaded, (g + 1) * 16)
                    moments(chain("next", g), x_in, n_stats, n_mv)
                    end("next")
                    eng.tensor_scalar(n_var[:, :], n_mv[:, :, 1], EPS, None, ALU.add).then_inc(n_var_ready, 1)
                    eng.wait_ge(n_rstd_ready, g + 1)
                    for t in range(TILES):
                        eng.tensor_scalar(temp[:, t, :], x_in[:, t, :], n_mv[:, t, 0:1], n_rstd[:, t:t + 1],
                                          ALU.subtract, ALU.mult).then_inc(xn_ready, 1)
                elif name == "a_project":
                    wait_full(eng, "k1", g)
                    for a in range(4):
                        rows = slice(32 * a, 32 * a + 32)
                        last = eng.tensor_copy(k_diag[rows, 2 * GB:4 * GB, a, :],
                                               bank("k1")[rows, :].rearrange("p (n s) -> p n s", s=SEQ))
                    freed(last, "k1")
                    wait_full(eng, "q1", g)
                    freed(eng.tensor_scalar(q_t[:, 2:4, :], bank("q1")[:, :].rearrange("p (a t) -> p a t", a=2),
                                            HD ** -0.5, None, ALU.mult), "q1")
                    wait_full(eng, "v1", g)
                    freed(eng.tensor_copy(v_sb[:, 1, :], bank("v1")[:, :]), "v1")
                elif name == "a_scores":
                    ch = chain("ab", g)
                    for t in range(TILES):
                        wait_full(eng, f"s{t}", g)
                        freed(eng.tensor_tensor(heads(probs[:, t, :]), heads(bank(f"s{t}")[:, :]),
                                                c["causal_add"].unsqueeze(1).to_broadcast([P, H, SEQ]), ALU.add), f"s{t}")
                        wait_evacuated(eng, f"s{t}", g)
                        ch.link(eng.tensor_reduce(row_max[:, t, :], heads(probs[:, t, :]), AX.X, ALU.max))
                        eng.tensor_tensor(heads(probs[:, t, :]), heads(probs[:, t, :]), per_head(row_max[:, t, :]),
                                          ALU.subtract).then_inc(centered, 1)
                elif name == "a_probs":
                    ch = chain("ab", g)
                    for t in range(TILES):
                        eng.wait_ge(exped, g * TILES + t + 1)
                        ch.link(eng.tensor_reduce(row_sum[:, t, :], heads(probs[:, t, :]), AX.X, ALU.add))
                        ch.link(eng.reciprocal(row_sum[:, t, :], row_sum[:, t, :]))
                        ch.link(eng.tensor_tensor(heads(probs[:, t, :]), heads(probs[:, t, :]),
                                                  per_head(row_sum[:, t, :]), ALU.mult))
                        for b in range(TB):
                            rows = slice(32 * b, 32 * b + 32)
                            last = eng.transpose(pair_t[rows, t, :, 32 * b:32 * b + 32], heads(probs[rows, t, :]))
                        last.then_inc(probs_ready, 1)
                elif name == "a_out":
                    ch = chain("ab", g)
                    for t in range(TILES):
                        wait_full(eng, f"w{t}", g)
                        freed(eng.tensor_tensor(x1[:, t, :], x_in[:, t, :], bank(f"w{t}")[:, :], ALU.add), f"w{t}")
                    wait_evacuated(eng, "w0", g)
                    wait_evacuated(eng, "w1", g)
                    moments(ch, x1, stats, mv)
                    eng.tensor_scalar(v2[:, 0:TILES], mv[:, :, 1], EPS, None, ALU.add).then_inc(var_ready, 1)
                    eng.wait_ge(rstd_ready, g * 5 + 1)
                    for t in range(TILES):
                        ch.add(eng.tensor_scalar(y[:, t, :], x1[:, t, :], mv[:, t, 0:1], r2[:, t:t + 1],
                                                 ALU.subtract, ALU.mult))
                    ch.link(eng.tensor_tensor(spare[:, 0:TILES], mv[:, :, 1], r2[:, 0:TILES], ALU.mult))
                    ch.link(eng.tensor_tensor(spare[:, 0:TILES], spare[:, 0:TILES], r2[:, 0:TILES], ALU.mult))
                    eng.tensor_scalar(v2[:, 0:TILES], spare[:, 0:TILES], EPS, None, ALU.add).then_inc(var_ready, 1)
                    eng.wait_ge(rstd_ready, g * 5 + 2)
                    for t in range(TILES):
                        eng.tensor_scalar(normed[:, t, :], y[:, t, :], r2[:, t:t + 1], None, ALU.mult).then_inc(yn_ready, 1)
                elif name == "b_turn":
                    for t in range(TILES):
                        wait_full(eng, f"yT{t}", g)
                        freed(eng.tensor_tensor(normed_t[:, :, t * P:(t + 1) * P],
                                                bank(f"yT{t}")[:, :].rearrange("p (k t) -> p k t", k=KD),
                                                ln1.unsqueeze(2).to_broadcast([P, KD, P]), ALU.mult), f"yT{t}")
                elif name == "b_decay":
                    ch = chain("ab", g)
                    wait_full(eng, "kz", g)
                    for n in range(GC):
                        cols = slice(n * GT, (n + 1) * GT)
                        ins = eng.tensor_scalar(gate_z[:, cols], bank("kz")[:, cols], bkg[:, n:n + 1], None, ALU.add)
                        if n == 0:
                            ch.add(ins)
                    freed(ins, "kz")
                    wait_evacuated(eng, "kz", g)
                    eng.tensor_scalar(spare[:, 0:1], mv[:, 0, 0:1], 1.0, None, ALU.mult).then_inc(z_in, 1)
                    eng.wait_ge(softplus_done, g + 1)
                    ch.link(eng.scalar_tensor_tensor(gate_z[:, :], gate_z[:, :], 0.0, gate_e[:, :], ALU.min, ALU.subtract))
                    ch.link(eng.tensor_tensor_scan(gate_sum[:, :], c["restart"], gate_z[:, :], 0.0, ALU.mult, ALU.add))
                    sums = gate_sum[:, :].rearrange("p (n s) -> p n s", s=SEQ)
                    ch.link(eng.tensor_tensor(gate_z[:, :].rearrange("p (n s) -> p n s", s=SEQ), sums,
                                              sums[:, :, SEQ // 2 - 1:SEQ // 2].to_broadcast([P, GC * GB, SEQ]), ALU.subtract))
                    eng.tensor_scalar(gate_z[:, :], gate_z[:, :], -80.0 * NORMALIZER, 80.0 * NORMALIZER,
                                      ALU.max, ALU.min).then_inc(decay_in, 1)
                elif name == "b_silu":
                    ch = chain("ab", g)
                    for t in range(TILES):
                        wait_full(eng, f"gg{t}", g)
                        freed(eng.tensor_tensor(silu_g[:, t, :], bank(f"gg{t}")[:, :], bg_b[:, :], ALU.add), f"gg{t}")
                    for t in range(TILES):
                        eng.wait_ge(g_tanhed, g * TILES + t + 1)
                        ch.add(eng.scalar_tensor_tensor(silu_g[:, t, :], temp[:, t, :], 1.0, silu_g[:, t, :], ALU.add, ALU.mult))
                elif name == "b_keys":
                    ch = chain("ab", g)
                    eng.wait_ge(decays, g + 1)
                    wait_full(eng, "gq", g)
                    ch.add(eng.scalar_tensor_tensor(q_even.rearrange("p c t -> p (c t)"), bank("gq")[:, :], c["even"], grow,
                                                    ALU.mult, ALU.mult))
                    freed(eng.scalar_tensor_tensor(q_odd.rearrange("p c t -> p (c t)"), bank("gq")[:, :], c["odd"], grow,
                                                   ALU.mult, ALU.mult), "gq")
                    wait_full(eng, "gk", g)
                    freed(eng.scalar_tensor_tensor(k_dec[:, :, :].rearrange("p c t -> p (c t)"), bank("gk")[:, :], HD ** -0.5,
                                                   shrink, ALU.mult, ALU.mult), "gk")
                elif name == "b_scores":
                    for t in range(TILES):
                        for r in range(4):
                            wait_full(eng, f"A{t}{r}", g)
                            freed(eng.tensor_tensor(pair_t[:, t, 4 * r:4 * r + 4, :],
                                                    bank(f"A{t}{r}")[:, :].rearrange("p (n t) -> p n t", t=P),
                                                    c["causal_mul"].unsqueeze(1).to_broadcast([P, 4, P]), ALU.mult), f"A{t}{r}")
                elif name == "b_read":
                    ch = chain("ab", g)
                    for t in range(TILES):
                        wait_full(eng, f"o{t}", g)
                        o = heads(bank(f"o{t}")[:, :])
                        ch.link(eng.tensor_reduce(head_mean[:, t, :], o, AX.X, ALU.add))
                        ch.link(eng.tensor_scalar(head_mean[:, t, :], head_mean[:, t, :], 1.0 / HD, None, ALU.mult))
                        freed(eng.tensor_tensor(heads(o_sb[:, t, :]), o, per_head(head_mean[:, t, :]), ALU.subtract), f"o{t}")
                        wait_evacuated(eng, f"o{t}", g)
                        eng.tensor_scalar(spare[:, 0:1], mv[:, 0, 0:1], 1.0, None, ALU.mult).then_inc(o_centered, 1)
                    for t in range(TILES):
                        eng.wait_ge(o_squared, g * TILES + t + 1)
                        ch.link(eng.tensor_reduce(row_sum[:, t, :], heads(temp[:, t, :]), AX.X, ALU.add))
                        eng.tensor_scalar(var_e[:, t, :], row_sum[:, t, :], 1.0 / HD, EPS,
                                          ALU.mult, ALU.add).then_inc(var_ready, 1)
                elif name == "b_read2":
                    ch = chain("ab", g)
                    for t in range(TILES):
                        eng.wait_ge(rstd_ready, g * 5 + 3 + t)
                        ch.link(eng.tensor_tensor(heads(o_sb[:, t, :]), heads(o_sb[:, t, :]), per_head(rstd[:, t, :]), ALU.mult))
                        eng.scalar_tensor_tensor(o_sb[:, t, :], o_sb[:, t, :], 0.5, silu_g[:, t, :],
                                                 ALU.mult, ALU.mult).then_inc(o_ready, 1)
                elif name == "b_out":
                    ch = chain("ab", g)
                    for t in range(TILES):
                        wait_full(eng, f"wo{t}", g)
                        freed(eng.tensor_tensor(y[:, t, :], y[:, t, :], bank(f"wo{t}")[:, :], ALU.add), f"wo{t}")
                    wait_evacuated(eng, "wo0", g)
                    wait_evacuated(eng, "wo1", g)
                    moments(ch, y, stats, mv)
                    ch.link(eng.tensor_tensor(spare[:, 0:TILES], mv[:, :, 0], mv[:, :, 0], ALU.mult))
                    ch.link(eng.tensor_tensor(spare[:, 0:TILES], spare[:, 0:TILES], mv[:, :, 1], ALU.add))
                    eng.tensor_scalar(v2[:, 0:TILES], spare[:, 0:TILES], EPS, None, ALU.add).then_inc(var_ready, 1)
                    for t in range(TILES):
                        ch.add(eng.tensor_tensor(resid[:, t, :], x1[:, t, :], y[:, t, :], ALU.add))
                    eng.wait_ge(rstd_ready, g * 5 + 5)
                    for t in range(TILES):
                        eng.tensor_scalar(normed[:, t, :], y[:, t, :], r2[:, t:t + 1], None, ALU.mult).then_inc(y1n_ready, 1)
                    ch.settle()
                    end("ab")
                elif name == "c_begin":
                    for t in range(TILES):
                        wait_full(eng, f"mT{t}", g)
                        freed(eng.tensor_tensor(normed2_t[:, :, t * P:(t + 1) * P],
                                                bank(f"mT{t}")[:, :].rearrange("p (k t) -> p k t", k=KD),
                                                ln2.unsqueeze(2).to_broadcast([P, KD, P]), ALU.mult), f"mT{t}")
                elif name == "c_norm":
                    ch = chain("c", g)
                    s, n, per = chunk(J - 1)
                    eng.wait_ge(w_free[s], g * per + n + 1)
                    for t in range(TILES):
                        eng.tensor_tensor(x2[:, t, :], resid[:, t, :], banks[6 + t][:, :], ALU.add).then_inc(mlp_read, 1)
                    eng.wait_ge(mlp_read, (g + 1) * TILES + 1)
                    moments(ch, x2, c_stats, c_mv)
                    eng.tensor_scalar(c_var[:, :], c_mv[:, :, 1], EPS, None, ALU.add).then_inc(c_var_ready, 1)
                    eng.wait_ge(c_rstd_ready, g + 1)
                    for t in range(TILES):
                        eng.tensor_scalar(z[:, t, :], x2[:, t, :], c_mv[:, t, 0:1], c_rstd[:, t:t + 1],
                                          ALU.subtract, ALU.mult).then_inc(z_ready, 1)
                elif name == "c_route":
                    ch = chain("c", g)
                    wait_full(eng, "lg", g)
                    freed(eng.tensor_copy(logits[:, :, :], bank("lg")[:, 0:TILES * E].rearrange("p (t e) -> p t e", e=E)), "lg")
                    wait_evacuated(eng, "lg", g)
                    for t in range(TILES):
                        apart(eng)
                        ch.link(eng.max(top[:, t, :], logits[:, t, :]))
                        eng.tensor_scalar(neg_max[:, t:t + 1], top[:, t, 0:1], -1.0, None, ALU.mult).then_inc(lg_centered, 1)
                elif name == "c_mask":
                    ch = chain("c", g)
                    for t in range(TILES):
                        eng.wait_ge(lg_exped, g * TILES + t + 1)
                        ch.link(eng.reciprocal(esum[:, t:t + 1], esum[:, t:t + 1]))
                        ch.link(eng.tensor_scalar(logits[:, t, :], logits[:, t, :], esum[:, t:t + 1], None, ALU.mult))
                        apart(eng)
                        ch.link(eng.max(top[:, t, :], logits[:, t, :]))
                        apart(eng)
                        ch.add(eng.max_index(top_id[:, t, :], top[:, t, :], logits[:, t, :]))
                        ch.link(eng.match_replace(left[:, t, :], top[:, t, :], logits[:, t, :], -1.0))
                        eng.tensor_scalar(chosen[:, t, :], left[:, t, :], 0.0, None, ALU.is_lt).then_inc(chosen_ready, 1)
                    ch.settle()
                    eng.tensor_copy(top_idf[:, :, :], top_id[:, :, :]).then_inc(counted, 1)
                elif name == "c_slots":
                    ch = chain("c", g)
                    wait_full(eng, "ps", g)
                    freed(eng.tensor_copy(pos[:, :, :], bank("ps")[:, 0:TILES * E].rearrange("p (t e) -> p t e", e=E)), "ps")
                    wait_evacuated(eng, "ps", g)
                    eng.wait_ge(counted, g + 1)
                    for t in range(TILES):
                        ch.link(eng.tensor_tensor(chosen_sum[:, :], chosen_sum[:, :], chosen[:, t, :], ALU.add))
                    ids = c["expert_slot"].unsqueeze(1).to_broadcast([P, TILES, E])
                    ch.add(eng.tensor_scalar(late[:, :, :], pos[:, :, :], float(P), -float(P * P - 1), ALU.is_ge, ALU.mult))
                    ch.link(eng.scalar_tensor_tensor(slot[:, :, :], pos[:, :, :], float(P), ids, ALU.mult, ALU.add))
                    ch.link(eng.tensor_tensor(slot[:, :, :], slot[:, :, :], late[:, :, :], ALU.add))
                    ch.link(eng.tensor_scalar(late[:, :, :], pos[:, :, :], float(CAP), FAR, ALU.is_ge, ALU.mult))
                    ch.link(eng.tensor_tensor(slot[:, :, :], slot[:, :, :], late[:, :, :], ALU.add))
                    eng.wait_ge(payload_sent, g + 1)
                    for t in range(TILES):
                        for k in range(TOP):
                            ch.link(eng.scalar_tensor_tensor(junk[:, :], c["expert_id"], top_idf[:, t, k:k + 1], slot[:, t, :],
                                                             ALU.is_equal, ALU.mult, accum_out=slot_f[:, t, k:k + 1]))
                        ch.add(eng.tensor_copy(slot_i[:, t, :], slot_f[:, t, :]))
                        ch.add(eng.tensor_copy(payload[:, t, :, 0], tok[:, t:t + 1].to_broadcast([P, TOP])))
                        ch.link(eng.tensor_copy(payload[:, t, :, 1].bitcast(f32), top[:, t, :]))
                        eng.tensor_scalar(tok[:, t:t + 1], tok[:, t:t + 1], float(GT), None, ALU.add).then_inc(payload_ready, 1)
                    eng.wait_ge(payload_ready, (g + 1) * TILES)
                    eng.wait_ge(rows_stored, (g + 1) * 32)
                    end("c")
                elif name[0] == "c" and name[1:].isdigit():
                    ch = chain("c", g)
                    j = int(name[1:])
                    eng.wait_ge(h_tanhed, g * J + j + 1)
                    if j == 0:
                        eng.wait_ge(rows_zeroed, 32)
                    ch.link(eng.scalar_tensor_tensor(h_e, h_e, 1.0, bank(f"h{j}")[:, 0:GT], ALU.add, ALU.mult))
                    freed(eng.scalar_tensor_tensor(h_t[:, j % 2, :], h_e, 0.5, bank(f"h{j}")[:, GT:2 * GT],
                                                   ALU.mult, ALU.mult), f"h{j}")

            iterate(eng, step)
            if phases < 2:
                return

            def split_up(e, par):
                eng.wait_ge(e_gu_hi_set, e + 1)
                eng.tensor_tensor(e_gu_lo[par][:, :], e_w[par][:, 0:GU], e_gu_hi[par][:, :].bitcast(f32),
                                  ALU.subtract).then_inc(e_gu_lo_set, 1)

            def split_down(e, par):
                eng.wait_ge(e_d_hi_set, e + 1)
                eng.tensor_tensor(e_d_lo[par][:, :], e_w[par][:, GU:WE_N], e_d_hi[par][:, :].bitcast(f32),
                                  ALU.subtract).then_inc(e_d_lo_set, 1)

            def turn_e(e, par):
                for h in range(HALVES):
                    eng.wait_ge(e_xt_hi_set, e * HALVES + h + 1)
                    cols = slice(h * P, (h + 1) * P)
                    eng.tensor_tensor(e_xt_lo[par][:, :, cols], banks[h][:, :].rearrange("p (k t) -> p k t", k=KD),
                                      e_xt_hi[par][:, :, cols].bitcast(f32), ALU.subtract).then_inc(e_xt_lo_set, 1)

            def gate(e, par, f):
                eng.wait_ge(e_silu, e * 2 + f + 1)
                eng.tensor_tensor(e_h[:, f, :], e_s[:, f, :], banks[2 + f][:, CAP:2 * CAP], ALU.mult).then_inc(e_h_set, 1)
                eng.wait_ge(e_h_set, e * 2 + f + 1)
                eng.tensor_copy(e_h_hi[par][:, f, :], e_h[:, f, :]).then_inc(e_h_hi_set, 1)
                eng.wait_ge(e_h_hi_set, e * 2 + f + 1)
                eng.tensor_tensor(e_h_lo[par][:, f, :], e_h[:, f, :], e_h_hi[par][:, f, :].bitcast(f32),
                                  ALU.subtract).then_inc(e_h_lo_set, 1)

            def scale_y(e, n, first=False):
                eng.wait_ge(e_down, e * HALVES + 2)
                if not first:
                    eng.wait_ge(e_added, (e - 1) * (16 * HALVES))
                eng.wait_ge(e_slot_set, e + 1)
                eng.tensor_scalar(e_y[n % 2][:, 1, :], banks[5][:, :], e_slot[n][:, 1, 1:2].bitcast(f32), None, ALU.mult)\
                   .then_inc(e_y_v, 1)

            def expert(e, n, first, last):
                par = n % 2
                if not last:
                    split_up(e + 1, 1 - par)
                gate(e, par, 0)
                if not first:
                    scale_y(e - 1, (n - 1) % AHEAD, first=isinstance(e, int) and e <= 2)
                if not last:
                    turn_e(e + 1, 1 - par)
                    split_down(e + 1, 1 - par)
                gate(e, par, 1)

            split_up(0, 0)
            split_down(0, 0)
            turn_e(0, 0)
            expert_loop(eng, expert)
            scale_y(E - 1, AHEAD - 1)


def loads(e, n, ring, each=1):
    return ((e - n) // ring + 1) * (16 * each) if isinstance(e, int) else (e - n + ring) * (16 // ring * each)


def expert_loop(eng, step):
    for e in range(AHEAD - 1):
        step(e, e, first=(e == 0), last=False)
    with eng.Fori(0, (E - AHEAD) // AHEAD) as m:
        for n in range(AHEAD - 1, 2 * AHEAD - 1):
            step(eng.snap(m * AHEAD + n), n % AHEAD, first=False, last=False)
    step(E - 1, AHEAD - 1, first=False, last=True)


def shape_constants():
    import numpy as np
    p = np.arange(P)
    a = {
        "ident": np.eye(P),
        "causal_add": np.where(np.arange(SEQ)[None, :] <= (p % SEQ)[:, None], 0.0, MASKED),
        "causal_mul": (p[:, None] // SEQ == p[None, :] // SEQ) & (p[:, None] <= p[None, :]),
        "before": p[:, None] < p[None, :],
        "ones": np.ones((P, P)),
        "restart": np.tile((np.arange(GC * GT) % SEQ != 0)[None, :], (P, 1)),
        "even": (p % 32 < GK)[:, None],
        "odd": (p % 32 >= GK)[:, None],
        "expert_id": np.tile(np.arange(E)[None, :], (P, 1)),
        "expert_slot": np.tile(HALVES * np.arange(E)[None, :], (P, 1)),
        "neg_half": np.full((P, 32), -0.5),
        "token": p[:, None],
    }
    return np.ascontiguousarray(np.concatenate([a[n].astype(np.float32) for n, _ in CONST], axis=1))


def lay_out(inputs):
    import numpy as np

    def chunks(w):
        k = w.shape[0] // P
        return w.reshape(k, P, -1).transpose(1, 0, 2).reshape(P, -1)

    g = {k: np.asarray(v) for k, v in inputs.items()}
    kv = g["L0_xattn_Wkv_expand"].T
    w13 = [g[n].reshape(KD, P, J, P).transpose(2, 1, 0, 3).reshape(J, P, D) for n in ("L0_attn_W1", "L0_attn_W3")]
    per_expert = [g[n].reshape(E, -1, P, g[n].shape[2]).transpose(0, 2, 1, 3).reshape(E, P, -1)
                  for n in ("L0_ffn_w_gate", "L0_ffn_w_up", "L0_ffn_w_down")]
    arrays = {
        "x": g["x"].reshape(T, D),
        "ctxt": g["ctx_512"].reshape(GROUPS, GB, CTX, CD).transpose(0, 3, 2, 1),
        "consts": shape_constants(),
        "vecs": np.concatenate([g["L0_attn_ln1_w"].reshape(KD, P).T, g["L0_attn_ln2_w"].reshape(KD, P).T,
                                g["L0_attn_bkg2"].reshape(GC, P).T], axis=1),
        "bg_row": g["L0_attn_bg"].reshape(1, D),
        "xw": np.concatenate([chunks(g["L0_xattn_Wq"].T), kv, chunks(g["L0_xattn_Wout"].T)], axis=1),
        "gw": np.concatenate([chunks(g[f"L0_attn_{n}"]) for n in ("Wq", "Wk", "Wv", "Wg", "Wo", "Wkg1")], axis=1),
        "kg2": g["L0_attn_Wkg2"],
        "cw": np.concatenate(w13 + [g["L0_attn_W2"].reshape(J, P, D)], axis=2),
        "gate_w": g["L0_ffn_gate_w"].T.reshape(KD, P, E).transpose(1, 0, 2),
        "ew": np.concatenate(per_expert, axis=2),
    }
    return {k: np.ascontiguousarray(v) for k, v in arrays.items()}


def kernel(**inputs):
    import concourse.bacc as bacc
    from concourse.bass_utils import run_bass_kernel_spmd

    nc = bacc.Bacc("TRN2", target_bir_lowering=False, num_devices=1)
    arrays = lay_out(inputs)
    handles = {k: nc.dram_tensor(f"in_{k}", v.shape, mybir.dt.from_np(v.dtype), kind="ExternalInput").ap()
               for k, v in arrays.items()}
    out = nc.dram_tensor("out", (ROWS, D), mybir.dt.float32, kind="ExternalOutput").ap()
    build(nc, out=out, **handles)
    result = run_bass_kernel_spmd(nc, [{f"in_{k}": v for k, v in arrays.items()}], core_ids=[0])
    return result.results[0]["out"][0:T].reshape(BATCH, SEQ, D)
```

```python
import concourse.bass as bass
from concourse import mybir
from contextlib import ExitStack

BATCH, SEQ, D = 64, 32, 512
CTX, CD = 257, 128
P = 128
T = BATCH * SEQ
TILES = 2
GT = TILES * P
GROUPS = T // GT
GB = GT // SEQ
TB = P // SEQ
KD = D // P
H, HD = 16, 32
HG = H // 4
GK = 16
GC = H * GK // P
LR = 16
F1 = 1408
J = F1 // P
SLOTS = 2
PARTS = slice(0, 2 * D), slice(2 * D, 3 * D)
WJ = 2 * D + D
E, TOP, CAP, FE = 64, 8, 256, 256
HALVES = CAP // P
AHEAD = 4
WE_N = 2 * KD * FE + (FE // P) * D
ROWS = T + CAP
EPS = 1e-5
NORMALIZER = 16.0
MASKED = -1.0e30
FAR = float(1 << 20)

CONST = [("ident", P), ("causal_add", SEQ), ("causal_mul", P), ("before", P), ("ones", P),
         ("restart", GC * GT), ("even", 1), ("odd", 1), ("expert_id", E), ("expert_slot", E),
         ("neg_half", 32), ("token", 1)]
CONST_N = sum(n for _, n in CONST)
VEC_N = 2 * KD + GC
XW_N = KD * D + 2 * D + KD * D
GW_N = 2 * KD * GC * P + 3 * KD * D + KD * LR

AB_USES = ["xT0", "xT1", "k0", "k1", "q0", "q1", "v0", "v1", "s0", "s1", "oT0", "oT1", "w0", "w1",
           "yT0", "yT1", "kg", "gv0", "gv1", "kz", "gg0", "gg1", "gq", "gk",
           "A00", "A01", "A02", "A03", "A10", "A11", "A12", "A13",
           "o0", "o1", "nT0", "nT1", "wo0", "wo1"]
AB_BANKS = 4
C_USES = ["mT0", "mT1"] + [f"h{j}" for j in range(J)] + ["zT0", "zT1", "lg", "ps"]
C_BANKS = 2


def place(name):
    uses, banks, first = (AB_USES, AB_BANKS, 0) if name in AB_USES else (C_USES, C_BANKS, AB_BANKS)
    n = uses.index(name)
    return first + n % banks, n // banks, len(range(n % banks, len(uses), banks))


TIMELINE = ["a_scores0", "a_scores1", "c0", "c1", "cy0", "cu2", "cd2", "a_probs0", "a_probs1", "cu3", "c2",
            "a_values0", "cy1", "cd3", "cu4", "a_values1", "a_out", "c3", "cy2", "c4", "cd4", "b_turn",
            "cy3", "b_gate", "cu5", "cu6", "b_values", "cd5", "b_decay", "c5", "b_silu", "b_keys",
            "next_load", "cy4", "cy5", "cu7", "cd6", "cd7", "b_scores0", "c6", "b_scores1", "cu8", "cy6",
            "b_read0", "b_read1", "b_variance0", "b_variance1", "cd8", "c7", "b_gated0", "cu9", "b_gated1",
            "c8", "cy7", "cu10", "c9", "cd9", "cy8", "next_norm", "c10", "b_turn_out0", "cy9", "cd10",
            "b_turn_out1", "cy10", "c_norm", "bu0", "b_out", "c_turn", "next_turn", "c_route", "c_mask",
            "next_keys", "next_queries0", "c_slots", "b_again", "c_pick", "bu1", "next_queries1", "bd0",
            "next_values", "bd1", "c_scatter", "b_begin"]

C_ALONE = [name for j in range(J + 1) for name in (f"c{j}", f"cu{j + 2}", f"cy{j - 1}", f"cd{j + 1}") if name in TIMELINE]
C_ALONE += [name for name in TIMELINE if name[:2] == "c_"]

V_N, V_AB, V_C, A_AB = 4, 36, 67, 3

SPLITS = {("b" if j < 2 else "c") + "ud"[part] + str(j): (j, part) for j in range(J) for part in range(2)}


def first(g):
    return isinstance(g, int) and g == 0


class Chain:

    def __init__(self, eng, sem, base):
        self.eng, self.sem, self.base, self.n = eng, sem, base, 0

    def add(self, ins):
        ins.then_inc(self.sem, 1)
        self.n += 1

    def settle(self):
        self.eng.wait_ge(self.sem, self.base + self.n)

    def link(self, ins):
        self.add(ins)
        self.settle()


def build(nc, x, ctxt, consts, vecs, bg_row, xw, gw, kg2, cw, gate_w, ew, out, phases=2):
    f32, i32, u32 = mybir.dt.float32, mybir.dt.int32, mybir.dt.uint32
    f32r = mybir.dt.float32r
    ALU, ACT, AX = mybir.AluOpType, mybir.ActivationFunctionType, mybir.AxisListType

    stack = ExitStack()
    with stack:
        def sb(name, shape, dt=f32):
            return stack.enter_context(nc.sbuf_tensor(name, shape, dt))

        def sem(name):
            return stack.enter_context(nc.semaphore(name))

        z_rows = nc.dram_tensor("z_rows", (ROWS, D), f32, kind="Internal").ap()
        slots_d = nc.dram_tensor("slots_d", (E * CAP, 2), i32, kind="Internal").ap()

        wkg2 = sb("wkg2", [LR, GC * P])
        w_gate = sb("w_gate", [P, KD, E])
        cring = sb("cring", [P, SLOTS, WJ])
        cring_hi = sb("cring_hi", [P, SLOTS, WJ], f32r)
        cring_lo = sb("cring_lo", [P, SLOTS, WJ], f32r)
        const = sb("const", [P, CONST_N])
        c, col = {}, 0
        for name, n in CONST:
            c[name] = const[:, col:col + n]
            col += n
        vec = sb("vec", [P, VEC_N])
        ln1, ln2, bkg = vec[:, 0:KD], vec[:, KD:2 * KD], vec[:, 2 * KD:VEC_N]
        bg_b = sb("bg_b", [P, D])

        normed = sb("normed", [P, TILES, D])
        resid = sb("resid", [P, TILES, D])
        normed2_hi = sb("normed2_hi", [P, KD, GT], f32r)
        normed2_lo = sb("normed2_lo", [P, KD, GT], f32r)
        h_hi = sb("h_hi", [P, 2, GT], f32r)
        h_lo = sb("h_lo", [P, 2, GT], f32r)
        z_t = sb("z_t", [P, KD, GT])
        x2, z = resid, normed
        normed2 = z_t[:, :, :].rearrange("p (t a) n -> p t (a n)", t=TILES).rearrange("p t (k n) -> p t k n", k=KD)
        h_e, h_f = z_t[:, 2, :], z_t[:, 3, :]

        stats = sb("stats", [P, TILES, 6])
        mv = sb("mv", [P, TILES, 2])
        var_e = sb("var_e", [P, TILES, H])
        rstd = sb("rstd", [P, TILES, H])
        row_max = sb("row_max", [P, TILES, H])
        row_sum = sb("row_sum", [P, TILES, H])
        head_mean = sb("head_mean", [P, TILES, H])
        n_stats = sb("n_stats", [P, TILES, 6])
        n_mv = sb("n_mv", [P, TILES, 2])
        n_var = sb("n_var", [P, TILES])
        n_rstd = sb("n_rstd", [P, TILES])
        c_stats = sb("c_stats", [P, TILES, 6])
        c_mv = sb("c_mv", [P, TILES, 2])
        c_var = sb("c_var", [P, TILES])
        c_rstd = sb("c_rstd", [P, TILES])
        logits = sb("logits", [P, TILES, E])
        neg_max = sb("neg_max", [P, TILES])
        esum = sb("esum", [P, TILES])
        top = sb("top", [P, TILES, TOP])
        top_id = sb("top_id", [P, TILES, TOP], u32)
        top_idf = sb("top_idf", [P, TILES, TOP])
        left = sb("left", [P, TILES, E])
        chosen = sb("chosen", [P, TILES, E])
        chosen_sum = sb("chosen_sum", [P, E])
        pos = sb("pos", [P, TILES, E])
        slot = sb("slot", [P, TILES, E])
        late = sb("late", [P, TILES, E])
        slot_f = sb("slot_f", [P, TILES, TOP])
        slot_i = sb("slot_i", [P, TILES, TOP], i32)
        payload = sb("payload", [P, TILES, TOP, 2], i32)
        tok = sb("tok", [P, TILES])
        table = sb("table", [P, E * HALVES, 2], i32)

        e_slot = [sb(f"e_slot{n}", [P, HALVES, 2], i32) for n in range(AHEAD)]

        attentions = ExitStack()

        def ab(name, shape, dt=f32):
            return attentions.enter_context(nc.sbuf_tensor(name, shape, dt))

        weights = ab("weights", [P, XW_N + GW_N])
        wq_x = weights[:, 0:KD * D].rearrange("p (k n) -> p k n", k=KD)
        wk_x = weights[:, KD * D:KD * D + D]
        wv_x = weights[:, KD * D + D:KD * D + 2 * D]
        wo_x = weights[:, KD * D + 2 * D:XW_N].rearrange("p (k n) -> p k n", k=KD)
        at = XW_N
        wq_g = weights[:, at:at + KD * GC * P].rearrange("p (k n) -> p k n", k=KD); at += KD * GC * P
        wk_g = weights[:, at:at + KD * GC * P].rearrange("p (k n) -> p k n", k=KD); at += KD * GC * P
        wv_g = weights[:, at:at + KD * D].rearrange("p (k n) -> p k n", k=KD); at += KD * D
        wg_g = weights[:, at:at + KD * D].rearrange("p (k n) -> p k n", k=KD); at += KD * D
        wo_g = weights[:, at:at + KD * D].rearrange("p (k n) -> p k n", k=KD); at += KD * D
        wkg1 = weights[:, at:at + KD * LR].rearrange("p (k n) -> p k n", k=KD)
        x_in = ab("x_in", [P, TILES, D])
        ctx_in = ab("ctx_in", [P, SEQ, GB])
        ctx_t = ab("ctx_t", [P, GB, SEQ])
        normed_t = ab("normed_t", [P, KD, GT])
        q_t = ab("q_t", [P, HG, GT])
        k_diag = ab("k_diag", [P, HG * GB, 4, SEQ])
        v_sb = ab("v_sb", [P, TILES, D])
        probs = ab("probs", [P, TILES, D])
        pair_t = ab("pair_t", [P, TILES, H, P])
        o_t = ab("o_t", [P, KD, GT])
        x1 = ab("x1", [P, TILES, D])
        y = ab("y", [P, TILES, D])
        kg_sb = ab("kg_sb", [LR, GT])
        gate_z = ab("gate_z", [P, GC * GT])
        silu_g = ab("silu_g", [P, TILES, D])
        q_even = normed[:, 0, :].rearrange("p (c t) -> p c t", c=GC)
        q_odd = normed[:, 1, :].rearrange("p (c t) -> p c t", c=GC)
        grow = o_t[:, 0:2, :].rearrange("p a t -> p (a t)")
        shrink = o_t[:, 2:4, :].rearrange("p a t -> p (a t)")
        temp = q_t[:, :, :].rearrange("p a t -> p (a t)").rearrange("p (a t) -> p a t", a=TILES)
        k_dec = temp[:, 0, :].rearrange("p (c t) -> p c t", c=GC)
        gate_e, gate_sum = silu_g[:, 0, :], silu_g[:, 1, :]
        o_sb = probs
        r2 = rstd[:, :, :].rearrange("p t h -> p (t h)")

        attentions.close()

        GU, DN = 2 * KD * FE, (FE // P) * D
        e_w = [sb(f"e_w{n}", [P, WE_N]) for n in range(2)]
        e_gu_hi = [sb(f"e_gu_hi{n}", [P, GU], f32r) for n in range(2)]
        e_gu_lo = [sb(f"e_gu_lo{n}", [P, GU], f32r) for n in range(2)]
        e_d_hi = [sb(f"e_d_hi{n}", [P, DN], f32r) for n in range(2)]
        e_d_lo = [sb(f"e_d_lo{n}", [P, DN], f32r) for n in range(2)]
        e_x = [sb(f"e_x{n}", [P, HALVES, D]) for n in range(AHEAD)]
        e_xt_hi = [sb(f"e_xt_hi{n}", [P, KD, CAP], f32r) for n in range(2)]
        e_xt_lo = [sb(f"e_xt_lo{n}", [P, KD, CAP], f32r) for n in range(2)]
        e_s = sb("e_s", [P, 2, CAP])
        e_h = sb("e_h", [P, 2, CAP])
        e_h_hi = [sb(f"e_h_hi{n}", [P, 2, CAP], f32r) for n in range(2)]
        e_h_lo = [sb(f"e_h_lo{n}", [P, 2, CAP], f32r) for n in range(2)]
        e_y = [sb(f"e_y{n}", [P, HALVES, D]) for n in range(2)]

        banks = [stack.enter_context(nc.psum_tensor(f"bank{n}", [P, 512], f32)) for n in range(8)]

        consts_in, xw_in, gw_in, small_in = sem("consts_in"), sem("xw_in"), sem("gw_in"), sem("small_in")
        zeroed, tok_ready, table_set, rows_zeroed = sem("zeroed"), sem("tok_ready"), sem("table_set"), sem("rows_zeroed")
        x_loaded, ctx_loaded, ctx_turned = sem("x_loaded"), sem("ctx_loaded"), sem("ctx_turned")
        bank_full = [sem(f"bank_full{n}") for n in range(6)]
        bank_free = [sem(f"bank_free{n}") for n in range(6)]
        n_var_ready, n_rstd_ready = sem("n_var_ready"), sem("n_rstd_ready")
        var_ready, rstd_ready = sem("var_ready"), sem("rstd_ready")
        xn_ready, yn_ready, y1n_ready = sem("xn_ready"), sem("yn_ready"), sem("y1n_ready")
        centered, exped, probs_ready = sem("centered"), sem("exped"), sem("probs_ready")
        folded, y_normed, m_scaled, m_hi_set = sem("folded"), sem("y_normed"), sem("m_scaled"), sem("m_hi_set")
        softplus_done, decay_in, decays = sem("softplus_done"), sem("decay_in"), sem("decays")
        g_tanhed = sem("g_tanhed")
        o_centered, o_squared, o_ready = sem("o_centered"), sem("o_squared"), sem("o_ready")
        w_loaded = [[sem(f"w_loaded{part}{n}") for n in range(SLOTS)] for part in range(2)]
        w_hi_set, w_lo_set = ([sem(f"{n}{part}") for part in range(2)] for n in ("w_hi_set", "w_lo_set"))
        w_free, w_lo_late = sem("w_free"), sem("w_lo_late")
        h_tanhed, h_split, m_split = sem("h_tanhed"), sem("h_split"), sem("m_split")
        mlp_read = sem("mlp_read")
        c_var_ready, c_rstd_ready, z_ready, rows_stored = sem("c_var_ready"), sem("c_rstd_ready"), sem("z_ready"), sem("rows_stored")
        lg_centered, lg_exped, chosen_ready, counted = sem("lg_centered"), sem("lg_exped"), sem("chosen_ready"), sem("counted")
        payload_ready, payload_sent, scattered = sem("payload_ready"), sem("payload_sent"), sem("scattered")
        v_next, v_ab, v_c, a_ab = sem("v_next"), sem("v_ab"), sem("v_c"), sem("a_ab")
        passed = sem("passed")
        table_in = sem("table_in")
        e_gu_in = [sem(f"e_gu_in{n}") for n in range(2)]
        e_d_in = [sem(f"e_d_in{n}") for n in range(2)]
        e_slot_set = sem("e_slot_set")
        e_rows = [sem(f"e_rows{n}") for n in range(AHEAD)]
        e_gu_hi_set, e_gu_lo_set, e_d_hi_set, e_d_lo_set = (sem(n) for n in ("e_gu_hi_set", "e_gu_lo_set", "e_d_hi_set", "e_d_lo_set"))
        e_turned, e_xt_hi_set, e_xt_lo_set = sem("e_turned"), sem("e_xt_hi_set"), sem("e_xt_lo_set")
        e_up, e_silu, e_h_set, e_h_hi_set, e_h_lo_set = (sem(n) for n in ("e_up", "e_silu", "e_h_set", "e_h_hi_set", "e_h_lo_set"))
        e_down, e_y_a, e_y_v, e_added = sem("e_down"), sem("e_y_a"), sem("e_y_v"), sem("e_added")

        def bank(name):
            return banks[place(name)[0]]

        def wait_bank_free(eng, name, g):
            b, n, per = place(name)
            eng.wait_ge(bank_free[b], g * per + n + 1)

        def wait_full(eng, name, g):
            b, n, per = place(name)
            eng.wait_ge(bank_full[b], g * per + n + 1)

        def wait_evacuated(eng, name, g):
            b, n, per = place(name)
            eng.wait_ge(bank_free[b], g * per + n + 2)

        def full(ins, name):
            ins.then_inc(bank_full[place(name)[0]], 1)

        def freed(ins, name):
            ins.then_inc(bank_free[place(name)[0]], 1)

        def chunk(j):
            return j % SLOTS, j // SLOTS, len(range(j % SLOTS, J, SLOTS))

        def wait_split(eng, sems, j, g, part):
            eng.wait_ge(sems[part], g * J + j + 1)

        def wait_low(eng, j, g, part):
            if part == 1 and j >= 2:
                eng.wait_ge(w_lo_late, g * (J - 2) + j - 1)
            elif part == 1:
                eng.wait_ge(w_lo_set[1], g * 2 + j + 1)
            else:
                eng.wait_ge(w_lo_set[0], g * J + j + 1)

        def wait_place_free(eng, j, g):
            eng.wait_ge(w_free, g * J + max(j - 1, 0) + 1)

        def three_passes(eng, out_, w_hi, w_lo, m_hi, m_lo, start, stop):
            eng.matmul(out_, w_hi, m_hi, start=start, stop=False)
            eng.matmul(out_, w_hi, m_lo, start=False, stop=False)
            return eng.matmul(out_, w_lo, m_hi, start=False, stop=stop)

        def apart(eng):
            eng.sem_inc(passed, 1)

        def iterate(eng, step):
            for name in TIMELINE:
                if name[0] == "n":
                    step(name, 0)
            for name in TIMELINE:
                if name[0] != "c":
                    step(name, 1 if name[0] == "n" else 0)
            with eng.Fori(1, GROUPS - 1) as i:
                before, after = eng.snap(i - 1), eng.snap(i + 1)
                for name in TIMELINE:
                    step(name, {"c": before, "n": after}.get(name[0], i))
            for name in TIMELINE:
                if name[0] != "n":
                    step(name, GROUPS - 2 if name[0] == "c" else GROUPS - 1)
            for name in C_ALONE:
                step(name, GROUPS - 1)

        block = stack.enter_context(nc.Block())

        @block.sync
        def _(eng):
            def load_chunk(j, g, part, first=False):
                s = chunk(j)[0]
                if not first:
                    if j >= SLOTS:
                        wait_low(eng, j - SLOTS, g, part)
                    elif part == 0:
                        eng.wait_ge(w_lo_set[0], g * J)
                    else:
                        eng.wait_ge(w_lo_late, g * (J - 2))
                eng.dma_start(cring[:, s, PARTS[part]], cw[j][:, PARTS[part]]).then_inc(w_loaded[part][s], 16)

            def load_group(g):
                eng.dma_start(x_in[:, :, :], x[bass.ds(g * GT, GT)].rearrange("(t p) d -> p t d", p=P))\
                   .then_inc(x_loaded, 16)
                eng.dma_start(ctx_in[:, :, :], ctxt[bass.ds(g, 1)].rearrange("o p s b -> (o p) s b")[:, 0:SEQ, :])\
                   .then_inc(ctx_loaded, 16)

            eng.dma_start(x_in[:, :, :], x[0:GT].rearrange("(t p) d -> p t d", p=P)).then_inc(x_loaded, 16)
            eng.dma_start(const[:, :], consts).then_inc(consts_in, 16)
            eng.dma_start(ctx_in[:, :, :], ctxt[0][:, 0:SEQ, :]).then_inc(ctx_loaded, 16)
            eng.dma_start(vec[:, :], vecs).then_inc(small_in, 16)
            eng.dma_start(bg_b[:, :], bg_row.to_broadcast([P, D])).then_inc(small_in, 16)
            eng.dma_start(wkg2[:, :], kg2).then_inc(small_in, 16)
            eng.dma_start(w_gate[:, :, :], gate_w).then_inc(small_in, 16)
            eng.dma_start(weights[:, 0:XW_N], xw).then_inc(xw_in, 16)
            eng.dma_start(weights[:, XW_N:], gw).then_inc(gw_in, 16)
            for j in range(SLOTS):
                for part in range(2):
                    load_chunk(j, 0, part, first=True)
            eng.wait_ge(zeroed, 6)
            eng.dma_start(z_rows[T:ROWS].rearrange("(t p) d -> p t d", p=P), x2[:, :, :]).then_inc(rows_zeroed, 16)
            eng.dma_start(out[T:ROWS].rearrange("(t p) d -> p t d", p=P), x2[:, :, :]).then_inc(rows_zeroed, 16)
            eng.dma_start(slots_d.rearrange("(p n) v -> p n v", p=P), table[:, :, :]).then_inc(table_set, 16)

            def step(name, g):
                if name == "next_load" and not first(g):
                    eng.wait_ge(yn_ready, g * TILES)
                    load_group(g)
                elif name == "c_norm":
                    if not (isinstance(g, int) and g == GROUPS - 1):
                        for j in range(SLOTS):
                            load_chunk(j, g + 1, 0)
                        for j in range(SLOTS):
                            load_chunk(j, g + 1, 1)
                    eng.wait_ge(z_ready, (g + 1) * TILES)
                    rows = bass.ds(g * GT, GT)
                    eng.dma_start(out[rows].rearrange("(t p) d -> p t d", p=P), x2[:, :, :]).then_inc(rows_stored, 16)
                    eng.dma_start(z_rows[rows].rearrange("(t p) d -> p t d", p=P), z[:, :, :]).then_inc(rows_stored, 16)
                elif name[0] == "c" and name[1:].isdigit() and int(name[1:]) + SLOTS < J:
                    load_chunk(int(name[1:]) + SLOTS, g, 0)
                elif name[:2] == "cy" and int(name[2:]) + SLOTS < J:
                    load_chunk(int(name[2:]) + SLOTS, g, 1)

            iterate(eng, step)
            if phases < 2:
                eng.wait_ge(rows_stored, 32 * GROUPS)
                eng.wait_ge(rows_zeroed, 32)
                return

            def load_expert(e, par):
                w = ew[e] if isinstance(e, int) else ew[bass.ds(e, 1)].rearrange("o p n -> (o p) n")
                eng.dma_start(e_w[par][:, 0:GU], w[:, 0:GU]).then_inc(e_gu_in[par], 16)
                eng.dma_start(e_w[par][:, GU:WE_N], w[:, GU:WE_N]).then_inc(e_d_in[par], 16)

            wait_full(eng, "wo1", GROUPS - 1)
            eng.wait_ge(y1n_ready, TILES * GROUPS)
            load_expert(0, 0)
            load_expert(1, 1)
            eng.wait_ge(scattered, 16 * TILES * TOP * GROUPS)
            eng.dma_start(table[:, :, :], slots_d.rearrange("(p n) v -> p n v", p=P)).then_inc(table_in, 16)
            with eng.Fori(0, (E - 2) // 2) as m:
                for par in range(2):
                    eng.wait_ge(e_d_lo_set, m * 2 + par + 1)
                    load_expert(eng.snap(m * 2 + 2 + par), par)
            eng.wait_ge(rows_stored, 32 * GROUPS)
            eng.wait_ge(rows_zeroed, 32)

        @block.gpsimd
        def _(eng):
            eng.memset(k_diag[:, :, :, :], 0.0).then_inc(zeroed, 1)
            eng.memset(pair_t[:, :, :, :], 0.0).then_inc(zeroed, 1)
            eng.memset(resid[:, :, :], 0.0).then_inc(zeroed, 1)
            eng.memset(chosen_sum[:, :], 0.0).then_inc(zeroed, 1)
            eng.iota(table[:, :, 0].rearrange("p (e h) -> p e h", h=HALVES), [[0, E], [P, HALVES]],
                     base=T, channel_multiplier=1).then_inc(zeroed, 1)
            eng.memset(table[:, :, 1], 0).then_inc(zeroed, 1)
            eng.wait_ge(consts_in, 16)

            def power(ready, done, count, src, dst, n):
                eng.wait_ge(ready, count)
                eng.tensor_tensor(dst, src, c["neg_half"][:, 0:n], ALU.pow).then_inc(done, 1)

            def ab_power(g, k, at, n):
                flat = var_e[:, :, :].rearrange("p t h -> p (t h)")[:, at:at + n]
                flat_r = rstd[:, :, :].rearrange("p t h -> p (t h)")[:, at:at + n]
                power(var_ready, rstd_ready, g * 5 + k + 1, flat, flat_r, n)

            def step(name, g):
                if name == "next_norm":
                    eng.wait_ge(ctx_loaded, (g + 1) * 16)
                    apart(eng)
                    eng.tensor_copy(ctx_t[:, :, :], ctx_in[:, :, :].rearrange("p s b -> p b s")).then_inc(ctx_turned, 1)
                    power(n_var_ready, n_rstd_ready, g + 1, n_var[:, :], n_rstd[:, :], TILES)
                elif name == "a_out":
                    ab_power(g, 0, 0, TILES)
                    ab_power(g, 1, 0, TILES)
                elif name in SPLITS and SPLITS[name][1] == 1 and SPLITS[name][0] >= 2:
                    j = SPLITS[name][0]
                    s = chunk(j)[0]
                    wait_split(eng, w_hi_set, j, g, 1)
                    apart(eng)
                    eng.tensor_tensor(cring_lo[:, s, PARTS[1]], cring[:, s, PARTS[1]], cring_hi[:, s, PARTS[1]].bitcast(f32),
                                      ALU.subtract).then_inc(w_lo_late, 1)
                elif name[:-1] == "b_variance":
                    t = int(name[-1])
                    ab_power(g, 2 + t, t * H, H)
                elif name == "b_out":
                    ab_power(g, 4, 0, TILES)
                elif name == "c_norm":
                    power(c_var_ready, c_rstd_ready, g + 1, c_var[:, :], c_rstd[:, :], TILES)
                elif name == "c_scatter":
                    eng.wait_ge(table_set, 16)
                    for t in range(TILES):
                        eng.wait_ge(payload_ready, g * TILES + t + 1)
                        apart(eng)
                        for k in range(TOP):
                            eng.indirect_dma_start(
                                slots_d, bass.IndirectOffsetOnAxis(ap=slot_i[:, t, k:k + 1].bitcast(u32), axis=0),
                                payload[:, t, k, :], None, bounds_check=E * CAP - 1, oob_is_err=False)\
                               .then_inc(scattered, 16)
                    eng.wait_ge(scattered, (g + 1) * (16 * TILES * TOP))
                    eng.sem_inc(payload_sent, 1)

            iterate(eng, step)
            if phases < 2:
                return

            def slots(e):
                return table[:, e * HALVES:(e + 1) * HALVES, :] if isinstance(e, int) else table[:, bass.ds(e * HALVES, HALVES), :]

            def gather(e, n):
                if not (isinstance(e, int) and e < AHEAD):
                    eng.wait_ge(e_turned, (e - AHEAD + 1) * HALVES)
                    eng.wait_ge(e_added, (e - AHEAD + 1) * (HALVES * 16))
                    apart(eng)
                eng.tensor_copy(e_slot[n][:, :, :], slots(e)).then_inc(e_slot_set, 1)
                eng.wait_ge(e_slot_set, e + 1)
                apart(eng)
                for h in range(HALVES):
                    eng.indirect_dma_start(
                        e_x[n][:, h, :], None, z_rows,
                        bass.IndirectOffsetOnAxis(ap=e_slot[n][:, h, 0:1].bitcast(u32), axis=0),
                        bounds_check=ROWS - 1, oob_is_err=False).then_inc(e_rows[n], 16)

            def scatter_add(e, n):
                for h in range(HALVES):
                    eng.wait_ge((e_y_a, e_y_v)[h], e + 1)
                    if h == 0 and not first(e):
                        eng.wait_ge(e_added, e * (HALVES * 16))
                    apart(eng)
                    eng.indirect_dma_start(
                        out, bass.IndirectOffsetOnAxis(ap=e_slot[n][:, h, 0:1].bitcast(u32), axis=0),
                        e_y[n % 2][:, h, :], None, bounds_check=ROWS - 1, oob_is_err=True,
                        compute_op=ALU.add).then_inc(e_added, 16)

            eng.wait_ge(rows_stored, 32 * GROUPS)
            eng.wait_ge(rows_zeroed, 32)
            eng.wait_ge(table_in, 16)
            wait_full(eng, "wo1", GROUPS - 1)
            for e in range(AHEAD - 1):
                gather(e, e)
            gather(AHEAD - 1, AHEAD - 1)
            scatter_add(0, 0)
            with eng.Fori(0, (E - AHEAD) // AHEAD) as m:
                for n in range(1, AHEAD + 1):
                    e = eng.snap(m * AHEAD + n)
                    gather(eng.snap(e + AHEAD - 1), n - 1)
                    scatter_add(e, n % AHEAD)
            for e in range(E - AHEAD + 1, E):
                scatter_add(e, e % AHEAD)
            eng.wait_ge(e_added, 16 * HALVES * E)

        @block.scalar
        def _(eng):
            for s in bank_free:
                eng.sem_inc(s, 1)
            eng.sem_inc(mlp_read, 1)
            eng.sem_inc(w_free, 1)
            eng.sem_inc(payload_sent, 1)
            eng.wait_ge(consts_in, 16)

            def turn_back(name, dst, t, g):
                wait_full(eng, name, g)
                freed(eng.activation(dst[:, :, t * P:(t + 1) * P], bank(name)[:, :].rearrange("p (k t) -> p k t", k=KD),
                                     ACT.Copy), name)

            def split(j, g, part):
                s, n, per = chunk(j)
                eng.wait_ge(w_loaded[part][s], (g * per + n + 1) * 16)
                if part == 1:
                    wait_place_free(eng, j, g)
                cols = PARTS[part]
                eng.activation(cring_hi[:, s, cols], cring[:, s, cols], ACT.Copy).then_inc(w_hi_set[part], 1)

            def step(name, g):
                if name == "next_turn":
                    for t in range(TILES):
                        turn_back(f"xT{t}", normed_t, t, g)
                elif name == "b_begin":
                    for t in range(TILES):
                        wait_full(eng, f"mT{t}", g)
                        for k in range(KD):
                            last = eng.activation(normed2[:, t, k, :], bank(f"mT{t}")[:, k * P:(k + 1) * P], ACT.Copy,
                                                  scale=ln2[:, k:k + 1])
                            if k == 0:
                                last.then_inc(m_scaled, 1)
                        freed(last, f"mT{t}")
                        wait_evacuated(eng, f"mT{t}", g)
                        eng.wait_ge(m_scaled, g * TILES + t + 1)
                        eng.activation(normed2_hi[:, :, t * P:(t + 1) * P], normed2[:, t, :, :], ACT.Copy).then_inc(m_hi_set, 1)
                elif name in SPLITS:
                    split(SPLITS[name][0], g, SPLITS[name][1])
                elif name == "a_out":
                    for t in range(TILES):
                        eng.wait_ge(y_normed, g * TILES + t + 1)
                        eng.wait_ge(rstd_ready, g * 5 + 2)
                        eng.activation(normed[:, t, :], y[:, t, :], ACT.Copy, scale=r2[:, t:t + 1]).then_inc(yn_ready, 1)
                elif name == "b_turn":
                    for t in range(TILES):
                        turn_back(f"yT{t}", normed_t, t, g)
                elif name == "next_keys":
                    eng.wait_ge(zeroed, 6)
                    for n in range(2):
                        wait_full(eng, f"k{n}", g)
                        for a in range(4):
                            rows = slice(32 * a, 32 * a + 32)
                            last = eng.activation(k_diag[rows, 2 * n * GB:2 * (n + 1) * GB, a, :],
                                                  bank(f"k{n}")[rows, :].rearrange("p (n s) -> p n s", s=SEQ), ACT.Copy)
                        freed(last, f"k{n}")
                elif name[:-1] == "next_queries":
                    n = int(name[-1])
                    wait_full(eng, f"q{n}", g)
                    freed(eng.activation(q_t[:, 2 * n:2 * n + 2, :], bank(f"q{n}")[:, :].rearrange("p (a t) -> p a t", a=2),
                                         ACT.Copy, scale=HD ** -0.5), f"q{n}")
                elif name in ("next_values", "b_values"):
                    for t in range(TILES):
                        use = ("v" if name[0] == "n" else "gv") + str(t)
                        wait_full(eng, use, g)
                        freed(eng.activation(v_sb[:, t, :], bank(use)[:, :], ACT.Copy), use)
                elif name[:-1] == "a_scores":
                    t = int(name[-1])
                    eng.wait_ge(centered, g * TILES + t + 1)
                    eng.activation(probs[:, t, :], probs[:, t, :], ACT.Exp).then_inc(exped, 1)
                elif name[:-1] == "a_values":
                    t = int(name[-1])
                    turn_back(f"oT{t}", o_t, t, g)
                elif name == "b_gate":
                    wait_full(eng, "kg", g)
                    freed(eng.activation(kg_sb[:, :], bank("kg")[0:LR, 0:GT], ACT.Copy), "kg")
                elif name == "b_decay":
                    chain = Chain(eng, a_ab, g * A_AB)
                    wait_full(eng, "kz", g)
                    for n in range(GC):
                        cols = slice(n * GT, (n + 1) * GT)
                        ins = eng.activation(gate_z[:, cols], bank("kz")[:, cols], ACT.Identity, bias=bkg[:, n:n + 1])
                        if n == 0:
                            chain.add(ins)
                    freed(ins, "kz")
                    wait_evacuated(eng, "kz", g)
                    chain.settle()
                    chain.link(eng.activation(gate_e[:, :], gate_z[:, :], ACT.Abs))
                    chain.link(eng.activation(gate_e[:, :], gate_e[:, :], ACT.Exp, scale=-1.0))
                    assert chain.n == A_AB
                    eng.activation(gate_e[:, :], gate_e[:, :], ACT.Ln, bias=1.0).then_inc(softplus_done, 1)
                elif name == "b_silu":
                    eng.wait_ge(decay_in, g + 1)
                    eng.activation(grow, gate_z[:, :], ACT.Exp, scale=1.0 / NORMALIZER)
                    eng.activation(shrink, gate_z[:, :], ACT.Exp, scale=-1.0 / NORMALIZER).then_inc(decays, 1)
                    for t in range(TILES):
                        wait_evacuated(eng, f"gg{t}", g)
                        eng.activation(temp[:, t, :], silu_g[:, t, :], ACT.Tanh, scale=0.5).then_inc(g_tanhed, 1)
                elif name[:-1] == "b_read":
                    t = int(name[-1])
                    eng.wait_ge(o_centered, g * TILES + t + 1)
                    eng.activation(temp[:, t, :], o_sb[:, t, :], ACT.Square).then_inc(o_squared, 1)
                elif name[:-1] == "b_turn_out":
                    t = int(name[-1])
                    turn_back(f"nT{t}", o_t, t, g)
                elif name == "b_again":
                    if not first(g):
                        eng.wait_ge(rows_stored, g * 32)
                        wait_full(eng, "zT1", g - 1)
                    eng.wait_ge(rstd_ready, g * 5 + 5)
                    for t in range(TILES):
                        eng.activation(normed[:, t, :], y[:, t, :], ACT.Copy, scale=r2[:, t:t + 1]).then_inc(y1n_ready, 1)
                elif name == "c_turn":
                    for t in range(TILES):
                        turn_back(f"zT{t}", z_t, t, g)
                elif name == "c_route":
                    for t in range(TILES):
                        eng.wait_ge(lg_centered, g * TILES + t + 1)
                        eng.activation(logits[:, t, :], logits[:, t, :], ACT.Exp, bias=neg_max[:, t:t + 1],
                                       accum_out=esum[:, t:t + 1]).then_inc(lg_exped, 1)
                elif name[0] == "c" and name[1:].isdigit():
                    j = int(name[1:])
                    wait_full(eng, f"h{j}", g)
                    if j:
                        wait_evacuated(eng, f"h{j - 1}", g)
                    eng.activation(h_e, bank(f"h{j}")[:, 0:GT], ACT.Tanh, scale=0.5).then_inc(h_tanhed, 1)

            iterate(eng, step)
            if phases < 2:
                return

            def split_up(e, par):
                if not (isinstance(e, int) and e < 2):
                    eng.wait_ge(e_up, (e - 1) * 2)
                eng.wait_ge(e_gu_in[par], loads(e, par, 2))
                eng.activation(e_gu_hi[par][:, :], e_w[par][:, 0:GU], ACT.Copy).then_inc(e_gu_hi_set, 1)

            def split_down(e, par):
                if not (isinstance(e, int) and e < 2):
                    eng.wait_ge(e_down, (e - 1) * HALVES)
                eng.wait_ge(e_d_in[par], loads(e, par, 2))
                eng.activation(e_d_hi[par][:, :], e_w[par][:, GU:WE_N], ACT.Copy).then_inc(e_d_hi_set, 1)

            def turn_e(e, par):
                for h in range(HALVES):
                    eng.wait_ge(e_turned, e * HALVES + h + 1)
                    eng.activation(e_xt_hi[par][:, :, h * P:(h + 1) * P], banks[h][:, :].rearrange("p (k t) -> p k t", k=KD),
                                   ACT.Copy).then_inc(e_xt_hi_set, 1)

            def silu(e, f):
                eng.wait_ge(e_up, e * 2 + f + 1)
                eng.activation(e_s[:, f, :], banks[2 + f][:, 0:CAP], ACT.Silu).then_inc(e_silu, 1)

            def scale_y(e, n, first=False):
                eng.wait_ge(e_down, e * HALVES + 1)
                if not first:
                    eng.wait_ge(e_added, (e - 1) * (16 * HALVES))
                eng.wait_ge(e_slot_set, e + 1)
                eng.activation(e_y[n % 2][:, 0, :], banks[4][:, :], ACT.Copy,
                               scale=e_slot[n][:, 0, 1:2].bitcast(f32)).then_inc(e_y_a, 1)

            def expert(e, n, first, last):
                par = n % 2
                if not last:
                    split_up(e + 1, 1 - par)
                silu(e, 0)
                if not first:
                    scale_y(e - 1, (n - 1) % AHEAD, first=isinstance(e, int) and e <= 2)
                if not last:
                    turn_e(e + 1, 1 - par)
                    split_down(e + 1, 1 - par)
                silu(e, 1)

            split_up(0, 0)
            split_down(0, 0)
            turn_e(0, 0)
            expert_loop(eng, expert)
            scale_y(E - 1, AHEAD - 1)

        @block.tensor
        def _(eng):
            eng.wait_ge(consts_in, 16)

            def turn(name, src, t, g):
                wait_bank_free(eng, name, g)
                for k in range(KD):
                    last = eng.transpose(bank(name)[:, k * P:(k + 1) * P], src[:, t, k * P:(k + 1) * P], c["ident"])
                full(last, name)

            def rows(name, src_t, t, w, g):
                wait_bank_free(eng, name, g)
                for k in range(KD):
                    last = eng.matmul(bank(name)[:, :], src_t[:, k, t * P:(t + 1) * P], w[:, k, :],
                                      start=(k == 0), stop=(k == KD - 1))
                full(last, name)

            def columns(name, w, src_t, first, g):
                wait_bank_free(eng, name, g)
                for n in range(2):
                    for k in range(KD):
                        last = eng.matmul(bank(name)[:, n * GT:(n + 1) * GT], w[:, k, (first + n) * P:(first + n + 1) * P],
                                          src_t[:, k, :], start=(k == 0), stop=(k == KD - 1))
                full(last, name)

            def down(j, g):
                eng.wait_ge(h_split, g * J + j + 1)
                wait_low(eng, j, g, 1)
                if j == 0:
                    eng.wait_ge(mlp_read, g * TILES + 1)
                s = chunk(j)[0]
                for t in range(TILES):
                    cols = slice(t * P, (t + 1) * P)
                    last = three_passes(eng, banks[6 + t][:, :], h_hi[:, j % 2, cols], h_lo[:, j % 2, cols],
                                        cring_hi[:, s, 2 * D:WJ], cring_lo[:, s, 2 * D:WJ], j == 0, j == J - 1)
                last.then_inc(w_free, 1)

            def step(name, g):
                if name == "next_turn":
                    for t in range(TILES):
                        eng.wait_ge(xn_ready, g * TILES + t + 1)
                        turn(f"xT{t}", temp, t, g)
                elif name == "next_keys":
                    if first(g):
                        eng.wait_ge(xw_in, 16)
                    eng.wait_ge(ctx_turned, g + 1)
                    ctx_cols = ctx_t[:, :, :].rearrange("p b s -> p (b s)")
                    for n in range(2):
                        wait_bank_free(eng, f"k{n}", g)
                        for m in range(2):
                            hg = 2 * n + m
                            last = eng.matmul(bank(f"k{n}")[:, m * GT:(m + 1) * GT], wk_x[:, hg * P:(hg + 1) * P],
                                              ctx_cols, start=True, stop=True)
                        full(last, f"k{n}")
                elif name[:-1] == "next_queries":
                    n = int(name[-1])
                    if n == 0:
                        for t in range(TILES):
                            wait_evacuated(eng, f"xT{t}", g)
                    columns(f"q{n}", wq_x, normed_t, 2 * n, g)
                elif name == "next_values":
                    ctx_cols = ctx_t[:, :, :].rearrange("p b s -> p (b s)")
                    for t in range(TILES):
                        wait_bank_free(eng, f"v{t}", g)
                        full(eng.matmul(bank(f"v{t}")[:, :], ctx_cols[:, t * P:(t + 1) * P], wv_x,
                                        start=True, stop=True), f"v{t}")
                elif name[:-1] == "a_scores":
                    t = int(name[-1])
                    if t == 0:
                        for n in range(2):
                            wait_evacuated(eng, f"k{n}", g)
                            wait_evacuated(eng, f"q{n}", g)
                    wait_bank_free(eng, f"s{t}", g)
                    for hg in range(HG):
                        for b in range(TB):
                            last = eng.matmul(
                                bank(f"s{t}")[32 * b:32 * b + 32, hg * P:(hg + 1) * P],
                                q_t[:, hg, t * P + 32 * b:t * P + 32 * b + 32],
                                k_diag[:, hg * GB + t * TB + b, :, :].rearrange("p a s -> p (a s)"),
                                start=True, stop=True)
                    full(last, f"s{t}")
                elif name[:-1] == "a_values":
                    t = int(name[-1])
                    wait_evacuated(eng, f"v{t}", g)
                    eng.wait_ge(probs_ready, g * TILES + t + 1)
                    wait_bank_free(eng, f"oT{t}", g)
                    for h in range(H):
                        a, hg = h % 4, h // 4
                        last = eng.matmul(bank(f"oT{t}")[32 * a:32 * a + 32, hg * P:(hg + 1) * P],
                                          v_sb[:, t, h * HD:(h + 1) * HD], pair_t[:, t, h, :],
                                          start=True, stop=True)
                    full(last, f"oT{t}")
                elif name == "a_out":
                    for t in range(TILES):
                        wait_evacuated(eng, f"oT{t}", g)
                        rows(f"w{t}", o_t, t, wo_x, g)
                elif name == "b_turn":
                    for t in range(TILES):
                        eng.wait_ge(yn_ready, g * TILES + t + 1)
                        turn(f"yT{t}", normed, t, g)
                elif name == "b_gate":
                    if first(g):
                        eng.wait_ge(folded, 5 * KD)
                        eng.wait_ge(small_in, 64)
                    for t in range(TILES):
                        wait_evacuated(eng, f"yT{t}", g)
                    wait_bank_free(eng, "kg", g)
                    for k in range(KD):
                        last = eng.matmul(bank("kg")[0:LR, 0:GT], wkg1[:, k, :], normed_t[:, k, :],
                                          start=(k == 0), stop=(k == KD - 1))
                    full(last, "kg")
                elif name == "b_values":
                    for t in range(TILES):
                        rows(f"gv{t}", normed_t, t, wv_g, g)
                elif name == "b_decay":
                    wait_evacuated(eng, "kg", g)
                    wait_bank_free(eng, "kz", g)
                    for n in range(GC):
                        last = eng.matmul(bank("kz")[:, n * GT:(n + 1) * GT], wkg2[:, n * P:(n + 1) * P], kg_sb[:, :],
                                          start=True, stop=True)
                    full(last, "kz")
                elif name == "b_silu":
                    for t in range(TILES):
                        rows(f"gg{t}", normed_t, t, wg_g, g)
                elif name == "b_keys":
                    columns("gq", wq_g, normed_t, 0, g)
                    columns("gk", wk_g, normed_t, 0, g)
                elif name[:-1] == "b_scores":
                    t = int(name[-1])
                    wait_evacuated(eng, "gq", g)
                    wait_evacuated(eng, "gk", g)
                    for r in range(4):
                        wait_bank_free(eng, f"A{t}{r}", g)
                    for n in range(GC):
                        for par, q in ((0, q_even), (1, q_odd)):
                            for r in range(4):
                                feats = slice(32 * r, 32 * r + 32)
                                last = eng.matmul(bank(f"A{t}{r}")[:, (2 * n + par) * P:(2 * n + par + 1) * P],
                                                  k_dec[feats, n, t * P:(t + 1) * P], q[feats, n, t * P:(t + 1) * P],
                                                  start=True, stop=True)
                                if n == GC - 1 and par == 1:
                                    full(last, f"A{t}{r}")
                elif name[:-1] == "b_read":
                    t = int(name[-1])
                    wait_evacuated(eng, f"gv{t}", g)
                    for r in range(4):
                        wait_evacuated(eng, f"A{t}{r}", g)
                    wait_bank_free(eng, f"o{t}", g)
                    for h in range(H):
                        n, r, par = h // 8, h % 8 // 2, h % 2
                        last = eng.matmul(bank(f"o{t}")[:, h * HD:(h + 1) * HD], pair_t[:, t, 4 * r + 2 * n + par, :],
                                          v_sb[:, t, h * HD:(h + 1) * HD], start=True, stop=True)
                    full(last, f"o{t}")
                elif name[:-1] == "b_turn_out":
                    t = int(name[-1])
                    eng.wait_ge(o_ready, g * TILES + t + 1)
                    turn(f"nT{t}", o_sb, t, g)
                elif name == "b_out":
                    for t in range(TILES):
                        wait_evacuated(eng, f"nT{t}", g)
                        rows(f"wo{t}", o_t, t, wo_g, g)
                elif name == "b_begin":
                    for t in range(TILES):
                        eng.wait_ge(y1n_ready, g * TILES + t + 1)
                        turn(f"mT{t}", normed, t, g)
                elif name[:2] == "cy":
                    down(int(name[2:]), g)
                elif name == "c_turn":
                    for t in range(TILES):
                        eng.wait_ge(z_ready, g * TILES + t + 1)
                        turn(f"zT{t}", z, t, g)
                elif name == "c_route":
                    for t in range(TILES):
                        wait_evacuated(eng, f"zT{t}", g)
                    wait_bank_free(eng, "lg", g)
                    for t in range(TILES):
                        for k in range(KD):
                            last = eng.matmul(bank("lg")[:, t * E:(t + 1) * E], z_t[:, k, t * P:(t + 1) * P],
                                              w_gate[:, k, :], start=(k == 0), stop=(k == KD - 1))
                    full(last, "lg")
                elif name == "c_slots":
                    eng.wait_ge(chosen_ready, g * TILES + TILES)
                    eng.wait_ge(counted, g + 1)
                    wait_bank_free(eng, "ps", g)
                    eng.matmul(bank("ps")[:, 0:E], c["ones"], chosen_sum[:, :], start=True, stop=False)
                    eng.matmul(bank("ps")[:, 0:E], c["before"], chosen[:, 0, :], start=False, stop=True)
                    eng.matmul(bank("ps")[:, E:2 * E], c["ones"], chosen_sum[:, :], start=True, stop=False)
                    eng.matmul(bank("ps")[:, E:2 * E], c["ones"], chosen[:, 0, :], start=False, stop=False)
                    full(eng.matmul(bank("ps")[:, E:2 * E], c["before"], chosen[:, 1, :], start=False, stop=True), "ps")
                elif name[0] == "c" and name[1:].isdigit():
                    j = int(name[1:])
                    s = chunk(j)[0]
                    if j == 0:
                        eng.wait_ge(m_split, (g + 1) * TILES)
                    wait_low(eng, j, g, 0)
                    wait_bank_free(eng, f"h{j}", g)
                    hi, lo = (w[:, s, 0:2 * D].rearrange("p (m k f) -> p m k f", m=2, k=KD) for w in (cring_hi, cring_lo))
                    for m in range(2):
                        for k in range(KD):
                            last = three_passes(eng, bank(f"h{j}")[:, m * GT:(m + 1) * GT], hi[:, m, k, :], lo[:, m, k, :],
                                                normed2_hi[:, k, :], normed2_lo[:, k, :], k == 0, k == KD - 1)
                    full(last, f"h{j}")

            iterate(eng, step)
            if phases < 2:
                return

            def turn_e(e, n):
                eng.wait_ge(e_rows[n], loads(e, n, AHEAD, HALVES))
                for h in range(HALVES):
                    if not (isinstance(e, int) and e == 0):
                        eng.wait_ge(e_xt_lo_set, (e - 1) * HALVES + h + 1)
                    for k in range(KD):
                        last = eng.transpose(banks[h][:, k * P:(k + 1) * P], e_x[n][:, h, k * P:(k + 1) * P], c["ident"])
                    last.then_inc(e_turned, 1)

            def up(e, par, f, first):
                if f == 0:
                    eng.wait_ge(e_gu_lo_set, e + 1)
                    eng.wait_ge(e_xt_lo_set, (e + 1) * HALVES)
                if not first:
                    eng.wait_ge(e_h_set, e * 2 - 1 + f)
                hi, lo = (w[par][:, :].rearrange("p (m k f) -> p m k f", m=2, k=KD) for w in (e_gu_hi, e_gu_lo))
                cols = slice(f * P, (f + 1) * P)
                for m in range(2):
                    for k in range(KD):
                        last = three_passes(eng, banks[2 + f][:, m * CAP:(m + 1) * CAP], hi[:, m, k, cols], lo[:, m, k, cols],
                                            e_xt_hi[par][:, k, :], e_xt_lo[par][:, k, :], k == 0, k == KD - 1)
                last.then_inc(e_up, 1)

            def down_e(e, par, first):
                eng.wait_ge(e_d_lo_set, e + 1)
                hi, lo = (w[par][:, :].rearrange("p (f d) -> p f d", d=D) for w in (e_d_hi, e_d_lo))
                eng.wait_ge(e_h_lo_set, e * 2 + 2)
                for h in range(HALVES):
                    if not first:
                        eng.wait_ge((e_y_a, e_y_v)[h], e)
                    cols = slice(h * P, (h + 1) * P)
                    for f in range(2):
                        last = three_passes(eng, banks[4 + h][:, :], e_h_hi[par][:, f, cols], e_h_lo[par][:, f, cols],
                                            hi[:, f, :], lo[:, f, :], f == 0, f == 1)
                    last.then_inc(e_down, 1)

            def expert(e, n, first, last):
                par = n % 2
                up(e, par, 0, first)
                if not first:
                    down_e(e - 1, 1 - par, first=isinstance(e, int) and e == 1)
                if not last:
                    turn_e(e + 1, (n + 1) % AHEAD)
                up(e, par, 1, first)

            turn_e(0, 0)
            expert_loop(eng, expert)
            down_e(E - 1, 1, False)

        @block.vector
        def _(eng):
            eng.wait_ge(consts_in, 16)
            eng.wait_ge(small_in, 64)
            eng.wait_ge(zeroed, 6)
            tok_set = Chain(eng, tok_ready, 0)
            for t in range(TILES):
                tok_set.add(eng.tensor_scalar(tok[:, t:t + 1], c["token"], float(t * P), None, ALU.add))
            tok_set.settle()
            chains = {}

            def chain(which, g):
                if which not in chains:
                    sem_, per = {"next": (v_next, V_N), "ab": (v_ab, V_AB), "c": (v_c, V_C)}[which]
                    chains[which] = Chain(eng, sem_, g * per)
                return chains[which]

            def end(which):
                n = chains.pop(which).n
                assert n == {"next": V_N, "ab": V_AB, "c": V_C}[which], (which, n)

            def heads(ap):
                return ap.rearrange("p (h d) -> p h d", d=HD)

            def per_head(ap):
                return ap.unsqueeze(2).to_broadcast([P, H, HD])

            def moments(ch, src, st, m):
                for t in range(TILES):
                    ch.add(eng.bn_stats(st[:, t, :], src[:, t, :]))
                ch.settle()
                apart(eng)
                for t in range(TILES):
                    ch.add(eng.bn_aggr(m[:, t, :], st[:, t, :]))
                ch.settle()

            v2 = var_e[:, :, :].rearrange("p t h -> p (t h)")
            spare = row_max[:, :, :].rearrange("p t h -> p (t h)")

            def split(j, g, part):
                s, cols = chunk(j)[0], PARTS[part]
                wait_split(eng, w_hi_set, j, g, part)
                eng.tensor_tensor(cring_lo[:, s, cols], cring[:, s, cols], cring_hi[:, s, cols].bitcast(f32),
                                  ALU.subtract).then_inc(w_lo_set[part], 1)

            def step(name, g):
                if name == "next_norm":
                    eng.wait_ge(x_loaded, (g + 1) * 16)
                    moments(chain("next", g), x_in, n_stats, n_mv)
                    end("next")
                    eng.tensor_scalar(n_var[:, :], n_mv[:, :, 1], EPS, None, ALU.add).then_inc(n_var_ready, 1)
                    eng.wait_ge(n_rstd_ready, g + 1)
                    for t in range(TILES):
                        eng.tensor_scalar(temp[:, t, :], x_in[:, t, :], n_mv[:, t, 0:1], n_rstd[:, t:t + 1],
                                          ALU.subtract, ALU.mult).then_inc(xn_ready, 1)
                elif name[:-1] == "a_scores":
                    t = int(name[-1])
                    ch = chain("ab", g)
                    wait_full(eng, f"s{t}", g)
                    freed(eng.tensor_tensor(heads(probs[:, t, :]), heads(bank(f"s{t}")[:, :]),
                                            c["causal_add"].unsqueeze(1).to_broadcast([P, H, SEQ]), ALU.add), f"s{t}")
                    wait_evacuated(eng, f"s{t}", g)
                    ch.link(eng.tensor_reduce(row_max[:, t, :], heads(probs[:, t, :]), AX.X, ALU.max))
                    eng.tensor_tensor(heads(probs[:, t, :]), heads(probs[:, t, :]), per_head(row_max[:, t, :]),
                                      ALU.subtract).then_inc(centered, 1)
                elif name[:-1] == "a_probs":
                    t = int(name[-1])
                    ch = chain("ab", g)
                    eng.wait_ge(exped, g * TILES + t + 1)
                    ch.link(eng.tensor_reduce(row_sum[:, t, :], heads(probs[:, t, :]), AX.X, ALU.add))
                    ch.link(eng.reciprocal(row_sum[:, t, :], row_sum[:, t, :]))
                    ch.link(eng.tensor_tensor(heads(probs[:, t, :]), heads(probs[:, t, :]),
                                              per_head(row_sum[:, t, :]), ALU.mult))
                    for b in range(TB):
                        rows = slice(32 * b, 32 * b + 32)
                        last = eng.transpose(pair_t[rows, t, :, 32 * b:32 * b + 32], heads(probs[rows, t, :]))
                    last.then_inc(probs_ready, 1)
                elif name == "a_out":
                    ch = chain("ab", g)
                    for t in range(TILES):
                        wait_full(eng, f"w{t}", g)
                        freed(eng.tensor_tensor(x1[:, t, :], x_in[:, t, :], bank(f"w{t}")[:, :], ALU.add), f"w{t}")
                    wait_evacuated(eng, "w0", g)
                    wait_evacuated(eng, "w1", g)
                    moments(ch, x1, stats, mv)
                    eng.tensor_scalar(v2[:, 0:TILES], mv[:, :, 1], EPS, None, ALU.add).then_inc(var_ready, 1)
                    eng.wait_ge(rstd_ready, g * 5 + 1)
                    for t in range(TILES):
                        eng.tensor_scalar(y[:, t, :], x1[:, t, :], mv[:, t, 0:1], r2[:, t:t + 1],
                                          ALU.subtract, ALU.mult).then_inc(y_normed, 1)
                    ch.link(eng.tensor_tensor(spare[:, 0:TILES], mv[:, :, 1], r2[:, 0:TILES], ALU.mult))
                    ch.link(eng.tensor_tensor(spare[:, 0:TILES], spare[:, 0:TILES], r2[:, 0:TILES], ALU.mult))
                    eng.tensor_scalar(v2[:, 0:TILES], spare[:, 0:TILES], EPS, None, ALU.add).then_inc(var_ready, 1)
                elif name == "a_values0" and first(g):
                    eng.wait_ge(gw_in, 16)
                    for w in (wq_g, wk_g, wv_g, wg_g, wkg1):
                        for k in range(KD):
                            eng.tensor_scalar(w[:, k, :], w[:, k, :], ln1[:, k:k + 1], None, ALU.mult).then_inc(folded, 1)
                elif name == "b_decay":
                    ch = chain("ab", g)
                    eng.wait_ge(softplus_done, g + 1)
                    ch.link(eng.scalar_tensor_tensor(gate_z[:, :], gate_z[:, :], 0.0, gate_e[:, :], ALU.min, ALU.subtract))
                    ch.link(eng.tensor_tensor_scan(gate_sum[:, :], c["restart"], gate_z[:, :], 0.0, ALU.mult, ALU.add))
                    sums = gate_sum[:, :].rearrange("p (n s) -> p n s", s=SEQ)
                    ch.link(eng.tensor_tensor(gate_z[:, :].rearrange("p (n s) -> p n s", s=SEQ), sums,
                                              sums[:, :, SEQ // 2 - 1:SEQ // 2].to_broadcast([P, GC * GB, SEQ]), ALU.subtract))
                    eng.tensor_scalar(gate_z[:, :], gate_z[:, :], -80.0 * NORMALIZER, 80.0 * NORMALIZER,
                                      ALU.max, ALU.min).then_inc(decay_in, 1)
                elif name == "b_silu":
                    ch = chain("ab", g)
                    for t in range(TILES):
                        wait_full(eng, f"gg{t}", g)
                        freed(eng.tensor_tensor(silu_g[:, t, :], bank(f"gg{t}")[:, :], bg_b[:, :], ALU.add), f"gg{t}")
                    for t in range(TILES):
                        eng.wait_ge(g_tanhed, g * TILES + t + 1)
                        ch.add(eng.scalar_tensor_tensor(silu_g[:, t, :], temp[:, t, :], 1.0, silu_g[:, t, :], ALU.add, ALU.mult))
                elif name == "b_keys":
                    ch = chain("ab", g)
                    eng.wait_ge(decays, g + 1)
                    wait_full(eng, "gq", g)
                    ch.add(eng.scalar_tensor_tensor(q_even.rearrange("p c t -> p (c t)"), bank("gq")[:, :], c["even"], grow,
                                                    ALU.mult, ALU.mult))
                    freed(eng.scalar_tensor_tensor(q_odd.rearrange("p c t -> p (c t)"), bank("gq")[:, :], c["odd"], grow,
                                                   ALU.mult, ALU.mult), "gq")
                    wait_full(eng, "gk", g)
                    ch.settle()
                    freed(eng.scalar_tensor_tensor(k_dec[:, :, :].rearrange("p c t -> p (c t)"), bank("gk")[:, :], HD ** -0.5,
                                                   shrink, ALU.mult, ALU.mult), "gk")
                elif name[:-1] == "b_scores":
                    t = int(name[-1])
                    for r in range(4):
                        wait_full(eng, f"A{t}{r}", g)
                        freed(eng.tensor_tensor(pair_t[:, t, 4 * r:4 * r + 4, :],
                                                bank(f"A{t}{r}")[:, :].rearrange("p (n t) -> p n t", t=P),
                                                c["causal_mul"].unsqueeze(1).to_broadcast([P, 4, P]), ALU.mult), f"A{t}{r}")
                elif name[:-1] == "b_read":
                    t = int(name[-1])
                    ch = chain("ab", g)
                    wait_full(eng, f"o{t}", g)
                    o = heads(bank(f"o{t}")[:, :])
                    ch.link(eng.tensor_reduce(head_mean[:, t, :], o, AX.X, ALU.add))
                    ch.link(eng.tensor_scalar(head_mean[:, t, :], head_mean[:, t, :], 1.0 / HD, None, ALU.mult))
                    freed(eng.tensor_tensor(heads(o_sb[:, t, :]), o, per_head(head_mean[:, t, :]), ALU.subtract), f"o{t}")
                    wait_evacuated(eng, f"o{t}", g)
                    eng.tensor_scalar(spare[:, 0:1], mv[:, 0, 0:1], 1.0, None, ALU.mult).then_inc(o_centered, 1)
                elif name[:-1] == "b_variance":
                    t = int(name[-1])
                    ch = chain("ab", g)
                    eng.wait_ge(o_squared, g * TILES + t + 1)
                    ch.link(eng.tensor_reduce(row_sum[:, t, :], heads(temp[:, t, :]), AX.X, ALU.add))
                    eng.tensor_scalar(var_e[:, t, :], row_sum[:, t, :], 1.0 / HD, EPS,
                                      ALU.mult, ALU.add).then_inc(var_ready, 1)
                elif name[:-1] == "b_gated":
                    t = int(name[-1])
                    ch = chain("ab", g)
                    eng.wait_ge(rstd_ready, g * 5 + 3 + t)
                    ch.link(eng.tensor_tensor(heads(o_sb[:, t, :]), heads(o_sb[:, t, :]), per_head(rstd[:, t, :]), ALU.mult))
                    eng.scalar_tensor_tensor(o_sb[:, t, :], o_sb[:, t, :], 0.5, silu_g[:, t, :],
                                             ALU.mult, ALU.mult).then_inc(o_ready, 1)
                elif name == "b_out":
                    ch = chain("ab", g)
                    for t in range(TILES):
                        wait_full(eng, f"wo{t}", g)
                        freed(eng.tensor_tensor(y[:, t, :], y[:, t, :], bank(f"wo{t}")[:, :], ALU.add), f"wo{t}")
                    wait_evacuated(eng, "wo0", g)
                    wait_evacuated(eng, "wo1", g)
                    moments(ch, y, stats, mv)
                    ch.link(eng.tensor_tensor(spare[:, 0:TILES], mv[:, :, 0], mv[:, :, 0], ALU.mult))
                    ch.link(eng.tensor_tensor(spare[:, 0:TILES], spare[:, 0:TILES], mv[:, :, 1], ALU.add))
                    eng.tensor_scalar(v2[:, 0:TILES], spare[:, 0:TILES], EPS, None, ALU.add).then_inc(var_ready, 1)
                    if first(g):
                        eng.wait_ge(rows_zeroed, 32)
                    else:
                        eng.wait_ge(rows_stored, g * 32)
                    for t in range(TILES):
                        ch.add(eng.tensor_tensor(resid[:, t, :], x1[:, t, :], y[:, t, :], ALU.add))
                    ch.settle()
                    end("ab")
                elif name == "b_begin":
                    for t in range(TILES):
                        cols = slice(t * P, (t + 1) * P)
                        eng.wait_ge(m_hi_set, g * TILES + t + 1)
                        eng.tensor_tensor(normed2_lo[:, :, cols], normed2[:, t, :, :], normed2_hi[:, :, cols].bitcast(f32),
                                          ALU.subtract).then_inc(m_split, 1)
                elif name in SPLITS and (SPLITS[name][1] == 0 or SPLITS[name][0] < 2):
                    split(SPLITS[name][0], g, SPLITS[name][1])
                elif name == "c_norm":
                    ch = chain("c", g)
                    eng.wait_ge(w_free, (g + 1) * J + 1)
                    for t in range(TILES):
                        eng.tensor_tensor(x2[:, t, :], resid[:, t, :], banks[6 + t][:, :], ALU.add).then_inc(mlp_read, 1)
                    eng.wait_ge(mlp_read, (g + 1) * TILES + 1)
                    moments(ch, x2, c_stats, c_mv)
                    eng.tensor_scalar(c_var[:, :], c_mv[:, :, 1], EPS, None, ALU.add).then_inc(c_var_ready, 1)
                    eng.wait_ge(c_rstd_ready, g + 1)
                    for t in range(TILES):
                        eng.tensor_scalar(z[:, t, :], x2[:, t, :], c_mv[:, t, 0:1], c_rstd[:, t:t + 1],
                                          ALU.subtract, ALU.mult).then_inc(z_ready, 1)
                elif name == "c_route":
                    ch = chain("c", g)
                    wait_full(eng, "lg", g)
                    freed(eng.tensor_copy(logits[:, :, :], bank("lg")[:, 0:TILES * E].rearrange("p (t e) -> p t e", e=E)), "lg")
                    wait_evacuated(eng, "lg", g)
                    for t in range(TILES):
                        apart(eng)
                        ch.link(eng.max(top[:, t, :], logits[:, t, :]))
                        eng.tensor_scalar(neg_max[:, t:t + 1], top[:, t, 0:1], -1.0, None, ALU.mult).then_inc(lg_centered, 1)
                elif name == "c_mask":
                    ch = chain("c", g)
                    for t in range(TILES):
                        eng.wait_ge(lg_exped, g * TILES + t + 1)
                        ch.link(eng.reciprocal(esum[:, t:t + 1], esum[:, t:t + 1]))
                        ch.link(eng.tensor_scalar(logits[:, t, :], logits[:, t, :], esum[:, t:t + 1], None, ALU.mult))
                        apart(eng)
                        ch.link(eng.max(top[:, t, :], logits[:, t, :]))
                        apart(eng)
                        ch.add(eng.max_index(top_id[:, t, :], top[:, t, :], logits[:, t, :]))
                        ch.link(eng.match_replace(left[:, t, :], top[:, t, :], logits[:, t, :], -1.0))
                        eng.tensor_scalar(chosen[:, t, :], left[:, t, :], 0.0, None, ALU.is_lt).then_inc(chosen_ready, 1)
                    ch.settle()
                    eng.tensor_copy(top_idf[:, :, :], top_id[:, :, :]).then_inc(counted, 1)
                elif name == "c_slots":
                    ch = chain("c", g)
                    wait_full(eng, "ps", g)
                    freed(eng.tensor_copy(pos[:, :, :], bank("ps")[:, 0:TILES * E].rearrange("p (t e) -> p t e", e=E)), "ps")
                    wait_evacuated(eng, "ps", g)
                    eng.wait_ge(counted, g + 1)
                    for t in range(TILES):
                        ch.link(eng.tensor_tensor(chosen_sum[:, :], chosen_sum[:, :], chosen[:, t, :], ALU.add))
                    ids = c["expert_slot"].unsqueeze(1).to_broadcast([P, TILES, E])
                    ch.add(eng.tensor_scalar(late[:, :, :], pos[:, :, :], float(P), -float(P * P - 1), ALU.is_ge, ALU.mult))
                    ch.link(eng.scalar_tensor_tensor(slot[:, :, :], pos[:, :, :], float(P), ids, ALU.mult, ALU.add))
                    ch.link(eng.tensor_tensor(slot[:, :, :], slot[:, :, :], late[:, :, :], ALU.add))
                    ch.link(eng.tensor_scalar(late[:, :, :], pos[:, :, :], float(CAP), FAR, ALU.is_ge, ALU.mult))
                    ch.link(eng.tensor_tensor(slot[:, :, :], slot[:, :, :], late[:, :, :], ALU.add))
                elif name == "c_pick":
                    ch = chain("c", g)
                    eng.wait_ge(payload_sent, g + 1)
                    for t in range(TILES):
                        for k in range(TOP):
                            ch.add(eng.scalar_tensor_tensor((left, late)[k // 2 % 2][:, k % 2, :], c["expert_id"],
                                                            top_idf[:, t, k:k + 1], slot[:, t, :],
                                                            ALU.is_equal, ALU.mult, accum_out=slot_f[:, t, k:k + 1]))
                            if k % 4 == 3:
                                ch.settle()
                        ch.add(eng.tensor_copy(slot_i[:, t, :], slot_f[:, t, :]))
                        ch.add(eng.tensor_copy(payload[:, t, :, 0], tok[:, t:t + 1].to_broadcast([P, TOP])))
                        ch.link(eng.tensor_copy(payload[:, t, :, 1].bitcast(f32), top[:, t, :]))
                        eng.tensor_scalar(tok[:, t:t + 1], tok[:, t:t + 1], float(GT), None, ALU.add).then_inc(payload_ready, 1)
                    eng.wait_ge(payload_ready, (g + 1) * TILES)
                    eng.wait_ge(rows_stored, (g + 1) * 32)
                    end("c")
                elif name[0] == "c" and name[1:].isdigit():
                    ch = chain("c", g)
                    j = int(name[1:])
                    eng.wait_ge(h_tanhed, g * J + j + 1)
                    ch.link(eng.scalar_tensor_tensor(h_e, h_e, 1.0, bank(f"h{j}")[:, 0:GT], ALU.add, ALU.mult))
                    if j:
                        eng.wait_ge(h_split, g * J + j)
                    freed(eng.scalar_tensor_tensor(h_f, h_e, 0.5, bank(f"h{j}")[:, GT:2 * GT], ALU.mult, ALU.mult), f"h{j}")
                    wait_evacuated(eng, f"h{j}", g)
                    ch.link(eng.tensor_copy(h_hi[:, j % 2, :], h_f))
                    eng.tensor_tensor(h_lo[:, j % 2, :], h_f, h_hi[:, j % 2, :].bitcast(f32), ALU.subtract).then_inc(h_split, 1)

            iterate(eng, step)
            if phases < 2:
                return

            def split_up(e, par):
                eng.wait_ge(e_gu_hi_set, e + 1)
                eng.tensor_tensor(e_gu_lo[par][:, :], e_w[par][:, 0:GU], e_gu_hi[par][:, :].bitcast(f32),
                                  ALU.subtract).then_inc(e_gu_lo_set, 1)

            def split_down(e, par):
                eng.wait_ge(e_d_hi_set, e + 1)
                eng.tensor_tensor(e_d_lo[par][:, :], e_w[par][:, GU:WE_N], e_d_hi[par][:, :].bitcast(f32),
                                  ALU.subtract).then_inc(e_d_lo_set, 1)

            def turn_e(e, par):
                for h in range(HALVES):
                    eng.wait_ge(e_xt_hi_set, e * HALVES + h + 1)
                    cols = slice(h * P, (h + 1) * P)
                    eng.tensor_tensor(e_xt_lo[par][:, :, cols], banks[h][:, :].rearrange("p (k t) -> p k t", k=KD),
                                      e_xt_hi[par][:, :, cols].bitcast(f32), ALU.subtract).then_inc(e_xt_lo_set, 1)

            def gate(e, par, f):
                eng.wait_ge(e_silu, e * 2 + f + 1)
                eng.tensor_tensor(e_h[:, f, :], e_s[:, f, :], banks[2 + f][:, CAP:2 * CAP], ALU.mult).then_inc(e_h_set, 1)
                eng.wait_ge(e_h_set, e * 2 + f + 1)
                eng.tensor_copy(e_h_hi[par][:, f, :], e_h[:, f, :]).then_inc(e_h_hi_set, 1)
                eng.wait_ge(e_h_hi_set, e * 2 + f + 1)
                eng.tensor_tensor(e_h_lo[par][:, f, :], e_h[:, f, :], e_h_hi[par][:, f, :].bitcast(f32),
                                  ALU.subtract).then_inc(e_h_lo_set, 1)

            def scale_y(e, n, first=False):
                eng.wait_ge(e_down, e * HALVES + 2)
                if not first:
                    eng.wait_ge(e_added, (e - 1) * (16 * HALVES))
                eng.wait_ge(e_slot_set, e + 1)
                eng.tensor_scalar(e_y[n % 2][:, 1, :], banks[5][:, :], e_slot[n][:, 1, 1:2].bitcast(f32), None, ALU.mult)\
                   .then_inc(e_y_v, 1)

            def expert(e, n, first, last):
                par = n % 2
                if not last:
                    split_up(e + 1, 1 - par)
                gate(e, par, 0)
                if not first:
                    scale_y(e - 1, (n - 1) % AHEAD, first=isinstance(e, int) and e <= 2)
                if not last:
                    turn_e(e + 1, 1 - par)
                    split_down(e + 1, 1 - par)
                gate(e, par, 1)

            split_up(0, 0)
            split_down(0, 0)
            turn_e(0, 0)
            expert_loop(eng, expert)
            scale_y(E - 1, AHEAD - 1)


def loads(e, n, ring, each=1):
    return ((e - n) // ring + 1) * (16 * each) if isinstance(e, int) else (e - n + ring) * (16 // ring * each)


def expert_loop(eng, step):
    for e in range(AHEAD - 1):
        step(e, e, first=(e == 0), last=False)
    with eng.Fori(0, (E - AHEAD) // AHEAD) as m:
        for n in range(AHEAD - 1, 2 * AHEAD - 1):
            step(eng.snap(m * AHEAD + n), n % AHEAD, first=False, last=False)
    step(E - 1, AHEAD - 1, first=False, last=True)


def shape_constants():
    import numpy as np
    p = np.arange(P)
    a = {
        "ident": np.eye(P),
        "causal_add": np.where(np.arange(SEQ)[None, :] <= (p % SEQ)[:, None], 0.0, MASKED),
        "causal_mul": (p[:, None] // SEQ == p[None, :] // SEQ) & (p[:, None] <= p[None, :]),
        "before": p[:, None] < p[None, :],
        "ones": np.ones((P, P)),
        "restart": np.tile((np.arange(GC * GT) % SEQ != 0)[None, :], (P, 1)),
        "even": (p % 32 < GK)[:, None],
        "odd": (p % 32 >= GK)[:, None],
        "expert_id": np.tile(np.arange(E)[None, :], (P, 1)),
        "expert_slot": np.tile(HALVES * np.arange(E)[None, :], (P, 1)),
        "neg_half": np.full((P, 32), -0.5),
        "token": p[:, None],
    }
    return np.ascontiguousarray(np.concatenate([a[n].astype(np.float32) for n, _ in CONST], axis=1))


def lay_out(inputs):
    import numpy as np

    def chunks(w):
        k = w.shape[0] // P
        return w.reshape(k, P, -1).transpose(1, 0, 2).reshape(P, -1)

    g = {k: np.asarray(v) for k, v in inputs.items()}
    kv = g["L0_xattn_Wkv_expand"].T
    w13 = [g[n].reshape(KD, P, J, P).transpose(2, 1, 0, 3).reshape(J, P, D) for n in ("L0_attn_W1", "L0_attn_W3")]
    per_expert = [g[n].reshape(E, -1, P, g[n].shape[2]).transpose(0, 2, 1, 3).reshape(E, P, -1)
                  for n in ("L0_ffn_w_gate", "L0_ffn_w_up", "L0_ffn_w_down")]
    arrays = {
        "x": g["x"].reshape(T, D),
        "ctxt": g["ctx_512"].reshape(GROUPS, GB, CTX, CD).transpose(0, 3, 2, 1),
        "consts": shape_constants(),
        "vecs": np.concatenate([g["L0_attn_ln1_w"].reshape(KD, P).T, g["L0_attn_ln2_w"].reshape(KD, P).T,
                                g["L0_attn_bkg2"].reshape(GC, P).T], axis=1),
        "bg_row": g["L0_attn_bg"].reshape(1, D),
        "xw": np.concatenate([chunks(g["L0_xattn_Wq"].T), kv, chunks(g["L0_xattn_Wout"].T)], axis=1),
        "gw": np.concatenate([chunks(g[f"L0_attn_{n}"]) for n in ("Wq", "Wk", "Wv", "Wg", "Wo", "Wkg1")], axis=1),
        "kg2": g["L0_attn_Wkg2"],
        "cw": np.concatenate(w13 + [g["L0_attn_W2"].reshape(J, P, D)], axis=2),
        "gate_w": g["L0_ffn_gate_w"].T.reshape(KD, P, E).transpose(1, 0, 2),
        "ew": np.concatenate(per_expert, axis=2),
    }
    return {k: np.ascontiguousarray(v) for k, v in arrays.items()}


def kernel(**inputs):
    import concourse.bacc as bacc
    from concourse.bass_utils import run_bass_kernel_spmd

    nc = bacc.Bacc("TRN2", target_bir_lowering=False, num_devices=1)
    arrays = lay_out(inputs)
    handles = {k: nc.dram_tensor(f"in_{k}", v.shape, mybir.dt.from_np(v.dtype), kind="ExternalInput").ap()
               for k, v in arrays.items()}
    out = nc.dram_tensor("out", (ROWS, D), mybir.dt.float32, kind="ExternalOutput").ap()
    build(nc, out=out, **handles)
    result = run_bass_kernel_spmd(nc, [{f"in_{k}": v for k, v in arrays.items()}], core_ids=[0])
    return result.results[0]["out"][0:T].reshape(BATCH, SEQ, D)
```
